# Optimizing a Trainium2 kernel written in Bass

```python
import numpy as np
import jax
import jax.numpy as jnp

def _softmax(x, axis=-1):
    return jax.nn.softmax(x, axis=axis)

def _gelu(x):
    return jax.nn.gelu(x, approximate=True)

def _silu(x):
    return jax.nn.silu(x)

def _sigmoid(x):
    return jax.nn.sigmoid(x)

def _layernorm(x, axis=-1, eps=1e-05):
    m = jnp.mean(x, axis=axis, keepdims=True)
    v = jnp.var(x, axis=axis, keepdims=True)
    return (x - m) / jnp.sqrt(v + eps)

def _scatter_add(tgt, idx, src, axis=0):
    return tgt.at[idx].add(src)

def _segment_sum(src, seg, n):
    return jax.ops.segment_sum(src, seg, n)
kernel_name = 'mk_perceiver_d2_seqx_r2_690035'

def setup_inputs(seed: int=0):
    np.random.seed(seed)
    _w = jnp.asarray

    def _rec_inputs():
        import jax
        import jax.numpy as jnp
        _rk = jax.random.key(seed)
        x = -0.0003929 + 0.9999 * jax.random.normal(jax.random.fold_in(_rk, 1), (16, 64, 512), jnp.float32)
        _lenS = 64 - jax.random.randint(jax.random.fold_in(_rk, 7), (16,), 0, max(1, 64 // 4) + 1, jnp.int32)
        _lenS2 = 512 - jax.random.randint(jax.random.fold_in(_rk, 8), (16,), 0, max(1, 512 // 4) + 1, jnp.int32)
        _ctx_768P = jax.random.normal(jax.random.fold_in(_rk, 11), (16, 16, 384), jnp.float32)
        _ctx_768c = jax.random.dirichlet(jax.random.fold_in(_rk, 511), 0.3 * jnp.ones((16,), jnp.float32), (16, 512))
        _ctx_768t = jnp.einsum('bsk,bkd->bsd', _ctx_768c, _ctx_768P)
        _ctx_768t = _ctx_768t * jax.lax.rsqrt(jnp.mean(jnp.square(_ctx_768t)) + 1e-12) * 0.953939
        ctx_768 = -7.36909e-05 + 0.999899 * (_ctx_768t + 0.3 * jax.random.normal(jax.random.fold_in(_rk, 611), (16, 512, 384), jnp.float32))
        return (x, ctx_768)
    x, ctx_768 = _rec_inputs()

    def _L0_xattn_setup():
        import jax, jax.numpy as jnp
        import numpy as np
        EPS = 1e-08
        key = jax.random.key(seed)
        kv, kt, k1, k2, k3, k4 = jax.random.split(key, 6)
        B, S = (16, 512)
        VD, TD, H = (512, 384, 256)
        visual_features = jax.random.normal(kv, (B, S, VD), dtype=jnp.float32)
        text_features = jax.random.normal(kt, (B, S, TD), dtype=jnp.float32)
        Wv = jax.random.normal(k1, (H, VD), dtype=jnp.float32) * (1.0 / np.sqrt(VD))
        bv = jax.random.normal(k2, (H,), dtype=jnp.float32) * 0.01
        Wt = jax.random.normal(k3, (H, TD), dtype=jnp.float32) * (1.0 / np.sqrt(TD))
        bt = jax.random.normal(k4, (H,), dtype=jnp.float32) * 0.01
        return {'visual_features': visual_features, 'text_features': text_features, 'Wv': Wv, 'bv': bv, 'Wt': Wt, 'bt': bt}
    _L0_xattn_all = _L0_xattn_setup()
    _L0_xattn_in = {k: v for k, v in _L0_xattn_all.items() if k in ('Wv', 'bv', 'Wt', 'bt')}
    del _L0_xattn_all

    def _L0_attn_setup():
        import jax, jax.numpy as jnp
        import numpy as np
        K_HEADS = 16
        key = jax.random.key(seed)
        k1, k2 = jax.random.split(key)
        z = jax.random.normal(k1, (2, 1024, 512), dtype=jnp.float32)
        W_qkv = jax.random.normal(k2, (1536, 512), dtype=jnp.float32) * (1.0 / np.sqrt(512))
        return {'z': z, 'W_qkv': W_qkv}
    _L0_attn_all = _L0_attn_setup()
    _L0_attn_in = {k: v for k, v in _L0_attn_all.items() if k in ('W_qkv',)}
    del _L0_attn_all

    def _L0_ffn_setup():
        import jax, jax.numpy as jnp
        import numpy as np
        N_EMBD = 512
        N_EXP = 8
        TOP_K = 2
        CAPACITY = 2048
        D_FF = 3 * N_EMBD
        key = jax.random.key(seed)
        k1, k2, k3, k4 = jax.random.split(key, 4)
        x = jax.random.normal(k1, (8, 1024, N_EMBD), dtype=jnp.float32)
        w_gate = jax.random.normal(k2, (N_EMBD, N_EXP), dtype=jnp.float32) * 0.02
        c_fc = jax.random.normal(k3, (N_EXP, N_EMBD, D_FF), dtype=jnp.float32) * 0.02
        c_proj = jax.random.normal(k4, (N_EXP, D_FF // 2, N_EMBD), dtype=jnp.float32) * 0.02
        return {'x': x, 'w_gate': w_gate, 'c_fc': c_fc, 'c_proj': c_proj}
    _L0_ffn_all = _L0_ffn_setup()
    _L0_ffn_in = {k: v for k, v in _L0_ffn_all.items() if k in ('w_gate', 'c_fc', 'c_proj')}
    del _L0_ffn_all

    def _L1_xattn_setup():
        import jax, jax.numpy as jnp
        import numpy as np
        HEADS = 16
        DIM_HEAD = 64
        key = jax.random.key(seed)
        ks = jax.random.split(key, 7)
        b, n, m = (2, 1024, 512)
        query_dim, context_dim = (512, 384)
        inner = HEADS * DIM_HEAD
        s_q = 1.0 / np.sqrt(query_dim)
        s_c = 1.0 / np.sqrt(context_dim)
        s_i = 1.0 / np.sqrt(inner)
        return {'x': jax.random.normal(ks[0], (b, n, query_dim), jnp.float32), 'context': jax.random.normal(ks[1], (b, m, context_dim), jnp.float32), 'Wq': jax.random.normal(ks[2], (query_dim, inner), jnp.float32) * s_q, 'Wk': jax.random.normal(ks[3], (context_dim, inner), jnp.float32) * s_c, 'Wv': jax.random.normal(ks[4], (context_dim, inner), jnp.float32) * s_c, 'Wo': jax.random.normal(ks[5], (inner, query_dim), jnp.float32) * s_i, 'bo': jax.random.normal(ks[6], (query_dim,), jnp.float32) * 0.01}
    _L1_xattn_all = _L1_xattn_setup()
    _L1_xattn_in = {k: v for k, v in _L1_xattn_all.items() if k in ('Wq', 'Wk', 'Wv', 'Wo', 'bo')}
    del _L1_xattn_all

    def _L1_attn_setup():
        import jax, jax.numpy as jnp
        import numpy as np
        import math
        B, S, D, H, DH = (4, 1024, 512, 8, 64)
        SCALE = 1.0 / math.sqrt(DH)
        EPS = 1e-08

        def _xavier(key, shape, gain):
            std = gain * np.sqrt(2.0 / (shape[0] + shape[1]))
            return (jax.random.normal(key, shape, jnp.float32) * std).astype(jnp.float32)

        def _stable_lse(a, b):
            m = jnp.maximum(a, b)
            return m + jnp.log1p(jnp.exp(-jnp.abs(a - b)))
        key = jax.random.key(seed)
        ks = jax.random.split(key, 7)
        return {'x': jax.random.normal(ks[0], (B, S, D), jnp.float32), 'W_q': _xavier(ks[1], (H * DH, D), 0.1), 'W_k': _xavier(ks[2], (H * DH, D), 0.1), 'W_v': _xavier(ks[3], (D, D), 1.0), 'W_alpha_w': jax.random.normal(ks[4], (H * DH, D), jnp.float32) * 0.01, 'W_alpha_b': jnp.ones((H * DH,), jnp.float32), 'W_o': _xavier(ks[5], (D, D), 0.1)}
    _L1_attn_all = _L1_attn_setup()
    _L1_attn_in = {k: v for k, v in _L1_attn_all.items() if k in ('W_q', 'W_k', 'W_v', 'W_alpha_w', 'W_alpha_b', 'W_o')}
    del _L1_attn_all

    def _L1_ffn_setup():
        import jax, jax.numpy as jnp
        import numpy as np
        MANT_BITS = 8
        _PWL_X = jnp.linspace(-4.0, 4.0, 33, dtype=jnp.float32)
        _PWL_Y = 0.5 * _PWL_X * (1.0 + jax.lax.erf(_PWL_X / jnp.sqrt(jnp.float32(2.0))))

        def float2fix(x, mantissa_bits):
            s = jnp.float32(2.0 ** mantissa_bits)
            q = jnp.round(x * s) / s
            return x + jax.lax.stop_gradient(q - x)

        def pwlin_gelu_basic(x, mantissa_bits_in, mantissa_bits_out):
            xq = float2fix(x, mantissa_bits_in)
            y = jnp.interp(xq, _PWL_X, _PWL_Y)
            y = jnp.where(xq > 4.0, xq, jnp.where(xq < -4.0, jnp.float32(0.0), y))
            return float2fix(y, mantissa_bits_out)
        key = jax.random.key(seed)
        k_x, k_w1, k_b1, k_w2, k_b2 = jax.random.split(key, 5)
        dim, ff_dim = (512, 2048)
        B, S = (32, 256)
        sc1 = 1.0 / np.sqrt(dim)
        sc2 = 1.0 / np.sqrt(ff_dim)
        return {'x': jax.random.normal(k_x, (B, S, dim), dtype=jnp.float32), 'w1': jax.random.uniform(k_w1, (dim, ff_dim), jnp.float32, -sc1, sc1), 'b1': jax.random.uniform(k_b1, (ff_dim,), jnp.float32, -sc1, sc1), 'w2': jax.random.uniform(k_w2, (ff_dim, dim), jnp.float32, -sc2, sc2), 'b2': jax.random.uniform(k_b2, (dim,), jnp.float32, -sc2, sc2)}
    _L1_ffn_all = _L1_ffn_setup()
    _L1_ffn_in = {k: v for k, v in _L1_ffn_all.items() if k in ('w1', 'b1', 'w2', 'b2')}
    del _L1_ffn_all
    return {'x': x, 'ctx_768': ctx_768, 'L0_xattn_Wv': _L0_xattn_in['Wv'], 'L0_xattn_bv': _L0_xattn_in['bv'], 'L0_xattn_Wt': _L0_xattn_in['Wt'], 'L0_xattn_bt': _L0_xattn_in['bt'], 'L0_attn_W_qkv': _L0_attn_in['W_qkv'], 'L0_ffn_w_gate': _L0_ffn_in['w_gate'], 'L0_ffn_c_fc': _L0_ffn_in['c_fc'], 'L0_ffn_c_proj': _L0_ffn_in['c_proj'], 'L1_xattn_Wq': _L1_xattn_in['Wq'], 'L1_xattn_Wk': _L1_xattn_in['Wk'], 'L1_xattn_Wv': _L1_xattn_in['Wv'], 'L1_xattn_Wo': _L1_xattn_in['Wo'], 'L1_xattn_bo': _L1_xattn_in['bo'], 'L1_attn_W_q': _L1_attn_in['W_q'], 'L1_attn_W_k': _L1_attn_in['W_k'], 'L1_attn_W_v': _L1_attn_in['W_v'], 'L1_attn_W_alpha_w': _L1_attn_in['W_alpha_w'], 'L1_attn_W_alpha_b': _L1_attn_in['W_alpha_b'], 'L1_attn_W_o': _L1_attn_in['W_o'], 'L1_ffn_w1': _L1_ffn_in['w1'], 'L1_ffn_b1': _L1_ffn_in['b1'], 'L1_ffn_w2': _L1_ffn_in['w2'], 'L1_ffn_b2': _L1_ffn_in['b2']}

def reference(x, ctx_768, L0_xattn_Wv, L0_xattn_bv, L0_xattn_Wt, L0_xattn_bt, L0_attn_W_qkv, L0_ffn_w_gate, L0_ffn_c_fc, L0_ffn_c_proj, L1_xattn_Wq, L1_xattn_Wk, L1_xattn_Wv, L1_xattn_Wo, L1_xattn_bo, L1_attn_W_q, L1_attn_W_k, L1_attn_W_v, L1_attn_W_alpha_w, L1_attn_W_alpha_b, L1_attn_W_o, L1_ffn_w1, L1_ffn_b1, L1_ffn_w2, L1_ffn_b2):
    import jax
    import jax.numpy as jnp

    def _L0_xattn_ref(visual_features, text_features, Wv, bv, Wt, bt):
        import jax, jax.numpy as jnp
        import numpy as np
        EPS = 1e-08
        v = jnp.einsum('bsd,hd->bsh', visual_features, Wv) + bv
        t = jnp.einsum('bsd,hd->bsh', text_features, Wt) + bt
        dots = jnp.einsum('bih,bjh->bij', v, t)
        vn = jnp.linalg.norm(v, axis=-1)
        tn = jnp.linalg.norm(t, axis=-1)
        denom = jnp.maximum(vn[:, :, None] * tn[:, None, :], EPS)
        return dots / denom

    def _L0_attn_ref(z, W_qkv):
        import jax, jax.numpy as jnp
        import numpy as np
        K_HEADS = 16
        b, n, D = z.shape
        k = K_HEADS
        Dh = D // k
        qkv = jnp.einsum('bnd,ed->bne', z, W_qkv)
        qkv = qkv.reshape(b, n, k, 3, Dh).transpose(3, 0, 2, 1, 4)
        q, kk, v = (qkv[0], qkv[1], qkv[2])
        scale = 1.0 / jnp.sqrt(jnp.asarray(Dh, dtype=z.dtype))
        scores = jnp.einsum('bhnd,bhmd->bhnm', q, kk) * scale
        A = jax.nn.softmax(scores, axis=-1)
        out = jnp.einsum('bhnm,bhmd->bhnd', A, v)
        return out.transpose(0, 2, 1, 3).reshape(b, n, D)

    def _L0_ffn_ref(x, w_gate, c_fc, c_proj):
        import jax, jax.numpy as jnp
        import numpy as np
        N_EMBD = 512
        N_EXP = 8
        TOP_K = 2
        CAPACITY = 2048
        D_FF = 3 * N_EMBD
        B, T, d = x.shape
        N = B * T
        xf = x.reshape(N, d)
        scores = jax.nn.softmax(xf @ w_gate, axis=-1)
        weights, idx = jax.lax.top_k(scores, TOP_K)
        flat_e = idx.reshape(-1)
        tok = jnp.repeat(jnp.arange(N), TOP_K)
        oh = jax.nn.one_hot(flat_e, N_EXP, dtype=jnp.int32)
        pos = (jnp.cumsum(oh, axis=0) * oh).sum(-1) - 1
        valid = pos < CAPACITY
        pos_c = jnp.where(valid, pos, 0)
        vmask = valid.astype(x.dtype)[:, None]
        exp_x = jnp.zeros((N_EXP, CAPACITY, d), x.dtype)
        exp_x = exp_x.at[flat_e, pos_c].add(xf[tok] * vmask)
        h = jnp.einsum('ecd,edf->ecf', exp_x, c_fc)
        a, g = jnp.split(h, 2, axis=-1)
        h = jax.nn.silu(a) * g
        exp_out = jnp.einsum('ecf,efd->ecd', h, c_proj)
        gathered = exp_out[flat_e, pos_c]
        w = weights.reshape(-1)[:, None] * vmask
        out = (gathered * w).reshape(N, TOP_K, d).sum(axis=1)
        return out.reshape(B, T, d)

    def _L1_xattn_ref(x, context, Wq, Wk, Wv, Wo, bo):
        import jax, jax.numpy as jnp
        import numpy as np
        HEADS = 16
        DIM_HEAD = 64
        b, n, _ = x.shape
        h, d = (HEADS, DIM_HEAD)
        scale = d ** (-0.5)
        q = (x @ Wq).reshape(b, n, h, d).transpose(0, 2, 1, 3)
        k = (context @ Wk).reshape(b, -1, h, d).transpose(0, 2, 1, 3)
        v = (context @ Wv).reshape(b, -1, h, d).transpose(0, 2, 1, 3)
        sim = jnp.einsum('bhid,bhjd->bhij', q, k) * scale
        attn = jax.nn.softmax(sim, axis=-1)
        out = jnp.einsum('bhij,bhjd->bhid', attn, v)
        out = out.transpose(0, 2, 1, 3).reshape(b, n, h * d)
        return out @ Wo + bo

    def _L1_attn_ref(x, W_q, W_k, W_v, W_alpha_w, W_alpha_b, W_o):
        import jax, jax.numpy as jnp
        import numpy as np
        import math
        B, S, D, H, DH = (4, 1024, 512, 8, 64)
        SCALE = 1.0 / math.sqrt(DH)
        EPS = 1e-08

        def _xavier(key, shape, gain):
            std = gain * np.sqrt(2.0 / (shape[0] + shape[1]))
            return (jax.random.normal(key, shape, jnp.float32) * std).astype(jnp.float32)

        def _stable_lse(a, b):
            m = jnp.maximum(a, b)
            return m + jnp.log1p(jnp.exp(-jnp.abs(a - b)))
        Bx, Sx, _ = x.shape
        q = (x @ W_q.T).reshape(Bx, Sx, H, DH)
        k = (x @ W_k.T).reshape(Bx, Sx, H, DH)
        v = x @ W_v.T
        b = (q * k).sum(-1) * SCALE
        alpha = (x @ W_alpha_w.T + W_alpha_b).reshape(Bx, Sx, H, DH)
        a = -jax.nn.softplus(alpha).sum(-1)
        vs = jnp.sign(v)
        vs = jnp.where(vs == 0, jnp.ones_like(vs), vs)
        vl = jnp.log(jnp.abs(v) + EPS)
        ln0 = b[:, 0]
        nm0 = b[:, 0, :, None] + vl[:, 0, None, :]
        sg0 = jnp.broadcast_to(vs[:, 0, None, :], nm0.shape)
        y0 = (sg0 * jnp.exp(nm0 - ln0[..., None])).sum(-2)

        def step(carry, inp):
            ln, nm, sg = carry
            a_t, b_t, vl_t, vs_t = inp
            ln = _stable_lse(a_t + ln, b_t)
            dec = a_t[..., None] + nm
            new = b_t[..., None] + vl_t[:, None, :]
            m = jnp.maximum(dec, new)
            ssum = sg * jnp.exp(dec - m) + vs_t[:, None, :] * jnp.exp(new - m)
            nsg = jnp.sign(ssum)
            nsg = jnp.where(nsg == 0, jnp.ones_like(nsg), nsg)
            nm = m + jnp.log(jnp.abs(ssum) + EPS)
            y = (nsg * jnp.exp(nm - ln[..., None])).sum(-2)
            return ((ln, nm, nsg), y)
        xs = (jnp.moveaxis(a[:, 1:], 1, 0), jnp.moveaxis(b[:, 1:], 1, 0), jnp.moveaxis(vl[:, 1:], 1, 0), jnp.moveaxis(vs[:, 1:], 1, 0))
        _, ys = jax.lax.scan(step, (ln0, nm0, sg0), xs)
        y = jnp.concatenate([y0[:, None, :], jnp.moveaxis(ys, 0, 1)], axis=1)
        return y @ W_o.T

    def _L1_ffn_ref(x, w1, b1, w2, b2):
        import jax, jax.numpy as jnp
        import numpy as np
        MANT_BITS = 8
        _PWL_X = jnp.linspace(-4.0, 4.0, 33, dtype=jnp.float32)
        _PWL_Y = 0.5 * _PWL_X * (1.0 + jax.lax.erf(_PWL_X / jnp.sqrt(jnp.float32(2.0))))

        def float2fix(x, mantissa_bits):
            s = jnp.float32(2.0 ** mantissa_bits)
            q = jnp.round(x * s) / s
            return x + jax.lax.stop_gradient(q - x)

        def pwlin_gelu_basic(x, mantissa_bits_in, mantissa_bits_out):
            xq = float2fix(x, mantissa_bits_in)
            y = jnp.interp(xq, _PWL_X, _PWL_Y)
            y = jnp.where(xq > 4.0, xq, jnp.where(xq < -4.0, jnp.float32(0.0), y))
            return float2fix(y, mantissa_bits_out)
        h = jnp.einsum('bsd,df->bsf', x, w1) + b1
        h = float2fix(h, MANT_BITS)
        h = pwlin_gelu_basic(h, MANT_BITS, MANT_BITS)
        h = float2fix(h, MANT_BITS)
        out = jnp.einsum('bsf,fd->bsd', h, w2) + b2
        return float2fix(out, MANT_BITS)
    x = x + _L0_xattn_ref(_layernorm(x, axis=-1), ctx_768, L0_xattn_Wv, L0_xattn_bv, L0_xattn_Wt, L0_xattn_bt)
    x = x + _L0_attn_ref(_layernorm(x, axis=-1), L0_attn_W_qkv)
    x = x + _L0_ffn_ref(_layernorm(x, axis=-1), L0_ffn_w_gate, L0_ffn_c_fc, L0_ffn_c_proj)
    x = x + _L1_xattn_ref(_layernorm(x, axis=-1), ctx_768, L1_xattn_Wq, L1_xattn_Wk, L1_xattn_Wv, L1_xattn_Wo, L1_xattn_bo)
    x = x + _L1_attn_ref(_layernorm(x, axis=-1), L1_attn_W_q, L1_attn_W_k, L1_attn_W_v, L1_attn_W_alpha_w, L1_attn_W_alpha_b, L1_attn_W_o)
    x = x + _L1_ffn_ref(_layernorm(x, axis=-1), L1_ffn_w1, L1_ffn_b1, L1_ffn_w2, L1_ffn_b2)
    return x

_drawn_inputs = setup_inputs


def setup_inputs(seed=0):
    import zlib

    import numpy as np

    out = dict(_drawn_inputs(seed))
    spreads = {'L1_attn_W_alpha_b': (1.0, 0.2)}
    factors = {'L0_xattn_bv': 8.0,
     'L0_xattn_bt': 37.781,
     'L0_ffn_w_gate': 4.234,
     'L0_ffn_c_fc': 3.689,
     'L0_ffn_c_proj': 3.704,
     'L1_xattn_bo': 6.586,
     'L1_attn_W_q': 64.0,
     'L1_attn_W_k': 64.0,
     'L1_ffn_b1': 8.0,
     'L1_ffn_b2': 6.467}
    for name, (base, spread) in spreads.items():
        noise = np.random.default_rng([zlib.crc32(name.encode()), seed]).standard_normal(out[name].shape)
        drawn = base * np.exp(spread * noise) if base else spread * noise
        out[name] = jnp.asarray(drawn.astype(out[name].dtype))
    for name, factor in factors.items():
        out[name] = (out[name] * factor).astype(out[name].dtype)
    return out
```

```python
from contextlib import ExitStack

import numpy as np

import concourse.bass as bass
from concourse import mybir

F32 = mybir.dt.float32
U32 = mybir.dt.uint32
I32 = mybir.dt.int32
ALU = mybir.AluOpType
ACT = mybir.ActivationFunctionType
AX = mybir.AxisListType

P = 128
B, S, D = 16, 64, 512
J, C = 512, 384
NT = B * S // P
DK = D // P
CK = C // P
HX = 256
H0, DH0 = 16, 32
NE, FE = 8, 768
ET = 2 * B * S // P + NE - 1
H1, DH1 = 16, 64
HC = H1 * DH1
HS, DHS = 8, 64
FF = 2048
LN_EPS = 1e-5
EPS = 1e-8
EPS_BITS = int(np.float32(EPS).view(np.uint32))
SIGN_BIT = 0x80000000
ROUND = 12582912.0
QUANT = 256.0

CN_ID = 0
CN_TRI = CN_ID + P
CN_ONE = CN_TRI + P
CN_SEL = CN_ONE + P
CN_IOTA = CN_SEL + B
CN_TILE = CN_IOTA + NT * NE
CN_MISC = CN_TILE + ET * NE
CN_HALF, CN_MHALF, CN_ROUND, CN_TOP, CN_K0, CN_K1 = range(CN_MISC, CN_MISC + 6)
CN_N = CN_MISC + 6


def constant_table():
    t = np.zeros((P, CN_N), np.float32)
    p = np.arange(P)
    t[:, CN_ID:CN_ID + P] = np.eye(P)
    t[:, CN_TRI:CN_TRI + P] = p[:, None] < p[None, :]
    t[:, CN_ONE:CN_ONE + P] = 1.0
    t[:, CN_SEL:CN_SEL + B] = p[:, None] // HS == np.arange(B)[None, :]
    t[:, CN_IOTA:CN_IOTA + NT * NE] = np.tile(np.arange(NE) - NE, NT)
    t[:, CN_TILE:CN_TILE + ET * NE] = np.repeat(np.arange(ET), NE)
    t[:, CN_HALF] = 0.5
    t[:, CN_MHALF] = -0.5
    t[:, CN_ROUND] = ROUND
    t[:, CN_TOP] = -4.0 * QUANT
    t[:, CN_K0] = -0.25 * ROUND
    t[:, CN_K1] = 0.25 - 0.25 * ROUND
    return t


BASE = 1


class Env:
    pass


class Chain:

    def __init__(self, eng, sem):
        self.eng, self.sem, self.base, self.n = eng, sem, 0, 0

    def turn(self, i, per):
        self.base, self.n = i * per + self.n, 0

    def link(self, ins):
        ins.then_inc(self.sem, 1)
        self.n += 1
        self.eng.wait_ge(self.sem, BASE + self.base + self.n)


class Norm:

    def __init__(self, nc, e, tag, sbuf, bank, xT):
        self.nc, self.x, self.cn, self.ident = nc, e.x, e.cn, e.ident
        sem = e.sem
        self.st = sbuf(f"st{tag}", [P, 6])
        self.mv = sbuf(f"mv{tag}", [P, 2])
        self.ve = sbuf(f"ve{tag}", [P, 1])
        self.rs = sbuf(f"rs{tag}", [P, 1])
        self.xn = sbuf(f"xn{tag}", [P, D])
        self.bank, self.xT = bank, xT
        self.var, self.rstd = sem(f"var{tag}"), sem(f"rstd{tag}")
        self.norm, self.turned = sem(f"norm{tag}"), sem(f"turned{tag}")
        self.xT_ready, self.seen = sem(f"xT_ready{tag}"), sem(f"seen{tag}")

    def vector_stats(self, ch, n):
        ch.link(self.nc.vector.bn_stats(self.st[:, :], self.x[:, n, :]))
        self.nc.vector.sem_inc(self.seen)
        ch.link(self.nc.vector.bn_aggr(self.mv[:, :], self.st[:, :]))
        self.nc.vector.tensor_scalar(self.ve[:, :], self.mv[:, 1:2], LN_EPS, None,
                                ALU.add).then_inc(self.var, 1)

    def pool(self, eng, n):
        eng.wait_ge(self.var, BASE + n + 1)
        self.nc.gpsimd.tensor_tensor(self.rs[:, :], self.ve[:, :], self.cn[:, CN_MHALF:CN_MHALF + 1],
                                ALU.pow).then_inc(self.rstd, 1)

    def vector_norm(self, eng, n):
        eng.wait_ge(self.rstd, BASE + n + 1)
        eng.wait_ge(self.turned, BASE + n)
        self.nc.vector.tensor_scalar(self.xn[:, :], self.x[:, n, :], self.mv[:, 0:1], self.rs[:, 0:1],
                                ALU.subtract, ALU.mult).then_inc(self.norm, 1)

    def tensor(self, eng, n):
        eng.wait_ge(self.norm, BASE + n + 1)
        eng.wait_ge(self.xT_ready, BASE + n)
        for k in range(DK):
            last = self.nc.tensor.transpose(self.bank[:, k * P:(k + 1) * P],
                                       self.xn[:, k * P:(k + 1) * P], self.ident)
        last.then_inc(self.turned, 1)

    def scalar(self, eng, n, used, count=None):
        eng.wait_ge(self.turned, BASE + n + 1)
        eng.wait_ge(used, BASE + (n if count is None else count))
        self.nc.scalar.activation(self.xT[:, :, :].rearrange("p k t -> p (k t)"), self.bank[:, :],
                             ACT.Copy).then_inc(self.xT_ready, 1)


def cosine_layer(nc, a, e):
    x, cn, ps, ones, ident, sem = e.x, e.cn, e.ps, e.ones, e.ident, e.sem
    s_cn, s_x, s_w12, s_xg0 = e.s_cn, e.s_x, e.s_w12, e.s_xg0
    wv0, wt0, wqkv, xg_d = e.wv0, e.wt0, e.wqkv, e.xg_d
    with ExitStack() as st:
        def sbuf(name, shape, dt=F32):
            return st.enter_context(nc.sbuf_tensor(name, shape, dt))

        cT = sbuf("cT1", [P, 2, CK, J])
        tT = sbuf("tT1", [P, 2, 2, J])
        sq = sbuf("sq1", [P, 2, 2, J])
        v = sbuf("v1", [P, HX])
        vsq = sbuf("vsq1", [P, HX])
        vT = sbuf("vT1", [P, 2, P])
        vn2 = sbuf("vn2_1", [P, 1])
        vn = sbuf("vn1", [P, 1])
        tn = sbuf("tn1", [P, J])
        den = sbuf("den1", [P, J])
        rden = sbuf("rden1", [P, J])
        cosv = sbuf("cos1", [P, J])
        bv = sbuf("bv1", [1, HX])
        bt = sbuf("bt1", [P, 2])
        xT = sbuf("xT1", [P, DK, P])
        zero = sbuf("zero1", [P, D])
        ln = Norm(nc, e, "1", sbuf, ps[7], xT)
        s_ct = [sem("s_ct1_0"), sem("s_ct1_1")]
        s_b = sem("s_b1")
        v_mm, v_sb, v_sq, v_n = sem("v_mm1"), sem("v_sb1"), sem("v_sq1"), sem("v_n1")
        vt_mm, vt_sb = sem("vt_mm1"), sem("vt_sb1")
        t_mm, t_sb, t_sq = sem("t_mm1"), sem("t_sb1"), sem("t_sq1")
        d_mm, n_mm, tn_sb = sem("d_mm1"), sem("n_mm1"), sem("tn_sb1")
        dots_read = sem("dots_read1")
        s_zero, s_zx = sem("s_zero1"), sem("s_zx1")
        dve = sem("dve1")
        psV, psVT, psT, psD, psN = ps[0], ps[1], (ps[2], ps[3]), ps[4], ps[5]

        e.open_sems()
        with nc.Block() as block:
            @block.sync
            def _(sp):
                sp.dma_start(cn[:, :], a["consts"]).then_inc(s_cn, 16)
                sp.dma_start(x[:, 0:NT, :], a["x"]).then_inc(s_x, 16)
                sp.dma_start(wv0, a["wv0"]).then_inc(s_w12, 16)
                sp.dma_start(wt0, a["wt0"]).then_inc(s_w12, 16)
                sp.dma_start(bv[:, :], a["bv0"]).then_inc(s_b, 16)
                sp.dma_start(bt[:, :], a["bt0"]).then_inc(s_b, 16)
                for u in range(2):
                    sp.dma_start(cT[:, u], a["ctxT"][u]).then_inc(s_ct[u], 16)
                sp.dma_start(wqkv, a["wqkv"]).then_inc(s_w12, 16)
                sp.wait_ge(s_zero, BASE + 1)
                for e in range(ET):
                    sp.dma_start(xg_d[e * P:(e + 1) * P, :], zero[:, :]).then_inc(s_xg0, 16)
                with sp.Fori(0, NT - 1) as i:
                    for u in range(2):
                        sp.wait_ge(t_mm, BASE + 4 * i + 2 * u + 2)
                        sp.dma_start(cT[:, u], a["ctxT"][2 * i + 2 + u]).then_inc(s_ct[u], 16)
                sp.wait_ge(s_xg0, BASE + 16 * ET)

            @block.gpsimd
            def _(pool):
                nc.gpsimd.memset(zero[:, :], 0.0).then_inc(s_zero, 1)
                nc.gpsimd.memset(x[:, NT, :], 0.0).then_inc(s_zx, 1)
                pool.wait_ge(s_cn, BASE + 16)
                ln.pool(pool, 0)
                with pool.Fori(0, NT) as i:
                    ln.pool(pool, i + 1)
                    pool.wait_ge(v_sq, BASE + i + 1)
                    nc.gpsimd.tensor_tensor(vn[:, :], vn2[:, :], cn[:, CN_HALF:CN_HALF + 1],
                                            ALU.pow).then_inc(v_n, 1)

            @block.vector
            def _(ve):
                ch = Chain(ve, dve)
                ve.wait_ge(s_x, BASE + 16)
                ln.vector_stats(ch, 0)
                ln.vector_norm(ve, 0)
                ve.wait_ge(s_zx, BASE + 1)
                with ve.Fori(0, NT) as i:
                    ch.turn(i, 6)
                    ln.vector_stats(ch, i + 1)
                    ve.wait_ge(v_mm, BASE + i + 1)
                    ve.wait_ge(vt_mm, BASE + i)
                    ve.wait_ge(v_sq, BASE + i)
                    nc.vector.tensor_copy(v[:, :], psV[:, 0:HX]).then_inc(v_sb, 1)
                    ln.vector_norm(ve, i + 1)
                    ve.wait_ge(vt_mm, BASE + i + 1)
                    ve.wait_ge(d_mm, BASE + i)
                    nc.vector.tensor_copy(vT[:, :, :].rearrange("p m t -> p (m t)"),
                                          psVT[:, 0:2 * P]).then_inc(vt_sb, 1)
                    ve.wait_ge(v_n, BASE + i + 1)
                    ve.wait_ge(tn_sb, BASE + i + 1)
                    ch.link(nc.vector.tensor_scalar(den[:, :], tn[:, :], vn[:, 0:1], EPS,
                                                    ALU.mult, ALU.max))
                    ch.link(nc.vector.reciprocal(rden[:, :], den[:, :]))
                    ve.wait_ge(d_mm, BASE + i + 1)
                    ch.link(nc.vector.tensor_tensor(cosv[:, :], psD[:, :], rden[:, :], ALU.mult))
                    ve.sem_inc(dots_read, 1)
                    ch.link(nc.vector.tensor_tensor(x[:, i, :], x[:, i, :], cosv[:, :], ALU.add))
                    assert ch.n == 6

            @block.tensor
            def _(pe):
                pe.wait_ge(s_cn, BASE + 16)
                ln.tensor(pe, 0)
                pe.wait_ge(s_w12, BASE + 32)
                pe.wait_ge(s_b, BASE + 32)

                def project(i, u):
                    pe.wait_ge(s_ct[u], BASE + 16 * i + 16)
                    for m in range(2):
                        if u:
                            pe.wait_ge(t_sb, BASE + 4 * i + 1 + m)
                            pe.wait_ge(t_sq, BASE + 4 * i + 1 + m)
                        else:
                            pe.wait_ge(t_sb, BASE + 4 * i)
                            pe.wait_ge(t_sq, BASE + 4 * i)
                        for k in range(CK):
                            mm = nc.tensor.matmul(psT[m][:, :], wt0[:, k, m * P:(m + 1) * P],
                                                  cT[:, u, k, :], start=(k == 0), stop=(k == CK - 1))
                        mm.then_inc(t_mm, 1)

                with pe.Fori(0, NT) as i:
                    pe.wait_ge(ln.xT_ready, BASE + i + 1)
                    pe.wait_ge(v_sb, BASE + i)
                    for k in range(DK):
                        nc.tensor.matmul(psV[:, 0:HX], xT[:, k, :], wv0[:, k, :],
                                         start=(k == 0), stop=False)
                    nc.tensor.matmul(psV[:, 0:HX], ones[0:1, :], bv[0:1, :],
                                     start=False, stop=True).then_inc(v_mm, 1)
                    project(i, 0)
                    pe.wait_ge(v_sb, BASE + i + 1)
                    pe.wait_ge(vt_sb, BASE + i)
                    for m in range(2):
                        tr = nc.tensor.transpose(psVT[:, m * P:(m + 1) * P],
                                                 v[:, m * P:(m + 1) * P], ident)
                    tr.then_inc(vt_mm, 1)
                    project(i, 1)
                    ln.tensor(pe, i + 1)
                    pe.wait_ge(vt_sb, BASE + i + 1)
                    pe.wait_ge(dots_read, BASE + i)
                    pe.wait_ge(tn_sb, BASE + i)
                    for u in range(2):
                        rows = slice(u * S, (u + 1) * S)
                        pe.wait_ge(t_sb, BASE + 4 * i + 2 * u + 2)
                        pe.wait_ge(t_sq, BASE + 4 * i + 2 * u + 2)
                        for m in range(2):
                            mn = nc.tensor.matmul(psN[rows, :], ones[:, 0:S], sq[:, u, m, :],
                                                  start=(m == 0), stop=(m == 1))
                        if u:
                            mn.then_inc(n_mm, 1)
                        for m in range(2):
                            mm = nc.tensor.matmul(psD[rows, :], vT[:, m, rows], tT[:, u, m, :],
                                                  start=(m == 0), stop=(m == 1))
                    mm.then_inc(d_mm, 1)

            @block.scalar
            def _(act):
                act.wait_ge(s_cn, BASE + 16)
                act.wait_ge(s_b, BASE + 32)
                ln.scalar(act, 0, v_mm)
                with act.Fori(0, NT) as i:
                    act.wait_ge(v_sb, BASE + i + 1)
                    act.wait_ge(v_n, BASE + i)
                    nc.scalar.activation(vsq[:, :], v[:, :], ACT.Square,
                                         accum_out=vn2[:, :]).then_inc(v_sq, 1)

                    def project_out(u):
                        for m in range(2):
                            act.wait_ge(t_mm, BASE + 4 * i + 2 * u + m + 1)
                            act.wait_ge(d_mm, BASE + i)
                            nc.scalar.activation(tT[:, u, m, :], psT[m][:, :], ACT.Identity,
                                                 bias=bt[:, m:m + 1]).then_inc(t_sb, 1)
                            nc.scalar.activation(sq[:, u, m, :], psT[m][:, :], ACT.Square,
                                                 bias=bt[:, m:m + 1]).then_inc(t_sq, 1)

                    project_out(0)
                    project_out(1)
                    ln.scalar(act, i + 1, v_mm)
                    act.wait_ge(n_mm, BASE + i + 1)
                    act.wait_ge(dots_read, BASE + i)
                    nc.scalar.activation(tn[:, :], psN[:, :], ACT.Sqrt).then_inc(tn_sb, 1)


def self_attention_layer(nc, a, e):
    x, cn, ps, PS, ident, sem, wqkv = e.x, e.cn, e.ps, e.PS, e.ident, e.sem, e.wqkv
    SCALE = float(np.float32(1.0) / np.sqrt(np.float32(DH0)))
    HH = P // DH0
    with ExitStack() as st:
        def sbuf(name, shape, dt=F32):
            return st.enter_context(nc.sbuf_tensor(name, shape, dt))

        xT = sbuf("xT2", [P, DK, P])
        q, k, v = sbuf("q2", [P, D]), sbuf("k2", [P, D]), sbuf("v2", [P, D])
        qT, kT = sbuf("qT2", [P, DK, P]), sbuf("kT2", [P, DK, P])
        mx = sbuf("mx2", [P, H0])
        sc = sbuf("sc2", [P, H0, S])
        pf = sbuf("pf2", [P, H0, P])
        pT = sbuf("pT2", [P, H0, P])
        sums, rs = sbuf("sums2", [P, H0]), sbuf("rsum2", [P, H0])
        o = sbuf("o2", [P, D])
        ln = Norm(nc, e, "2", sbuf, ps[7], xT)
        q_mm, k_mm, v_mm = sem("q_mm2"), sem("k_mm2"), sem("v_mm2")
        q_sb, k_sb, v_sb = sem("q_sb2"), sem("k_sb2"), sem("v_sb2")
        qT_mm, kT_mm, qT_sb, kT_sb = sem("qT_mm2"), sem("kT_mm2"), sem("qT_sb2"), sem("kT_sb2")
        s_mm, sub_done, e_sb, summed = sem("s_mm2"), sem("sub_done2"), sem("e_sb2"), sem("summed2")
        pt_mm, pt_act, pt_dve = sem("pt_mm2"), sem("pt_act2"), sem("pt_dve2")
        o_mm, o_read, zeroed, dve = sem("o_mm2"), sem("o_read2"), sem("zeroed2"), sem("dve2")
        S_BANKS = PS[:, 3:3 + HH, 0:DK * S]

        e.open_sems()
        with nc.Block() as block:
            @block.gpsimd
            def _(pool):
                nc.gpsimd.memset(pf[:, :, :], 0.0).then_inc(zeroed, 1)
                ln.pool(pool, 0)
                with pool.Fori(0, NT) as i:
                    ln.pool(pool, i + 1)

            @block.tensor
            def _(pe):
                def project(n):
                    pe.wait_ge(ln.xT_ready, BASE + n + 1)
                    for w, done, out_read in ((0, q_mm, qT_sb), (1, k_mm, kT_sb), (2, v_mm, v_sb)):
                        pe.wait_ge(out_read, BASE + n)
                        for kk in range(DK):
                            mm = nc.tensor.matmul(ps[w], xT[:, kk, :], wqkv[:, kk, w * D:(w + 1) * D],
                                                  start=(kk == 0), stop=(kk == DK - 1))
                        mm.then_inc(done, 1)

                pe.wait_ge(e.s_w12, BASE + 48)
                ln.tensor(pe, 0)
                project(0)
                with pe.Fori(0, NT) as i:
                    for src, bank, ready, done in ((q, 0, q_sb, qT_mm), (k, 1, k_sb, kT_mm)):
                        pe.wait_ge(ready, BASE + i + 1)
                        for m in range(DK):
                            tr = nc.tensor.transpose(ps[bank][:, m * P:(m + 1) * P],
                                                     src[:, m * P:(m + 1) * P], ident)
                        tr.then_inc(done, 1)
                    pe.wait_ge(qT_sb, BASE + i + 1)
                    pe.wait_ge(kT_sb, BASE + i + 1)
                    pe.wait_ge(pt_act, BASE + 2 * i)
                    pe.wait_ge(pt_dve, BASE + 2 * i)
                    for m in range(DK):
                        for hh in range(HH):
                            part = slice(hh * DH0, (hh + 1) * DH0)
                            for u in range(2):
                                tok = slice(u * S, (u + 1) * S)
                                mm = nc.tensor.matmul(PS[tok, 3 + hh, m * S:(m + 1) * S],
                                                      qT[part, m, tok], kT[part, m, tok],
                                                      start=True, stop=True)
                    mm.then_inc(s_mm, 1)
                    pe.wait_ge(o_read, BASE + i)
                    ln.tensor(pe, i + 1)
                    project(i + 1)
                    pe.wait_ge(e_sb, BASE + 2 * i + 2)
                    for g in range(HH):
                        for m in range(DK):
                            tr = nc.tensor.transpose(ps[3 + g][:, m * P:(m + 1) * P],
                                                     pf[:, g * DK + m, :], ident)
                        tr.then_inc(pt_mm, 1)
                    pe.wait_ge(pt_act, BASE + 2 * i + 2)
                    pe.wait_ge(pt_dve, BASE + 2 * i + 2)
                    pe.wait_ge(v_sb, BASE + i + 1)
                    for m in range(DK):
                        for hh in range(HH):
                            h = m * HH + hh
                            mm = nc.tensor.matmul(ps[7][:, h * DH0:(h + 1) * DH0], pT[:, hh * DK + m, :],
                                                  v[:, h * DH0:(h + 1) * DH0], start=True, stop=True)
                    mm.then_inc(o_mm, 1)

            @block.scalar
            def _(act):
                def take(n):
                    for dst, bank, done, turned, ready in ((q, 0, q_mm, qT_mm, q_sb),
                                                           (k, 1, k_mm, kT_mm, k_sb)):
                        act.wait_ge(done, BASE + n + 1)
                        act.wait_ge(turned, BASE + n)
                        nc.scalar.activation(dst[:, :], ps[bank], ACT.Copy).then_inc(ready, 1)

                ln.scalar(act, 0, v_mm)
                take(0)
                act.wait_ge(zeroed, BASE + 1)
                with act.Fori(0, NT) as i:
                    act.wait_ge(qT_mm, BASE + i + 1)
                    act.wait_ge(s_mm, BASE + i)
                    nc.scalar.activation(qT[:, :, :].rearrange("p m t -> p (m t)"), ps[0],
                                         ACT.Copy).then_inc(qT_sb, 1)
                    ln.scalar(act, i + 1, v_mm)
                    act.wait_ge(sub_done, BASE + i + 1)
                    act.wait_ge(pt_mm, BASE + 4 * i)
                    act.wait_ge(summed, BASE + i)
                    for u in range(2):
                        tok = slice(u * S, (u + 1) * S)
                        nc.scalar.activation(pf[tok, :, tok], sc[tok, :, :], ACT.Exp,
                                             scale=SCALE).then_inc(e_sb, 1)
                    take(i + 1)
                    for g in range(2):
                        act.wait_ge(pt_mm, BASE + 4 * i + g + 1)
                        act.wait_ge(o_mm, BASE + i)
                        nc.scalar.activation(pT[:, g * DK:(g + 1) * DK, :].rearrange("p m t -> p (m t)"),
                                             ps[3 + g], ACT.Copy).then_inc(pt_act, 1)

            @block.vector
            def _(ve):
                ch = Chain(ve, dve)
                ln.vector_stats(ch, 0)
                ln.vector_norm(ve, 0)

                def take_v(n):
                    ve.wait_ge(v_mm, BASE + n + 1)
                    ve.wait_ge(o_mm, BASE + n)
                    nc.vector.tensor_copy(v[:, :], ps[2]).then_inc(v_sb, 1)

                take_v(0)
                with ve.Fori(0, NT) as i:
                    ch.turn(i, 7)
                    ln.vector_stats(ch, i + 1)
                    ve.wait_ge(kT_mm, BASE + i + 1)
                    ve.wait_ge(s_mm, BASE + i)
                    nc.vector.tensor_copy(kT[:, :, :].rearrange("p m t -> p (m t)"),
                                          ps[1]).then_inc(kT_sb, 1)
                    ln.vector_norm(ve, i + 1)
                    ve.wait_ge(s_mm, BASE + i + 1)
                    s4 = S_BANKS.rearrange("p g (m s) -> p g m s", m=DK)
                    ch.link(nc.vector.tensor_reduce(mx[:, :].rearrange("p (g m) -> p g m", g=HH), s4,
                                                    AX.X, ALU.max))
                    ve.wait_ge(e_sb, BASE + 2 * i)
                    for g in range(HH):
                        part = sc[:, g * DK:(g + 1) * DK, :]
                        ins = nc.vector.tensor_tensor(part, s4[:, g],
                                                      mx[:, g * DK:(g + 1) * DK].unsqueeze(2).to_broadcast([P, DK, S]),
                                                      ALU.subtract)
                    ins.then_inc(sub_done, 1)
                    ve.wait_ge(e_sb, BASE + 2 * i + 2)
                    for u in range(2):
                        tok = slice(u * S, (u + 1) * S)
                        ins = nc.vector.tensor_reduce(sums[tok, :], pf[tok, :, tok], AX.X, ALU.add)
                        if u == 0:
                            ins.then_inc(dve, 1)
                            ch.n += 1
                    ch.link(ins)
                    ve.sem_inc(summed, 1)
                    ch.link(nc.vector.reciprocal(rs[:, :], sums[:, :]))
                    for g in range(2, HH):
                        ve.wait_ge(pt_mm, BASE + 4 * i + g + 1)
                        ve.wait_ge(o_mm, BASE + i)
                        nc.vector.tensor_copy(pT[:, g * DK:(g + 1) * DK, :].rearrange("p m t -> p (m t)"),
                                              ps[3 + g]).then_inc(pt_dve, 1)
                    ve.wait_ge(o_mm, BASE + i + 1)
                    r = rs[:, :].rearrange("p (hh m) -> p m hh", hh=HH).unsqueeze(3)
                    ch.link(nc.vector.tensor_tensor(
                        o[:, :].rearrange("p (m hh d) -> p m hh d", m=DK, hh=HH),
                        ps[7].rearrange("p (m hh d) -> p m hh d", m=DK, hh=HH),
                        r.to_broadcast([P, DK, HH, DH0]), ALU.mult))
                    ve.sem_inc(o_read, 1)
                    nc.vector.tensor_tensor(x[:, i, :], x[:, i, :], o[:, :], ALU.add)
                    take_v(i + 1)
                    assert ch.n == 7, ch.n


def expert_layer(nc, a, e):
    x, cn, ps, ones, ident, sem, W1 = e.x, e.cn, e.ps, e.ones, e.ident, e.sem, e.W1
    xg_d, yg_d = e.xg_d, e.yg_d
    tri = cn[:, CN_TRI:CN_TRI + P]
    iota = cn[:, CN_IOTA:CN_IOTA + NT * NE].rearrange("p (t e) -> p t e", t=NT)
    FK = FE // P
    HFE = FE // 2
    NFC = DK * 2 * FE
    with ExitStack() as st:
        def sbuf(name, shape, dt=F32):
            return st.enter_context(nc.sbuf_tensor(name, shape, dt))

        xn = sbuf("xnall3", [P, NT, D])
        slot = sbuf("slot3", [P, NT, 2], U32)
        top = sbuf("top3", [P, NT, 2])
        owner = sbuf("owner3", [1, ET], I32)
        s_slot, s_owner = sem("s_slot3"), sem("s_owner3")
        s_scat = sem("s_scat3", pool_dma=True)

        with ExitStack() as rt:
            def rbuf(name, shape, dt=F32):
                return rt.enter_context(nc.sbuf_tensor(name, shape, dt))

            xT = rbuf("xT3", [P, DK, P])
            gate = rbuf("gate3", [P, DK, NE])
            ln = Norm(nc, e, "3", rbuf, ps[7], xT)
            TE = [P, NT, NE]
            logit, prob, prob2 = rbuf("logit3", TE), rbuf("prob3", TE), rbuf("prob23", TE)
            eq, cand = rbuf("eq3", TE), rbuf("cand3", TE)
            oh = [rbuf("oh13", TE), rbuf("oh23", TE)]
            both, before, place, pick = rbuf("both3", TE), rbuf("before3", TE), rbuf("place3", TE), rbuf("pick3", TE)
            r8, first = rbuf("r83", [P, NT]), rbuf("first3", [P, NT])
            total, tiles, ends, starts = (rbuf(n, [P, NE]) for n in ("total3", "tiles3", "ends3", "starts3"))
            slotf = rbuf("slotf3", [P, NT])
            under = rbuf("under3", [1, ET, NE])
            ownf = rbuf("ownf3", [1, ET])
            s_gate, g_mm, kept = sem("s_gate3"), sem("g_mm3"), sem("kept3")
            s_max, s_exp, s_cnt, s_pos = sem("s_max3"), sem("s_exp3"), sem("s_cnt3"), sem("s_pos3")
            dve = sem("dve3")

            def wide(ap, shape=TE):
                return ap.unsqueeze(2).to_broadcast(shape)

            e.open_sems()
            with nc.Block() as block:
                @block.sync
                def _(sp):
                    sp.dma_start(gate[:, :, :], a["gate"]).then_inc(s_gate, 16)
                    for dst, name in ((e.wq4, "wq4"), (e.wk4, "wk4"), (e.wv4, "wv4"), (e.wo4, "wo4")):
                        sp.dma_start(dst, a[name]).then_inc(e.s_w4, 16)

                @block.gpsimd
                def _(pool):
                    ln.pool(pool, 0)
                    with pool.Fori(0, NT) as i:
                        pool.wait_ge(ln.norm, BASE + i + 1)
                        nc.gpsimd.tensor_copy(xn[:, i, :], ln.xn[:, :]).then_inc(kept, 1)
                        ln.pool(pool, i + 1)
                    pool.wait_ge(kept, BASE + NT)
                    pool.wait_ge(e.s_xg0, BASE + 16 * ET)
                    pool.wait_ge(s_slot, BASE + 2)
                    for t in range(NT):
                        for c in range(2):
                            nc.gpsimd.indirect_dma_start(
                                out=xg_d, out_offset=bass.IndirectOffsetOnAxis(slot[:, t, c:c + 1], axis=0),
                                in_=xn[:, t, :], in_offset=None).then_inc(s_scat, 16)
                    pool.wait_ge(s_scat, 16 * 2 * NT)

                @block.tensor
                def _(pe):
                    ln.tensor(pe, 0)
                    pe.wait_ge(s_gate, BASE + 16)
                    with pe.Fori(0, NT) as i:
                        pe.wait_ge(ln.xT_ready, BASE + i + 1)
                        for k in range(DK):
                            mm = nc.tensor.matmul(ps[0][:, bass.ds(i * NE, NE)], xT[:, k, :], gate[:, k, :],
                                                  start=(k == 0), stop=(k == DK - 1))
                        mm.then_inc(g_mm, 1)
                        ln.tensor(pe, i + 1)
                    pe.wait_ge(s_cnt, BASE + 1)
                    nc.tensor.matmul(ps[1][:, 0:NE], ones, total[:, :], start=True, stop=True)
                    nc.tensor.matmul(ps[2][:, 0:NT * NE], tri, both[:, :, :].rearrange("p t e -> p (t e)"),
                                     start=True, stop=False)
                    nc.tensor.matmul(ps[2][:, 0:NT * NE], ones, before[:, :, :].rearrange("p t e -> p (t e)"),
                                     start=False, stop=True).then_inc(s_pos, 1)

                @block.scalar
                def _(act):
                    ln.scalar(act, 0, g_mm)
                    with act.Fori(0, NT) as i:
                        ln.scalar(act, i + 1, g_mm)
                    act.wait_ge(s_max, BASE + 1)
                    nc.scalar.activation(prob[:, :, :], logit[:, :, :], ACT.Exp).then_inc(s_exp, 1)

                @block.vector
                def _(ve):
                    ch = Chain(ve, dve)
                    ln.vector_stats(ch, 0)
                    ln.vector_norm(ve, 0)
                    with ve.Fori(0, NT) as i:
                        ch.turn(i, 2)
                        ln.vector_stats(ch, i + 1)
                        ve.wait_ge(kept, BASE + i + 1)
                        ln.vector_norm(ve, i + 1)
                    ch.base, ch.n = 2 + 2 * NT, 0
                    ve.wait_ge(g_mm, BASE + NT)
                    lg = ps[0][:, 0:NT * NE].rearrange("p (t e) -> p t e", t=NT)
                    ch.link(nc.vector.tensor_reduce(r8[:, :], lg, AX.X, ALU.max))
                    nc.vector.tensor_tensor(logit[:, :, :], lg, wide(r8[:, :]), ALU.subtract).then_inc(s_max, 1)
                    ve.wait_ge(s_exp, BASE + 1)
                    ch.link(nc.vector.tensor_reduce(r8[:, :], prob[:, :, :], AX.X, ALU.add))
                    ch.link(nc.vector.reciprocal(first[:, :], r8[:, :]))
                    ch.link(nc.vector.tensor_tensor(prob[:, :, :], prob[:, :, :], wide(first[:, :]), ALU.mult))
                    for c, p in ((0, prob), (1, prob2)):
                        ch.link(nc.vector.tensor_reduce(top[:, :, c], p[:, :, :], AX.X, ALU.max))
                        ch.link(nc.vector.tensor_tensor(eq[:, :, :], p[:, :, :], wide(top[:, :, c]), ALU.is_equal))
                        ch.link(nc.vector.tensor_tensor(cand[:, :, :], eq[:, :, :], iota, ALU.mult))
                        ch.link(nc.vector.tensor_reduce(first[:, :], cand[:, :, :], AX.X, ALU.min))
                        ch.link(nc.vector.tensor_tensor(oh[c][:, :, :], iota, wide(first[:, :]), ALU.is_equal))
                        if c == 0:
                            ch.link(nc.vector.scalar_tensor_tensor(prob2[:, :, :], oh[0][:, :, :], -2.0,
                                                                   prob[:, :, :], ALU.mult, ALU.add))
                    ch.link(nc.vector.tensor_tensor(both[:, :, :], oh[0][:, :, :], oh[1][:, :, :], ALU.add))
                    ch.link(nc.vector.memset(before[:, 0, :], 0.0))
                    for t in range(1, NT):
                        ch.link(nc.vector.tensor_tensor(before[:, t, :], before[:, t - 1, :], both[:, t - 1, :],
                                                        ALU.add))
                    nc.vector.tensor_tensor(total[:, :], before[:, NT - 1, :], both[:, NT - 1, :],
                                            ALU.add).then_inc(s_cnt, 1)
                    ve.wait_ge(s_pos, BASE + 1)
                    ch.link(nc.vector.tensor_scalar(tiles[:, :], ps[1][:, 0:NE], (P - 1) / 2.0, 1.0 / P,
                                                    ALU.add, ALU.mult))
                    ch.link(nc.vector.tensor_scalar(tiles[:, :], tiles[:, :], ROUND, ROUND, ALU.add, ALU.subtract))
                    ch.link(nc.vector.tensor_tensor_scan(ends[:, :], ones[:, 0:NE], tiles[:, :], 0.0,
                                                         ALU.mult, ALU.add))
                    ch.link(nc.vector.tensor_tensor(starts[:, :], ends[:, :], tiles[:, :], ALU.subtract))
                    ch.link(nc.vector.tensor_scalar(starts[:, :], starts[:, :], float(P), None, ALU.mult))
                    ch.link(nc.vector.tensor_tensor(
                        under[:, :, :], ends[0:1, :].unsqueeze(1).to_broadcast([1, ET, NE]),
                        cn[0:1, CN_TILE:CN_TILE + ET * NE].rearrange("p (j e) -> p j e", j=ET), ALU.is_le))
                    ch.link(nc.vector.tensor_reduce(ownf[:, :], under[:, :, :], AX.X, ALU.add))
                    nc.vector.tensor_scalar(owner[:, :], ownf[:, :], float(NE - 1), None, ALU.min).then_inc(s_owner, 1)
                    ch.link(nc.vector.tensor_tensor(
                        place[:, :, :], ps[2][:, 0:NT * NE].rearrange("p (t e) -> p t e", t=NT),
                        starts[:, :].unsqueeze(1).to_broadcast(TE), ALU.add))
                    for c in range(2):
                        ch.link(nc.vector.tensor_tensor(pick[:, :, :], place[:, :, :], oh[c][:, :, :], ALU.mult))
                        ch.link(nc.vector.tensor_reduce(slotf[:, :], pick[:, :, :], AX.X, ALU.add))
                        nc.vector.tensor_copy(slot[:, :, c], slotf[:, :]).then_inc(s_slot, 1)

        xg = sbuf("xg3", [P, 2, D])
        xgT = sbuf("xgT3", [P, DK, P])
        gated, hid = sbuf("gated3", [P, FE]), sbuf("hid3", [P, FE])
        hT = sbuf("hT3", [P, FK, P])
        y = sbuf("y3", [P, 2, D])
        yb = sbuf("yb3", [P, 4, D])
        fc = [W1[:, u * 9216:u * 9216 + NFC].rearrange("p (k n) -> p k n", k=DK) for u in range(2)]
        pj = [W1[:, u * 9216 + NFC:(u + 1) * 9216].rearrange("p (k n) -> p k n", k=FK) for u in range(2)]
        s_fc, s_pj = [sem("s_fc3_0"), sem("s_fc3_1")], [sem("s_pj3_0"), sem("s_pj3_1")]
        xg_in, y_out = [sem("xg_in3_0"), sem("xg_in3_1")], [sem("y_out3_0"), sem("y_out3_1")]
        tr_mm, xgT_sb, a_mm, gl_mm = sem("tr_mm3"), sem("xgT_sb3"), sem("a_mm3"), sem("gl_mm3")
        silu_sb, hid_sb, hT_mm, hT_sb = sem("silu_sb3"), sem("hid_sb3"), sem("hT_mm3"), sem("hT_sb3")
        y_mm, y_sb = sem("y_mm3"), sem("y_sb3")
        s_yb = [sem(f"s_yb3_{n}", pool_dma=True) for n in range(2)]
        added, half = sem("added3"), sem("half3")
        TURNS = (ET - 3) // 2

        def steps(eng, step):
            step(0, 0, 0)
            step(1, 1, 0)
            with eng.Fori(0, TURNS) as i:
                step(2 * i + 2, 0, i + 1)
                step(2 * i + 3, 1, i + 1)
            step(ET - 1, 0, TURNS + 1)

        e.open_sems()
        with nc.Block() as block:
            @block.sync
            def _(sp):
                sp.wait_ge(s_owner, BASE + 1)

                def step(s, u, pair):
                    first = isinstance(s, int) and s < 2
                    own = sp.value_load(owner[0:1, bass.ds(s, 1)], min_val=0, max_val=NE - 1)
                    if not first:
                        sp.wait_ge(tr_mm, BASE + s - 1)
                    sp.dma_start(xg[:, u, :], xg_d[bass.ds(s * P, P), :]).then_inc(xg_in[u], 16)
                    if not first:
                        sp.wait_ge(gl_mm, BASE + s - 1)
                    sp.dma_start(fc[u], a["fc"][bass.ds(own, 1)].rearrange("o p k n -> (o p) k n")).then_inc(s_fc[u], 16)
                    if not first:
                        sp.wait_ge(y_mm, BASE + s - 1)
                    sp.dma_start(pj[u], a["proj"][bass.ds(own, 1)].rearrange("o p k n -> (o p) k n")).then_inc(s_pj[u], 16)
                    if not first:
                        store(s - 2, u)

                def store(s, u):
                    sp.wait_ge(y_sb, BASE + s + 1)
                    sp.dma_start(yg_d[bass.ds(s * P, P), :], y[:, u, :]).then_inc(y_out[u], 16)

                steps(sp, step)
                store(ET - 2, 1)
                store(ET - 1, 0)
                for u in range(2):
                    sp.wait_ge(y_out[u], BASE + 16 * ((ET + 1 - u) // 2))

            @block.tensor
            def _(pe):
                def out_proj(s, u, pair):
                    pe.wait_ge(hid_sb, BASE + s + 1)
                    pe.wait_ge(hT_sb, BASE + 2 * s)
                    for g in range(2):
                        for f in range(FK // 2):
                            tr = nc.tensor.transpose(ps[5 + g][:, f * P:(f + 1) * P],
                                                     hid[:, (g * FK // 2 + f) * P:(g * FK // 2 + f + 1) * P], ident)
                        tr.then_inc(hT_mm, 1)
                    pe.wait_ge(s_pj[u], BASE + 16 * pair + 16)
                    pe.wait_ge(y_sb, BASE + s)
                    for f in range(FK):
                        if f % (FK // 2) == 0:
                            pe.wait_ge(hT_sb, BASE + 2 * s + 1 + f // (FK // 2))
                        mm = nc.tensor.matmul(ps[7], hT[:, f, :], pj[u][:, f, :], start=(f == 0), stop=(f == FK - 1))
                    mm.then_inc(y_mm, 1)

                def step(s, u, pair):
                    pe.wait_ge(xg_in[u], BASE + 16 * pair + 16)
                    pe.wait_ge(xgT_sb, BASE + s)
                    for k in range(DK):
                        tr = nc.tensor.transpose(ps[4][:, k * P:(k + 1) * P], xg[:, u, k * P:(k + 1) * P], ident)
                    tr.then_inc(tr_mm, 1)
                    if not (isinstance(s, int) and s < 2):
                        out_proj(s - 2, u, pair - 1)
                    pe.wait_ge(xgT_sb, BASE + s + 1)
                    pe.wait_ge(s_fc[u], BASE + 16 * pair + 16)
                    for c in range(4):
                        pe.wait_ge(silu_sb if c < 2 else hid_sb, BASE + s)
                        for k in range(DK):
                            mm = nc.tensor.matmul(ps[c][:, 0:HFE], xgT[:, k, :], fc[u][:, k, c * HFE:(c + 1) * HFE],
                                                  start=(k == 0), stop=(k == DK - 1))
                        if c == 1:
                            mm.then_inc(a_mm, 1)
                    mm.then_inc(gl_mm, 1)

                steps(pe, step)
                out_proj(ET - 2, 1, (ET - 2) // 2)
                out_proj(ET - 1, 0, (ET - 1) // 2)

            @block.scalar
            def _(act):
                def hidden_out(s):
                    act.wait_ge(y_mm, BASE + s)
                    for g in range(2):
                        act.wait_ge(hT_mm, BASE + 2 * s + g + 1)
                        n = FK // 2
                        nc.scalar.activation(hT[:, g * n:(g + 1) * n, :].rearrange("p f t -> p (f t)"),
                                             ps[5 + g][:, 0:n * P], ACT.Copy).then_inc(hT_sb, 1)

                def step(s, u, pair):
                    act.wait_ge(tr_mm, BASE + s + 1)
                    act.wait_ge(gl_mm, BASE + s)
                    nc.scalar.activation(xgT[:, :, :].rearrange("p k t -> p (k t)"), ps[4],
                                         ACT.Copy).then_inc(xgT_sb, 1)
                    if not (isinstance(s, int) and s < 2):
                        hidden_out(s - 2)
                    act.wait_ge(a_mm, BASE + s + 1)
                    act.wait_ge(hid_sb, BASE + s)
                    for c in range(2):
                        ins = nc.scalar.activation(gated[:, c * HFE:(c + 1) * HFE], ps[c][:, 0:HFE], ACT.Silu)
                    ins.then_inc(silu_sb, 1)

                steps(act, step)
                hidden_out(ET - 2)
                hidden_out(ET - 1)

            @block.vector
            def _(ve):
                def y_take(s, u, pair):
                    ve.wait_ge(y_mm, BASE + s + 1)
                    ve.wait_ge(y_out[u], BASE + 16 * pair)
                    nc.vector.tensor_copy(y[:, u, :], ps[7]).then_inc(y_sb, 1)

                def step(s, u, pair):
                    if not (isinstance(s, int) and s < 2):
                        y_take(s - 2, u, pair - 1)
                    ve.wait_ge(silu_sb, BASE + s + 1)
                    ve.wait_ge(gl_mm, BASE + s + 1)
                    ve.wait_ge(hT_mm, BASE + 2 * s)
                    for c in range(2):
                        ins = nc.vector.tensor_tensor(hid[:, c * HFE:(c + 1) * HFE], gated[:, c * HFE:(c + 1) * HFE],
                                                      ps[2 + c][:, 0:HFE], ALU.mult)
                    ins.then_inc(hid_sb, 1)

                steps(ve, step)
                y_take(ET - 2, 1, (ET - 2) // 2)
                y_take(ET - 1, 0, (ET - 1) // 2)
                for t in range(NT):
                    ve.wait_ge(s_yb[t % 2], 32 * (t // 2 + 1))
                    for c in range(2):
                        ins = nc.vector.scalar_tensor_tensor(x[:, t, :], yb[:, t % 2 * 2 + c, :], top[:, t, c:c + 1],
                                                             x[:, t, :], ALU.mult, ALU.add)
                        if c == 0:
                            ins.then_inc(half, 1)
                            ve.wait_ge(half, BASE + t + 1)
                    ins.then_inc(added, 1)

            @block.gpsimd
            def _(pool):
                for u in range(2):
                    pool.wait_ge(y_out[u], BASE + 16 * ((ET + 1 - u) // 2))
                for t in range(NT):
                    if t >= 2:
                        pool.wait_ge(added, BASE + t - 1)
                    for c in range(2):
                        nc.gpsimd.indirect_dma_start(
                            out=yb[:, t % 2 * 2 + c, :], out_offset=None, in_=yg_d,
                            in_offset=bass.IndirectOffsetOnAxis(slot[:, t, c:c + 1], axis=0)).then_inc(s_yb[t % 2], 16)


def cross_attention_layer(nc, a, e):
    x, cn, ps, ones, ident, sem, W0, W1 = e.x, e.cn, e.ps, e.ones, e.ident, e.sem, e.W0, e.W1
    wq4, wk4, wv4, wo4 = e.wq4, e.wk4, e.wv4, e.wo4
    MK = HC // P
    PAIRS = 2 * MK
    JK = J // P
    SCALE = DH1 ** -0.5
    U_Q, U_QT, U_QP, U_U, U_O, U_Y, USES = 0, 2, 4, 16, 28, 30, 32
    BANKS = 2
    with ExitStack() as st:
        def sbuf(name, shape, dt=F32):
            return st.enter_context(nc.sbuf_tensor(name, shape, dt))

        cT, cN = sbuf("cT4", [P, 2, CK, J]), sbuf("cN4", [P, 2, JK, C])
        qp = W1[:, 10240:16384].rearrange("p (b c h t) -> p b c h t", b=2, c=CK, h=H1)
        pT = [W1[:, 16384:18432].rearrange("p (j n) -> p j n", j=JK),
              W0[:, 14336:16384].rearrange("p (j n) -> p j n", j=JK)]
        pb = sbuf("pb4", [P, 4, J])
        qo = sbuf("qo4", [P, HC])
        oT = qo[:, :].rearrange("p (m t) -> p m t", m=MK)
        qT = sbuf("qT4", [P, MK, P])
        ys = sbuf("ys4", [P, D])
        nmax, rsum, rinv = sbuf("nmax4", [P, 4]), sbuf("rsum4", [P, 4]), sbuf("rinv4", [P, 4])
        bo = sbuf("bo4", [1, D])
        xT = sbuf("xT4", [P, DK, P])
        ln = Norm(nc, e, "4", sbuf, ps[6], xT)
        s_cT, s_cN = [sem("s_cT4_0"), sem("s_cT4_1")], [sem("s_cN4_0"), sem("s_cN4_1")]
        s_bo, w_mm, w_sb = sem("s_bo4"), sem("w_mm4"), sem("w_sb4")
        s_mm, m_dve, e_sb, p_dve = sem("s_mm4"), sem("m_dve4"), sem("e_sb4"), sem("p_dve4")
        pt_mm, pt_sb, added, dve = sem("pt_mm4"), sem("pt_sb4"), sem("added4"), sem("dve4")
        work = [ps[4], ps[5]]

        e.open_sems()
        with nc.Block() as block:
            @block.sync
            def _(sp):
                sp.dma_start(bo[:, :], a["bo4"]).then_inc(s_bo, 16)
                for u in range(2):
                    sp.dma_start(cT[:, u], a["ctxT"][u]).then_inc(s_cT[u], 16)
                    sp.dma_start(cN[:, u], a["ctxN"][u]).then_inc(s_cN[u], 16)
                sp.dma_start(e.w5, a["w5"]).then_inc(e.s_w5, 16)
                with sp.Fori(0, NT - 1) as i:
                    for u in range(2):
                        sp.wait_ge(s_mm, BASE + PAIRS * i + MK * (u + 1))
                        sp.dma_start(cT[:, u], a["ctxT"][2 * i + 2 + u]).then_inc(s_cT[u], 16)
                        sp.wait_ge(w_mm, BASE + USES * i + U_U + 6 * (u + 1))
                        sp.dma_start(cN[:, u], a["ctxN"][2 * i + 2 + u]).then_inc(s_cN[u], 16)

            @block.gpsimd
            def _(pool):
                ln.pool(pool, 0)
                with pool.Fori(0, NT) as i:
                    ln.pool(pool, i + 1)

            @block.tensor
            def _(pe):
                def work_bank(i, use):
                    pe.wait_ge(w_sb, BASE + USES * i + use + 1)
                    return work[use % BANKS]

                def taken(i, use):
                    pe.wait_ge(w_sb, BASE + USES * i + use + 1 + BANKS)

                def scores(i, g):
                    b, m = g // MK, g % MK
                    if m == 0:
                        pe.wait_ge(s_cT[b], BASE + 16 * i + 16)
                    pe.wait_ge(e_sb, BASE + PAIRS * i + g + 1)
                    for c in range(CK):
                        mm = nc.tensor.matmul(ps[g % BANKS], qp[:, b, c, 2 * m:2 * m + 2, :].rearrange("p h t -> p (h t)"),
                                              cT[:, b, c, :], start=(c == 0), stop=(c == CK - 1))
                    mm.then_inc(s_mm, 1)

                def turn(i, g):
                    pe.wait_ge(p_dve, BASE + PAIRS * i + g + 1)
                    pe.wait_ge(pt_sb, BASE + PAIRS * i + g + 1)
                    for j in range(JK):
                        tr = nc.tensor.transpose(ps[2 + g % BANKS][:, j * P:(j + 1) * P],
                                                 pb[:, g % 4, j * P:(j + 1) * P], ident)
                    tr.then_inc(pt_mm, 1)

                def weigh(i, h):
                    b = h // 2
                    if h % 2 == 0:
                        pe.wait_ge(s_cN[b], BASE + 16 * i + 16)
                    pe.wait_ge(pt_sb, BASE + PAIRS * i + 4 * h + 4 + BANKS)
                    for c in range(CK):
                        bank = work_bank(i, U_U + 3 * h + c)
                        for j in range(JK):
                            mm = nc.tensor.matmul(bank, cN[:, b, j, c * P:(c + 1) * P], pT[h % 2][:, j, :],
                                                  start=(j == 0), stop=(j == JK - 1))
                        mm.then_inc(w_mm, 1)

                ln.tensor(pe, 0)
                pe.wait_ge(e.s_w4, BASE + 64)
                pe.wait_ge(s_bo, BASE + 16)
                with pe.Fori(0, NT) as i:
                    pe.wait_ge(ln.xT_ready, BASE + i + 1)
                    for n in range(2):
                        bank = work_bank(i, U_Q + n)
                        for k in range(DK):
                            mm = nc.tensor.matmul(bank, xT[:, k, :], wq4[:, k, n * 512:(n + 1) * 512],
                                                  start=(k == 0), stop=(k == DK - 1))
                        mm.then_inc(w_mm, 1)
                    ln.tensor(pe, i + 1)
                    for n in range(2):
                        taken(i, U_Q + n)
                        bank = work_bank(i, U_QT + n)
                        for m in range(4):
                            tr = nc.tensor.transpose(bank[:, m * P:(m + 1) * P],
                                                     qo[:, (4 * n + m) * P:(4 * n + m + 1) * P], ident)
                        tr.then_inc(w_mm, 1)
                    use = U_QP
                    for n in range(2):
                        taken(i, U_QT + n)
                        for r in range(2):
                            part = slice(r * DH1, (r + 1) * DH1)
                            for c in range(CK):
                                bank = work_bank(i, use)
                                for m in range(4):
                                    mm = nc.tensor.matmul(bank[:, m * P:(m + 1) * P],
                                                          wk4[part, 4 * n + m, c * P:(c + 1) * P],
                                                          qT[part, 4 * n + m, :], start=True, stop=True)
                                mm.then_inc(w_mm, 1)
                                use += 1
                    taken(i, U_U - 1)
                    scores(i, 0)
                    scores(i, 1)
                    for g in range(PAIRS):
                        if g + 2 < PAIRS:
                            scores(i, g + 2)
                        turn(i, g)
                        if g % 4 == 0 and g:
                            weigh(i, g // 4 - 1)
                    weigh(i, 3)
                    taken(i, U_O - 1)
                    for n in range(2):
                        bank = work_bank(i, U_O + n)
                        for m in range(4):
                            for r in range(2):
                                h = 2 * (4 * n + m) + r
                                for c in range(CK):
                                    mm = nc.tensor.matmul(
                                        bank[r * DH1:(r + 1) * DH1, m * P:(m + 1) * P].rearrange("p (b t) -> p b t", b=2),
                                        wv4[:, c, h * DH1:(h + 1) * DH1], qp[:, :, c, h, :],
                                        start=(c == 0), stop=(c == CK - 1))
                        mm.then_inc(w_mm, 1)
                    bank = work_bank(i, U_Y)
                    for m in range(MK):
                        if m % 4 == 0:
                            taken(i, U_O + m // 4)
                        nc.tensor.matmul(bank, oT[:, m, :], wo4[:, m, :], start=(m == 0), stop=False)
                    nc.tensor.matmul(bank, ones[0:1, :], bo[0:1, :], start=False, stop=True).then_inc(w_mm, 2)

            @block.scalar
            def _(act):
                def take(i, use, out, scale=1.0, count=1):
                    act.wait_ge(w_mm, BASE + USES * i + use + count)
                    src = work[use % BANKS]
                    if len(out.shape) == 4:
                        src = src.rearrange("p (m b t) -> p m b t", m=4, b=2)
                    nc.scalar.activation(out, src, ACT.Copy, scale=scale).then_inc(w_sb, count)

                def exponent(i, g):
                    act.wait_ge(m_dve, BASE + PAIRS * i + g + 1)
                    nc.scalar.activation(pb[:, g % 4, :], ps[g % BANKS], ACT.Exp, bias=nmax[:, g % 4:g % 4 + 1],
                                         accum_out=rsum[:, g % 4:g % 4 + 1]).then_inc(e_sb, 1)

                def weighed(i, h):
                    for c in range(CK):
                        take(i, U_U + 3 * h + c,
                             qp[:, h // 2, c, 8 * (h % 2):8 * (h % 2) + 8, :].rearrange("p h t -> p (h t)"))

                act.sem_inc(w_sb, BANKS)
                act.sem_inc(e_sb, BANKS)
                ln.scalar(act, 0, w_mm, 0)
                with act.Fori(0, NT) as i:
                    for n in range(2):
                        take(i, U_Q + n, qo[:, n * 512:(n + 1) * 512], SCALE)
                    ln.scalar(act, i + 1, w_mm, USES * i + U_Q + 2)
                    for n in range(2):
                        take(i, U_QT + n, qT[:, 4 * n:4 * n + 4, :].rearrange("p m t -> p (m t)"))
                    use = U_QP
                    for n in range(2):
                        for r in range(2):
                            for c in range(CK):
                                heads = qp[:, :, c, 8 * n + r:8 * n + 8:2, :].rearrange("p b m t -> p m b t")
                                take(i, use, heads)
                                use += 1
                    for g in range(PAIRS):
                        exponent(i, g)
                        if g % 4 == 2 and g > 2:
                            weighed(i, g // 4 - 1)
                    weighed(i, 3)
                    for n in range(2):
                        take(i, U_O + n, qo[:, n * 512:(n + 1) * 512])
                    act.wait_ge(added, BASE + i)
                    take(i, U_Y, ys[:, :], count=2)

            @block.vector
            def _(ve):
                ch = Chain(ve, dve)

                def maximum(i, g):
                    ve.wait_ge(s_mm, BASE + PAIRS * i + g + 1)
                    nc.vector.tensor_reduce(nmax[:, g % 4:g % 4 + 1], ps[g % BANKS], AX.X, ALU.max,
                                            negate=True).then_inc(m_dve, 1)

                ve.sem_inc(pt_sb, BANKS)
                ln.vector_stats(ch, 0)
                ln.vector_norm(ve, 0)
                with ve.Fori(0, NT) as i:
                    ch.turn(i, 2 + PAIRS)
                    ln.vector_stats(ch, i + 1)
                    ln.vector_norm(ve, i + 1)
                    maximum(i, 0)
                    maximum(i, 1)
                    for g in range(PAIRS):
                        ve.wait_ge(e_sb, BASE + PAIRS * i + g + 1 + BANKS)
                        r = rinv[:, g % 4:g % 4 + 1]
                        ch.link(nc.vector.reciprocal(r, rsum[:, g % 4:g % 4 + 1]))
                        nc.vector.tensor_scalar(pb[:, g % 4, :], pb[:, g % 4, :], r, None, ALU.mult).then_inc(p_dve, 1)
                        if g + 2 < PAIRS:
                            maximum(i, g + 2)
                        ve.wait_ge(pt_mm, BASE + PAIRS * i + g + 1)
                        nc.vector.tensor_copy(pT[g // 4 % 2][:, :, (g % 4) * P:(g % 4 + 1) * P],
                                              ps[2 + g % BANKS].rearrange("p (j n) -> p j n", j=JK)).then_inc(pt_sb, 1)
                    ve.wait_ge(w_sb, BASE + USES * (i + 1) + BANKS)
                    nc.vector.tensor_tensor(x[:, i, :], x[:, i, :], ys[:, :], ALU.add).then_inc(added, 1)


def decayed_attention_layer(nc, a, e):
    x, cn, ps, ones, ident, sem, w5, W0 = e.x, e.cn, e.ps, e.ones, e.ident, e.sem, e.w5, e.W0
    v_d, ba_d = e.v_d, e.ba_d
    sel = cn[:, CN_SEL:CN_SEL + B]
    G = 8
    NG = S // G
    with ExitStack() as st:
        def sbuf(name, shape, dt=F32):
            return st.enter_context(nc.sbuf_tensor(name, shape, dt))

        ba = sbuf("ba5", [P, NT, 2 * HS])
        baT = sbuf("baT5", [2 * HS, B * S])
        s_v, s_ba, baT_sb = sem("s_v5"), sem("s_ba5"), sem("baT_sb5")

        with ExitStack() as pt:
            def pbuf(name, shape, dt=F32):
                return pt.enter_context(nc.sbuf_tensor(name, shape, dt))

            xT = pbuf("xT5", [P, DK, P])
            ln = Norm(nc, e, "5", pbuf, ps[7], xT)
            q, qk, mag, ex, lg, soft = (pbuf(n, [P, D]) for n in ("q5", "qk5", "mag5", "ex5", "lg5", "soft5"))
            v0, ve_, vv = pbuf("v05", [P, D]), pbuf("veps5", [P, D]), pbuf("vv5", [P, 2, D])
            bal = pbuf("bal5", [1, D])
            s_bal, q_mm, k_mm, v_mm, a_mm = sem("s_bal5"), sem("q_mm5"), sem("k_mm5"), sem("v_mm5"), sem("a_mm5")
            q_sb, mag_sb, ex_sb, lg_sb = sem("q_sb5"), sem("mag_sb5"), sem("ex_sb5"), sem("lg_sb5")
            k_used, v_used, a_used, v_sb, vv_sb = sem("k_used5"), sem("v_used5"), sem("a_used5"), sem("v_sb5"), sem("vv_sb5")
            v_out = [sem("v_out5_0"), sem("v_out5_1")]
            ba_sb, t_mm, dve = sem("ba_sb5"), sem("t_mm5"), sem("dve5")

            e.open_sems()
            with nc.Block() as block:
                @block.sync
                def _(sp):
                    sp.dma_start(bal[:, :], a["ba5"]).then_inc(s_bal, 16)
                    sp.dma_start(e.w16, a["w16"]).then_inc(e.s_w6, 16)
                    sp.dma_start(e.w26, a["w26"]).then_inc(e.s_w6, 16)
                    with sp.Fori(0, NT // 2) as i:
                        for u in range(2):
                            sp.wait_ge(vv_sb, BASE + 2 * i + u + 1)
                            sp.dma_start(v_d[bass.ds((2 * i + u) * P, P), :], vv[:, u, :]).then_inc(v_out[u], 16)
                    sp.wait_ge(baT_sb, BASE + 2)
                    for c in range(2):
                        sp.dma_start(ba_d[c].rearrange("(b h) t -> h b t", b=B),
                                     baT[c * HS:(c + 1) * HS, :].rearrange("h (b t) -> h b t", b=B)).then_inc(s_ba, 16)
                    for u in range(2):
                        sp.wait_ge(v_out[u], BASE + 16 * NT // 2)
                    sp.wait_ge(s_ba, BASE + 32)

                @block.gpsimd
                def _(pool):
                    ln.pool(pool, 0)
                    with pool.Fori(0, NT) as i:
                        ln.pool(pool, i + 1)

                @block.tensor
                def _(pe):
                    ln.tensor(pe, 0)
                    pe.wait_ge(e.s_w5, BASE + 16)
                    pe.wait_ge(s_bal, BASE + 16)
                    with pe.Fori(0, NT) as i:
                        pe.wait_ge(ln.xT_ready, BASE + i + 1)
                        for bank, w, done, used in ((0, 0, q_mm, q_sb), (1, 3, a_mm, a_used),
                                                    (2, 1, k_mm, k_used), (3, 2, v_mm, v_used)):
                            pe.wait_ge(used, BASE + i)
                            for k in range(DK):
                                mm = nc.tensor.matmul(ps[bank], xT[:, k, :], w5[:, w, k, :], start=(k == 0),
                                                      stop=(w != 3 and k == DK - 1))
                            if w == 3:
                                mm = nc.tensor.matmul(ps[bank], ones[0:1, :], bal[0:1, :], start=False, stop=True)
                            mm.then_inc(done, 1)
                        ln.tensor(pe, i + 1)
                    pe.wait_ge(ba_sb, BASE + 2 * NT)
                    for t in range(NT):
                        tr = nc.tensor.transpose(ps[4 + t // 4][0:2 * HS, t % 4 * P:(t % 4 + 1) * P], ba[:, t, :], ident)
                        if t % 4 == 3:
                            tr.then_inc(t_mm, 1)

                @block.scalar
                def _(act):
                    ln.scalar(act, 0, v_mm)
                    with act.Fori(0, NT) as i:
                        act.wait_ge(q_mm, BASE + i + 1)
                        act.wait_ge(k_used, BASE + i)
                        nc.scalar.activation(q[:, :], ps[0], ACT.Copy, scale=DHS ** -0.5).then_inc(q_sb, 1)
                        act.wait_ge(a_mm, BASE + i + 1)
                        nc.scalar.activation(mag[:, :], ps[1], ACT.Abs).then_inc(mag_sb, 1)
                        act.wait_ge(mag_sb, BASE + i + 1)
                        nc.scalar.activation(ex[:, :], mag[:, :], ACT.Exp, scale=-1.0).then_inc(ex_sb, 1)
                        act.wait_ge(ex_sb, BASE + i + 1)
                        act.wait_ge(a_used, BASE + i)
                        nc.scalar.activation(lg[:, :], ex[:, :], ACT.Ln, bias=cn[:, CN_ONE:CN_ONE + 1]).then_inc(lg_sb, 1)
                        ln.scalar(act, i + 1, v_mm)
                    for g in range(2):
                        act.wait_ge(t_mm, BASE + g + 1)
                        nc.scalar.activation(baT[:, g * 512:(g + 1) * 512], ps[4 + g][0:2 * HS, :],
                                             ACT.Copy).then_inc(baT_sb, 1)

                @block.vector
                def _(ve):
                    ch = Chain(ve, dve)
                    ln.vector_stats(ch, 0)
                    ln.vector_norm(ve, 0)
                    with ve.Fori(0, NT // 2) as i2:
                        ch.turn(i2, 4)
                        for u in range(2):
                            i = 2 * i2 + u
                            ln.vector_stats(ch, i + 1)
                            ve.wait_ge(lg_sb, BASE + i + 1)
                            nc.vector.scalar_tensor_tensor(soft[:, :], ps[1], 0.0, lg[:, :], ALU.max,
                                                           ALU.add).then_inc(a_used, 1)
                            ve.wait_ge(a_used, BASE + i + 1)
                            nc.vector.tensor_reduce(ba[:, i, HS:2 * HS], soft[:, :].rearrange("p (h d) -> p h d", h=HS),
                                                    AX.X, ALU.add, negate=True).then_inc(ba_sb, 1)
                            ve.wait_ge(q_sb, BASE + i + 1)
                            ve.wait_ge(k_mm, BASE + i + 1)
                            nc.vector.tensor_tensor(qk[:, :], q[:, :], ps[2], ALU.mult).then_inc(k_used, 1)
                            ln.vector_norm(ve, i + 1)
                            ve.wait_ge(k_used, BASE + i + 1)
                            nc.vector.tensor_reduce(ba[:, i, 0:HS], qk[:, :].rearrange("p (h d) -> p h d", h=HS),
                                                    AX.X, ALU.add).then_inc(ba_sb, 1)
                            ve.wait_ge(v_mm, BASE + i + 1)
                            nc.vector.tensor_scalar(v0[:, :], ps[3], 0.0, None, ALU.add).then_inc(v_used, 1)
                            ve.wait_ge(v_used, BASE + i + 1)
                            nc.vector.tensor_scalar(ve_[:, :].bitcast(U32), v0[:, :].bitcast(U32), SIGN_BIT, EPS_BITS,
                                                    ALU.bitwise_and, ALU.bitwise_or).then_inc(v_sb, 1)
                            ve.wait_ge(v_sb, BASE + i + 1)
                            ve.wait_ge(v_out[u], BASE + 16 * i2)
                            nc.vector.tensor_tensor(vv[:, u, :], v0[:, :], ve_[:, :], ALU.add).then_inc(vv_sb, 1)
                        assert ch.n == 4

        BS = [P, S]
        bS, aS, mx, t1, t2, eA, eB, dn, rd = (sbuf(n, BS) for n in
                                              ("bS5", "aS5", "mx5", "t15", "t25", "eA5", "eB5", "dn5", "rd5"))
        al, be, eal, ebe = (sbuf(n, BS) for n in ("al5", "be5", "eal5", "ebe5"))
        vb = sbuf("vb5", [P, 2, G, D])
        W1 = e.W1
        off = 10240
        rb = W1[:, off:off + 2048].rearrange("p (n d) -> p n d", n=4)
        bv = W1[:, off + 2048:off + 3072].rearrange("p (n d) -> p n d", n=2)
        ebv = W1[:, off + 3072:off + 4096].rearrange("p (n d) -> p n d", n=2)
        ear, s_, ep, sg = (W1[:, off + 4096 + n * D:off + 4096 + (n + 1) * D] for n in range(4))
        yT = W1[:, 0:DK * B * S].rearrange("p (k n) -> p k n", k=DK)
        s_in, s_vb = sem("s_in5"), [sem("s_vb5_0"), sem("s_vb5_1")]
        t_dve, t_exp, coef = sem("t_dve5"), sem("t_exp5"), sem("coef5")
        bv_sb, ebv_sb, ear_sb, r_sb = sem("bv_sb5"), sem("ebv_sb5"), sem("ear_sb5"), sem("r_sb5")
        s_sb, sg_sb = sem("s_sb5"), sem("sg_sb5")
        y_mm, yT_sb, z_mm, z_used, ch5 = sem("y_mm5"), sem("yT_sb5"), sem("z_mm5"), sem("z_used5"), sem("ch5")
        RB = 4

        e.open_sems()
        with nc.Block() as block:
            @block.sync
            def _(sp):
                sp.dma_start(bS[:, :], ba_d[0]).then_inc(s_in, 16)
                sp.dma_start(aS[:, :], ba_d[1]).then_inc(s_in, 16)

                def load(group, u):
                    for b in range(B):
                        rows = v_d[bass.ds(group * G + b * S, G), :].rearrange("t d -> (t d)")
                        sp.dma_start(vb[b * HS:(b + 1) * HS, u].rearrange("p t d -> p (t d)"),
                                     rows.partition_broadcast(HS)).then_inc(s_vb[u], 16)

                load(0, 0)
                load(1, 1)
                with sp.Fori(0, NG // 2 - 1) as i:
                    for u in range(2):
                        sp.wait_ge(ebv_sb, BASE + 2 * G * i + G * (u + 1))
                        load(2 * i + 2 + u, u)

            @block.vector
            def _(ve):
                ch = Chain(ve, ch5)
                ve.wait_ge(s_in, BASE + 32)
                ch.link(nc.vector.memset(eA[:, 0:1], 0.0))
                ch.link(nc.vector.memset(al[:, 0:1], 0.0))
                ch.link(nc.vector.memset(rb[:, RB - 1, :], 0.0))
                ch.link(nc.vector.tensor_tensor_scan(mx[:, :], aS[:, :], bS[:, :], -3.0e38, ALU.add, ALU.max))
                ch.link(nc.vector.tensor_tensor(t1[:, 1:S], aS[:, 1:S], mx[:, 0:S - 1], ALU.add))
                nc.vector.tensor_tensor(t1[:, 1:S], t1[:, 1:S], mx[:, 1:S], ALU.subtract).then_inc(t_dve, 1)
                nc.vector.tensor_tensor(t2[:, :], bS[:, :], mx[:, :], ALU.subtract).then_inc(t_dve, 1)
                ve.wait_ge(t_exp, BASE + 2)
                ch.link(nc.vector.tensor_tensor_scan(dn[:, :], eA[:, :], eB[:, :], 0.0, ALU.mult, ALU.add))
                ch.link(nc.vector.reciprocal(rd[:, :], dn[:, :]))
                ch.link(nc.vector.tensor_tensor(al[:, 1:S], eA[:, 1:S], dn[:, 0:S - 1], ALU.mult))
                ch.link(nc.vector.tensor_tensor(al[:, 1:S], al[:, 1:S], rd[:, 1:S], ALU.mult))
                ch.link(nc.vector.tensor_tensor(be[:, :], eB[:, :], rd[:, :], ALU.mult))
                ch.link(nc.vector.tensor_scalar(eal[:, :], al[:, :], EPS, None, ALU.mult))
                ch.link(nc.vector.tensor_scalar(ebe[:, :], be[:, :], EPS, None, ALU.mult))
                nc.vector.memset(ebe[:, 0:1], 0.0).then_inc(coef, 1)
                ve.wait_ge(coef, BASE + 1)
                with ve.Fori(0, S // (2 * G)) as i:
                    for j in range(2 * G):
                        t = 2 * G * i + j
                        old, new = rb[:, (j - 1) % RB, :], rb[:, j % RB, :]
                        ve.wait_ge(r_sb, BASE + t)
                        ve.wait_ge(bv_sb, BASE + t + 1)
                        nc.vector.scalar_tensor_tensor(s_, old, al[:, bass.ds(t, 1)], bv[:, j % 2, :],
                                                       ALU.mult, ALU.add).then_inc(s_sb, 1)
                        ve.wait_ge(ebv_sb, BASE + t + 1)
                        ve.wait_ge(ear_sb, BASE + t + 1)
                        nc.vector.tensor_tensor(ep, ear, ebv[:, j % 2, :], ALU.max).then_inc(sg_sb, 1)
                        ve.wait_ge(sg_sb, BASE + 2 * t + 1)
                        ve.wait_ge(s_sb, BASE + t + 1)
                        nc.vector.scalar_tensor_tensor(sg.bitcast(U32), s_.bitcast(U32), SIGN_BIT, ep.bitcast(U32),
                                                       ALU.bitwise_and, ALU.bitwise_or).then_inc(sg_sb, 1)
                        ve.wait_ge(sg_sb, BASE + 2 * t + 2)
                        ve.wait_ge(y_mm, BASE + t + 1)
                        nc.vector.tensor_tensor(new, s_, sg, ALU.add).then_inc(r_sb, 1)
                for t in range(NT):
                    ve.wait_ge(z_mm, BASE + t + 1)
                    nc.vector.tensor_tensor(x[:, t, :], x[:, t, :], ps[2 + t % 4], ALU.add).then_inc(z_used, 1)

            @block.scalar
            def _(act):
                act.wait_ge(t_dve, BASE + 2)
                nc.scalar.activation(eA[:, 1:S], t1[:, 1:S], ACT.Exp).then_inc(t_exp, 1)
                nc.scalar.activation(eB[:, :], t2[:, :], ACT.Exp).then_inc(t_exp, 1)
                act.wait_ge(coef, BASE + 1)
                with act.Fori(0, S // (2 * G)) as i:
                    for j in range(2 * G):
                        t = 2 * G * i + j
                        u = j // G
                        if j % G == 0:
                            act.wait_ge(s_vb[u], BASE + 16 * B * (i + 1))
                        act.wait_ge(s_sb, BASE + t)
                        nc.scalar.activation(bv[:, j % 2, :], vb[:, u, j % G, :], ACT.Copy,
                                             scale=be[:, bass.ds(t, 1)]).then_inc(bv_sb, 1)
                        nc.scalar.activation(ebv[:, j % 2, :], vb[:, u, j % G, :], ACT.Abs,
                                             scale=ebe[:, bass.ds(t, 1)]).then_inc(ebv_sb, 1)
                        act.wait_ge(r_sb, BASE + t)
                        nc.scalar.activation(ear, rb[:, (j - 1) % RB, :], ACT.Abs,
                                             scale=eal[:, bass.ds(t, 1)]).then_inc(ear_sb, 1)
                    for u in range(2):
                        act.wait_ge(y_mm, BASE + 2 * G * i + G * (u + 1) + RB)
                        out = yT[:, :, :].rearrange("p k (b t) -> p k t b", b=B)[:, :, bass.ds(2 * G * i + G * u, G), :]
                        nc.scalar.activation(out, ps[u].rearrange("p (k t b) -> p k t b", k=DK, t=G),
                                             ACT.Copy).then_inc(yT_sb, 1)

            @block.tensor
            def _(pe):
                pe.sem_inc(y_mm, RB)
                with pe.Fori(0, S // (2 * G)) as i:
                    for j in range(2 * G):
                        t = 2 * G * i + j
                        u = j // G
                        if j == 0:
                            pe.wait_ge(yT_sb, BASE + 2 * i)
                        pe.wait_ge(r_sb, BASE + t + 1)
                        for k in range(DK):
                            col = k * G * B + (j % G) * B
                            mm = nc.tensor.matmul(ps[u][:, col:col + B], rb[:, j % RB, k * P:(k + 1) * P], sel,
                                                  start=True, stop=True)
                        mm.then_inc(y_mm, 1)
                pe.wait_ge(yT_sb, BASE + NG)
                for t in range(NT):
                    if t >= 4:
                        pe.wait_ge(z_used, BASE + t - 3)
                    for k in range(DK):
                        mm = nc.tensor.matmul(ps[2 + t % 4], yT[:, k, t * P:(t + 1) * P], w5[:, 4, k, :],
                                              start=(k == 0), stop=(k == DK - 1))
                    mm.then_inc(z_mm, 1)


def feed_forward_layer(nc, a, e):
    x, cn, ps, ident, sem, w16, w26, W1 = e.x, e.cn, e.ps, e.ident, e.sem, e.w16, e.w26, e.W1
    FT = FF // P
    TG = 4
    NGR = NT // TG
    TOP = 4.0 * QUANT
    STEP = QUANT / 4.0
    out = e.out
    with ExitStack() as st:
        def sbuf(name, shape, dt=F32):
            return st.enter_context(nc.sbuf_tensor(name, shape, dt))

        hs = W1[:, 0:NGR * FT * 512].rearrange("p (g f t) -> p g f t", g=NGR, f=FT)
        xT = [sbuf("xT6", [P, DK, TG * P]), W1[:, NGR * FT * 512:].rearrange("p (k t) -> p k t", k=DK)]
        b1, b1q = sbuf("b16", [P, FT]), sbuf("b1q6", [P, FT])
        b2 = sbuf("b26", [P, D])
        h, r, c, w, km, g0, g1, up = (sbuf(n, [P, 2, 512]) for n in
                                      ("h6", "r6", "c6", "w6", "km6", "g06", "g16", "up6"))
        dg = sbuf("dg6", [P, 2, 512])
        y = sbuf("y6", [P, 512])
        z = x[:, NT, :]
        ln = Norm(nc, e, "6", sbuf, ps[7], None)
        s_b, b_q, dve = sem("s_b6"), sem("b_q6"), sem("dve6")
        h_mm, h_sb, r_sb, c_sb, w_sb, km_sb, g_sb, up_sb, dg_sb, hs_sb = (
            sem(n) for n in ("h_mm6", "h_sb6", "r_sb6", "c_sb6", "w_sb6", "km_sb6", "g_sb6", "up_sb6", "dg_sb6", "hs_sb6"))
        z_mm, z_used, x_done, s_out = sem("z_mm6"), sem("z_used6"), sem("x_done6"), sem("s_out6")
        N = NGR * FT
        HB, ZB = 3, 3
        NORM_AT = [3 + 2 * t for t in range(TG)]

        e.open_sems()
        with nc.Block() as block:
            @block.sync
            def _(sp):
                sp.dma_start(b1[:, :], a["b16"]).then_inc(s_b, 16)
                sp.dma_start(b2[:, :], a["b26"]).then_inc(s_b, 16)
                for t in range(NT):
                    sp.wait_ge(x_done, BASE + t + 1)
                    sp.dma_start(out[:, t, :], x[:, t, :]).then_inc(s_out, 16)
                sp.wait_ge(s_out, BASE + 16 * NT)

            @block.gpsimd
            def _(pool):
                def slope(n):
                    pool.wait_ge(g_sb, BASE + 2 * n + 2)
                    if n >= 2:
                        pool.wait_ge(hs_sb, BASE + n - 1)
                    nc.gpsimd.tensor_tensor(dg[:, n % 2, :], g1[:, n % 2, :], g0[:, n % 2, :],
                                            ALU.subtract).then_inc(dg_sb, 1)

                for t in range(TG):
                    ln.pool(pool, t)
                for n in range(N):
                    slope(n)
                    if n in NORM_AT:
                        ln.pool(pool, TG + NORM_AT.index(n))

            @block.tensor
            def _(pe):
                def hidden(n):
                    g, f = divmod(n, FT)
                    if f == 0:
                        pe.wait_ge(ln.xT_ready, BASE + TG * (g + 1))
                    if n >= HB:
                        pe.wait_ge(h_sb, BASE + n - HB + 1)
                    for k in range(DK):
                        mm = nc.tensor.matmul(ps[n % HB], w16[:, k, f * P:(f + 1) * P], xT[g][:, k, :],
                                              start=(k == 0), stop=(k == DK - 1))
                    mm.then_inc(h_mm, 1)

                def output(t, f0, f1):
                    if f0 == 0 and t >= ZB:
                        pe.wait_ge(z_used, BASE + t - ZB + 1)
                    for f in range(f0, f1):
                        pe.wait_ge(hs_sb, BASE + FT * (t // TG) + f + 1)
                        mm = nc.tensor.matmul(ps[HB + t % ZB], hs[:, t // TG, f, (t % TG) * P:(t % TG + 1) * P],
                                              w26[:, f, :], start=(f == 0), stop=(f == FT - 1))
                    if f1 == FT:
                        mm.then_inc(z_mm, 1)

                for t in range(TG):
                    ln.tensor(pe, t)
                pe.wait_ge(e.s_w6, BASE + 32)
                for n in range(FT):
                    hidden(n)
                    if n - 2 in NORM_AT:
                        ln.tensor(pe, TG + NORM_AT.index(n - 2))
                per = FT // TG
                for f in range(FT):
                    hidden(FT + f)
                    output(f // per, f % per * per, (f % per + 1) * per)
                for t in range(TG, NT):
                    output(t, 0, FT)

            @block.scalar
            def _(act):
                def norm_out(t):
                    act.wait_ge(ln.turned, BASE + t + 1)
                    part = xT[t // TG][:, :, t % TG * P:(t % TG + 1) * P]
                    nc.scalar.activation(part, ps[7].rearrange("p (k t) -> p k t", k=DK),
                                         ACT.Copy).then_inc(ln.xT_ready, 1)

                def stage_a(n):
                    act.wait_ge(h_mm, BASE + n + 1)
                    if n >= 2:
                        act.wait_ge(r_sb, BASE + n - 1)
                    nc.scalar.activation(h[:, n % 2, :], ps[n % HB], ACT.Identity, scale=QUANT,
                                         bias=b1q[:, n % FT:n % FT + 1]).then_inc(h_sb, 1)

                def stage_b(n):
                    u = n % 2
                    act.wait_ge(w_sb, BASE + n + 1)
                    if n >= 2:
                        act.wait_ge(hs_sb, BASE + n - 1)
                        act.wait_ge(dg_sb, BASE + n - 1)
                    nc.scalar.activation(km[:, u, :], w[:, u, :], ACT.Identity,
                                         bias=cn[:, CN_ROUND:CN_ROUND + 1]).then_inc(km_sb, 1)
                    nc.scalar.activation(up[:, u, :], r[:, u, :], ACT.Relu,
                                         bias=cn[:, CN_TOP:CN_TOP + 1]).then_inc(up_sb, 1)
                    act.wait_ge(km_sb, BASE + n + 1)
                    nc.scalar.activation(g0[:, u, :], km[:, u, :], ACT.Gelu, scale=0.25,
                                         bias=cn[:, CN_K0:CN_K0 + 1]).then_inc(g_sb, 1)
                    nc.scalar.activation(g1[:, u, :], km[:, u, :], ACT.Gelu, scale=0.25,
                                         bias=cn[:, CN_K1:CN_K1 + 1]).then_inc(g_sb, 1)

                for t in range(TG):
                    norm_out(t)
                act.wait_ge(b_q, BASE + 2)
                stage_a(0)
                for n in range(N):
                    if n + 1 < N:
                        stage_a(n + 1)
                    stage_b(n)
                    if n - 2 in NORM_AT:
                        norm_out(TG + NORM_AT.index(n - 2))

            @block.vector
            def _(ve):
                ch = Chain(ve, dve)

                def round_(n):
                    u = n % 2
                    ve.wait_ge(h_sb, BASE + n + 1)
                    if n >= 2:
                        ve.wait_ge(up_sb, BASE + n - 1)
                    nc.vector.tensor_scalar(r[:, u, :], h[:, u, :], ROUND, ROUND, ALU.add,
                                            ALU.subtract).then_inc(r_sb, 1)
                    ve.wait_ge(r_sb, BASE + n + 1)
                    nc.vector.tensor_scalar(c[:, u, :], r[:, u, :], -TOP, TOP, ALU.max, ALU.min).then_inc(c_sb, 1)
                    ve.wait_ge(c_sb, BASE + n + 1)
                    if n >= 2:
                        ve.wait_ge(km_sb, BASE + n - 1)
                    nc.vector.tensor_scalar(w[:, u, :], c[:, u, :], -(STEP - 1) / 2, 1.0 / STEP, ALU.add,
                                            ALU.mult).then_inc(w_sb, 1)

                def interpolate(n):
                    g, f = divmod(n, FT)
                    u = n % 2
                    ve.wait_ge(km_sb, BASE + n + 1)
                    ch.link(nc.vector.scalar_tensor_tensor(c[:, u, :], km[:, u, :], ROUND, w[:, u, :],
                                                           ALU.subtract, ALU.subtract))
                    ve.wait_ge(dg_sb, BASE + n + 1)
                    ch.link(nc.vector.scalar_tensor_tensor(c[:, u, :], c[:, u, :], (STEP - 1) / 2 / STEP, dg[:, u, :],
                                                           ALU.subtract, ALU.mult))
                    ch.link(nc.vector.tensor_tensor(y[:, :], g0[:, u, :], c[:, u, :], ALU.subtract))
                    ch.link(nc.vector.tensor_scalar(y[:, :], y[:, :], QUANT, ROUND, ALU.mult, ALU.add))
                    ve.wait_ge(up_sb, BASE + n + 1)
                    nc.vector.scalar_tensor_tensor(hs[:, g, f, :], y[:, :], ROUND, up[:, u, :], ALU.subtract,
                                                   ALU.add).then_inc(hs_sb, 1)

                def finish(t):
                    if t:
                        ve.wait_ge(x_done, BASE + t)
                    ve.wait_ge(z_mm, BASE + t + 1)
                    nc.vector.tensor_tensor(z, ps[HB + t % ZB], b2[:, :], ALU.add).then_inc(z_used, 1)
                    ve.wait_ge(z_used, BASE + t + 1)
                    ch.link(nc.vector.tensor_scalar(z, z, ROUND, ROUND, ALU.add, ALU.subtract))
                    nc.vector.scalar_tensor_tensor(x[:, t, :], z, 1.0 / QUANT, x[:, t, :], ALU.mult,
                                                   ALU.add).then_inc(x_done, 1)

                ve.wait_ge(s_b, BASE + 32)
                nc.vector.tensor_scalar(b1q[:, :], b1[:, :], QUANT, None, ALU.mult).then_inc(b_q, 1)
                nc.vector.tensor_scalar(b2[:, :], b2[:, :], QUANT, None, ALU.mult).then_inc(b_q, 1)
                for t in range(TG):
                    ln.vector_stats(ch, t)
                    ln.vector_norm(ve, t)
                round_(0)
                for n in range(N):
                    if n + 1 < N:
                        round_(n + 1)
                    interpolate(n)
                    if n in NORM_AT:
                        ln.vector_stats(ch, TG + NORM_AT.index(n))
                        ln.vector_norm(ve, TG + NORM_AT.index(n))
                    per = FT // TG
                    if n >= FT + 1 and (n - FT) % per == 1 and (n - FT) // per >= 1:
                        finish((n - FT) // per - 1)
                for t in range(TG - 1, NT):
                    finish(t)


def perceiver_kernel(nc, a, out, stages=6):
    ctx = ExitStack()
    with ctx:
        def dram(name, shape, dt=F32):
            return nc.dram_tensor(name, shape, dt, kind="Internal").ap()

        xg_d = dram("routed_x", [ET * P, D])
        yg_d = dram("routed_y", [ET * P, D])
        v_d = dram("scan_v", [B * S, D])
        ba_d = dram("scan_ba", [2, B * HS, S])

        def sb(name, shape, dt=F32):
            return ctx.enter_context(nc.sbuf_tensor(name, shape, dt))

        x = sb("x", [P, NT + 1, D])
        cn = sb("cn", [P, CN_N])
        W0 = sb("W0", [P, 16384])
        W1 = sb("W1", [P, 2 * (DK * 2 * FE + FE // P * D)])
        PS = ctx.enter_context(nc.psum_tensor("PS", [P, 8, 512], F32))
        ps = [PS[:, i, :] for i in range(8)]
        ident = cn[:, CN_ID:CN_ID + P]
        ones = cn[:, CN_ONE:CN_ONE + P]

        wv0 = W0[:, 0:1024].rearrange("p (k n) -> p k n", k=DK)
        wt0 = W0[:, 1024:1792].rearrange("p (k n) -> p k n", k=CK)
        wqkv = W0[:, 1792:1792 + 6144].rearrange("p (k n) -> p k n", k=DK)
        wq4 = W0[:, 0:4096].rearrange("p (k n) -> p k n", k=DK)
        wk4 = W0[:, 4096:7168].rearrange("p (m n) -> p m n", m=H1 // 2)
        wv4 = W0[:, 7168:10240].rearrange("p (k n) -> p k n", k=CK)
        wo4 = W0[:, 10240:14336].rearrange("p (k n) -> p k n", k=HC // P)
        w5 = W1[:, 0:10240].rearrange("p (w k n) -> p w k n", w=5, k=DK)
        w16 = W0[:, 0:8192].rearrange("p (k n) -> p k n", k=DK)
        w26 = W0[:, 8192:16384].rearrange("p (k n) -> p k n", k=FF // P)

        fresh = []
        layer_sems = []

        def held(name):
            fresh.append(ctx.enter_context(nc.semaphore(name)))
            return fresh[-1]

        def sem(name, pool_dma=False):
            layer_sems.append(nc.alloc_semaphore(name=name))
            if not pool_dma:
                fresh.append(layer_sems[-1])
            return layer_sems[-1]

        def open_sems():
            with nc.Block() as block:
                for n, part in enumerate((block.gpsimd, block.vector, block.scalar, block.tensor, block.sync)):
                    @part
                    def _(eng, mine=fresh[n::5]):
                        for h in mine:
                            eng.sem_inc(h, BASE)
            fresh.clear()

        def reset_sems():
            with nc.Block() as block:
                @block.gpsimd
                def _(pool):
                    for h in layer_sems:
                        pool.sem_clear(h)
            for h in layer_sems:
                nc.release_semaphore(h)
            layer_sems.clear()

        s_cn, s_x = held("s_cn"), held("s_x")
        s_w12, s_w4, s_w5, s_w6 = held("s_w12"), held("s_w4"), held("s_w5"), held("s_w6")

        env = Env()
        env.x, env.cn, env.W0, env.W1, env.PS, env.ps, env.ident, env.ones = x, cn, W0, W1, PS, ps, ident, ones
        env.out, env.xg_d, env.yg_d, env.v_d, env.ba_d = out, xg_d, yg_d, v_d, ba_d
        env.sem, env.open_sems = sem, open_sems
        env.s_cn, env.s_x, env.s_xg0 = s_cn, s_x, held("s_xg0")
        env.s_w12, env.s_w4, env.s_w5, env.s_w6 = s_w12, s_w4, s_w5, s_w6
        env.wv0, env.wt0, env.wqkv, env.wq4, env.wk4, env.wv4, env.wo4 = wv0, wt0, wqkv, wq4, wk4, wv4, wo4
        env.w5, env.w16, env.w26 = w5, w16, w26
        cosine_layer(nc, a, env)
        layers = [self_attention_layer, expert_layer, cross_attention_layer, decayed_attention_layer,
                  feed_forward_layer]
        for layer in layers[:stages - 1]:
            layer(nc, a, env)
            if layer is expert_layer:
                reset_sems()
        if stages < 6:
            s_o = sem("s_o")
            open_sems()
            with nc.Block() as block:
                @block.sync
                def _(sp):
                    sp.dma_start(out, x[:, 0:NT, :]).then_inc(s_o, 16)
                    sp.wait_ge(s_o, BASE + 16)


def arrays_of(i):
    def tiles(w):
        w = np.asarray(w)
        return np.ascontiguousarray(w.reshape(-1, P, w.shape[1]).transpose(1, 0, 2))

    g = {k: np.asarray(v) for k, v in i.items()}
    c = g["ctx_768"]
    w = g["L0_attn_W_qkv"].reshape(H0, 3, DH0, D).transpose(1, 0, 2, 3).reshape(3 * D, D)
    return {
        "consts": constant_table(),
        "x": tiles(g["x"].reshape(B * S, D)),
        "ctxT": np.ascontiguousarray(c.reshape(B, J, CK, P).transpose(0, 3, 2, 1)),
        "ctxN": np.ascontiguousarray(c.reshape(B, J // P, P, C).transpose(0, 2, 1, 3)),
        "wv0": tiles(g["L0_xattn_Wv"].T),
        "wt0": tiles(g["L0_xattn_Wt"].T),
        "bv0": g["L0_xattn_bv"].reshape(1, HX),
        "bt0": np.ascontiguousarray(g["L0_xattn_bt"].reshape(2, P).T),
        "wqkv": tiles(w.T),
        "gate": tiles(g["L0_ffn_w_gate"]),
        "fc": np.ascontiguousarray(g["L0_ffn_c_fc"].reshape(NE, DK, P, 2 * FE).transpose(0, 2, 1, 3)),
        "proj": np.ascontiguousarray(g["L0_ffn_c_proj"].reshape(NE, FE // P, P, D).transpose(0, 2, 1, 3)),
        "wq4": tiles(g["L1_xattn_Wq"]),
        "wk4": tiles(g["L1_xattn_Wk"].T),
        "wv4": tiles(g["L1_xattn_Wv"]),
        "wo4": tiles(g["L1_xattn_Wo"]),
        "bo4": g["L1_xattn_bo"].reshape(1, D),
        "w5": np.ascontiguousarray(np.stack([tiles(g["L1_attn_" + n].T) for n in
                                             ("W_q", "W_k", "W_v", "W_alpha_w", "W_o")], 1)),
        "ba5": g["L1_attn_W_alpha_b"].reshape(1, HS * DHS),
        "w16": tiles(g["L1_ffn_w1"]),
        "w26": tiles(g["L1_ffn_w2"]),
        "b16": np.ascontiguousarray(g["L1_ffn_b1"].reshape(FF // P, P).T),
        "b26": np.ascontiguousarray(np.broadcast_to(g["L1_ffn_b2"].reshape(1, D), (P, D))),
    }


def kernel(**inputs):
    import concourse.bacc as _bacc
    from concourse.bass_utils import run_bass_kernel_spmd as _run

    nc = _bacc.Bacc("TRN2", target_bir_lowering=False, num_devices=1)
    arrays, aps = {}, {}
    for name, w in arrays_of(inputs).items():
        arrays[f"in_{name}"] = np.ascontiguousarray(w)
        aps[name] = nc.dram_tensor(f"in_{name}", w.shape, mybir.dt.from_np(w.dtype), kind="ExternalInput").ap()
    out = nc.dram_tensor("out", (P, NT, D), F32, kind="ExternalOutput").ap()
    perceiver_kernel(nc, aps, out)
    r = _run(nc, [arrays], core_ids=[0])
    return r.results[0]["out"].transpose(1, 0, 2).reshape(B, S, D)
```

```python
from contextlib import ExitStack

import numpy as np

import concourse.bass as bass
from concourse import mybir

F32 = mybir.dt.float32
F32R = mybir.dt.float32r
U32 = mybir.dt.uint32
I32 = mybir.dt.int32
ALU = mybir.AluOpType
ACT = mybir.ActivationFunctionType
AX = mybir.AxisListType

P = 128
B, S, D = 16, 64, 512
J, C = 512, 384
NT = B * S // P
DK = D // P
CK = C // P
HX = 256
H0, DH0 = 16, 32
NE, FE = 8, 768
ET = 2 * B * S // P + NE - 1
H1, DH1 = 16, 64
HC = H1 * DH1
HS, DHS = 8, 64
FF = 2048
LN_EPS = 1e-5
EPS = 1e-8
EPS_BITS = int(np.float32(EPS).view(np.uint32))
SIGN_BIT = 0x80000000
ROUND = 12582912.0
QUANT = 256.0

CN_ID = 0
CN_TRI = CN_ID + P
CN_ONE = CN_TRI + P
CN_SEL = CN_ONE + P
CN_IOTA = CN_SEL + B
CN_TILE = CN_IOTA + NT * NE
CN_MISC = CN_TILE + ET * NE
CN_HALF, CN_MHALF, CN_ROUND, CN_TOP, CN_K0, CN_K1 = range(CN_MISC, CN_MISC + 6)
CN_N = CN_MISC + 6


def constant_table():
    t = np.zeros((P, CN_N), np.float32)
    p = np.arange(P)
    t[:, CN_ID:CN_ID + P] = np.eye(P)
    t[:, CN_TRI:CN_TRI + P] = p[:, None] < p[None, :]
    t[:, CN_ONE:CN_ONE + P] = 1.0
    t[:, CN_SEL:CN_SEL + B] = p[:, None] // HS == np.arange(B)[None, :]
    t[:, CN_IOTA:CN_IOTA + NT * NE] = np.tile(np.arange(NE) - NE, NT)
    t[:, CN_TILE:CN_TILE + ET * NE] = np.repeat(np.arange(ET), NE)
    t[:, CN_HALF] = 0.5
    t[:, CN_MHALF] = -0.5
    t[:, CN_ROUND] = ROUND
    t[:, CN_TOP] = -4.0 * QUANT
    t[:, CN_K0] = -0.25 * ROUND
    t[:, CN_K1] = 0.25 - 0.25 * ROUND
    return t


BASE = 1


class Env:
    pass


class Chain:

    def __init__(self, eng, sem):
        self.eng, self.sem, self.base, self.n = eng, sem, 0, 0

    def turn(self, i, per):
        self.start, self.per = self.n, per
        self.again(i)

    def again(self, i):
        self.base, self.n = i * self.per + self.start, 0

    def link(self, ins):
        ins.then_inc(self.sem, 1)
        self.n += 1
        self.eng.wait_ge(self.sem, BASE + self.base + self.n)


class Norm:

    def __init__(self, nc, e, tag, sbuf, bank, xT):
        self.nc, self.x, self.cn, self.ident = nc, e.x, e.cn, e.ident
        sem = e.sem
        self.st = sbuf(f"st{tag}", [P, 6])
        self.mv = sbuf(f"mv{tag}", [P, 2])
        self.ve = sbuf(f"ve{tag}", [P, 1])
        self.rs = sbuf(f"rs{tag}", [P, 1])
        self.xn = sbuf(f"xn{tag}", [P, D])
        self.bank, self.xT = bank, xT
        self.var, self.rstd = sem(f"var{tag}"), sem(f"rstd{tag}")
        self.norm, self.turned = sem(f"norm{tag}"), sem(f"turned{tag}")
        self.xT_ready, self.seen = sem(f"xT_ready{tag}"), sem(f"seen{tag}")

    def vector_stats(self, ch, n):
        ch.link(self.nc.vector.bn_stats(self.st[:, :], self.x[:, n, :]))
        self.nc.vector.sem_inc(self.seen)
        ch.link(self.nc.vector.bn_aggr(self.mv[:, :], self.st[:, :]))
        self.nc.vector.tensor_scalar(self.ve[:, :], self.mv[:, 1:2], LN_EPS, None,
                                ALU.add).then_inc(self.var, 1)

    def pool(self, eng, n):
        eng.wait_ge(self.var, BASE + n + 1)
        self.nc.gpsimd.tensor_tensor(self.rs[:, :], self.ve[:, :], self.cn[:, CN_MHALF:CN_MHALF + 1],
                                ALU.pow).then_inc(self.rstd, 1)

    def vector_norm(self, eng, n):
        eng.wait_ge(self.rstd, BASE + n + 1)
        eng.wait_ge(self.turned, BASE + n)
        self.nc.vector.tensor_scalar(self.xn[:, :], self.x[:, n, :], self.mv[:, 0:1], self.rs[:, 0:1],
                                ALU.subtract, ALU.mult).then_inc(self.norm, 1)

    def tensor(self, eng, n):
        eng.wait_ge(self.norm, BASE + n + 1)
        eng.wait_ge(self.xT_ready, BASE + n)
        for k in range(DK):
            last = self.nc.tensor.transpose(self.bank[:, k * P:(k + 1) * P],
                                       self.xn[:, k * P:(k + 1) * P], self.ident)
        last.then_inc(self.turned, 1)

    def scalar(self, eng, n, used, count=None):
        eng.wait_ge(self.turned, BASE + n + 1)
        eng.wait_ge(used, BASE + (n if count is None else count))
        self.nc.scalar.activation(self.xT[:, :, :].rearrange("p k t -> p (k t)"), self.bank[:, :],
                             ACT.Copy).then_inc(self.xT_ready, 1)


def cosine_layer(nc, a, e):
    x, cn, ps, ones, ident, sem = e.x, e.cn, e.ps, e.ones, e.ident, e.sem
    s_cn, s_x, s_w12, s_xg0 = e.s_cn, e.s_x, e.s_w12, e.s_xg0
    wv0, wt0, wqkv, xg_d = e.wv0, e.wt0, e.wqkv, e.xg_d
    with ExitStack() as st:
        def sbuf(name, shape, dt=F32):
            return st.enter_context(nc.sbuf_tensor(name, shape, dt))

        cT = sbuf("cT1", [P, 2, CK, J])
        tT = sbuf("tT1", [P, 2, 2, J])
        sq = sbuf("sq1", [P, 2, 2, J])
        v = sbuf("v1", [P, HX])
        vsq = sbuf("vsq1", [P, HX])
        vT = sbuf("vT1", [P, 2, P])
        vn2 = sbuf("vn2_1", [P, 1])
        vn = sbuf("vn1", [P, 1])
        tn = sbuf("tn1", [P, J])
        den = sbuf("den1", [P, J])
        rden = sbuf("rden1", [P, J])
        cosv = sbuf("cos1", [P, J])
        bv = sbuf("bv1", [1, HX])
        bt = sbuf("bt1", [P, 2])
        xT = sbuf("xT1", [P, DK, P])
        zero = sbuf("zero1", [P, D])
        ln = Norm(nc, e, "1", sbuf, ps[7], xT)
        s_ct = [sem("s_ct1_0"), sem("s_ct1_1")]
        s_b = sem("s_b1")
        v_mm, v_sb, v_sq, v_n = sem("v_mm1"), sem("v_sb1"), sem("v_sq1"), sem("v_n1")
        vt_mm, vt_sb = sem("vt_mm1"), sem("vt_sb1")
        t_mm, t_sb, t_sq = sem("t_mm1"), sem("t_sb1"), sem("t_sq1")
        d_mm, n_mm, tn_sb = sem("d_mm1"), sem("n_mm1"), sem("tn_sb1")
        dots_read = sem("dots_read1")
        s_zero, s_zx = sem("s_zero1"), sem("s_zx1")
        dve = sem("dve1")
        psV, psVT, psT, psD, psN = ps[0], ps[1], (ps[2], ps[3]), ps[4], ps[5]

        e.open_sems()
        with nc.Block() as block:
            @block.sync
            def _(sp):
                sp.dma_start(cn[:, :], a["consts"]).then_inc(s_cn, 16)
                sp.dma_start(x[:, 0:NT, :], a["x"]).then_inc(s_x, 16)
                sp.dma_start(wv0, a["wv0"]).then_inc(s_w12, 16)
                sp.dma_start(wt0, a["wt0"]).then_inc(s_w12, 16)
                sp.dma_start(bv[:, :], a["bv0"]).then_inc(s_b, 16)
                sp.dma_start(bt[:, :], a["bt0"]).then_inc(s_b, 16)
                for u in range(2):
                    sp.dma_start(cT[:, u], a["ctxT"][u]).then_inc(s_ct[u], 16)
                sp.dma_start(wqkv, a["wqkv"]).then_inc(s_w12, 16)
                sp.wait_ge(s_zero, BASE + 1)
                for e in range(ET):
                    sp.dma_start(xg_d[e * P:(e + 1) * P, :], zero[:, :]).then_inc(s_xg0, 16)
                with sp.Fori(0, NT - 1) as i:
                    for u in range(2):
                        sp.wait_ge(t_mm, BASE + 4 * i + 2 * u + 2)
                        sp.dma_start(cT[:, u], a["ctxT"][2 * i + 2 + u]).then_inc(s_ct[u], 16)
                sp.wait_ge(s_xg0, BASE + 16 * ET)

            @block.gpsimd
            def _(pool):
                nc.gpsimd.memset(zero[:, :], 0.0).then_inc(s_zero, 1)
                nc.gpsimd.memset(x[:, NT, :], 0.0).then_inc(s_zx, 1)
                pool.wait_ge(s_cn, BASE + 16)
                ln.pool(pool, 0)
                with pool.Fori(0, NT) as i:
                    ln.pool(pool, i + 1)
                    pool.wait_ge(v_sq, BASE + i + 1)
                    nc.gpsimd.tensor_tensor(vn[:, :], vn2[:, :], cn[:, CN_HALF:CN_HALF + 1],
                                            ALU.pow).then_inc(v_n, 1)

            @block.vector
            def _(ve):
                ch = Chain(ve, dve)
                ve.wait_ge(s_x, BASE + 16)
                ln.vector_stats(ch, 0)
                ln.vector_norm(ve, 0)
                ve.wait_ge(s_zx, BASE + 1)
                with ve.Fori(0, NT) as i:
                    ch.turn(i, 6)
                    ln.vector_stats(ch, i + 1)
                    ve.wait_ge(v_mm, BASE + i + 1)
                    ve.wait_ge(vt_mm, BASE + i)
                    ve.wait_ge(v_sq, BASE + i)
                    nc.vector.tensor_copy(v[:, :], psV[:, 0:HX]).then_inc(v_sb, 1)
                    ln.vector_norm(ve, i + 1)
                    ve.wait_ge(vt_mm, BASE + i + 1)
                    ve.wait_ge(d_mm, BASE + i)
                    nc.vector.tensor_copy(vT[:, :, :].rearrange("p m t -> p (m t)"),
                                          psVT[:, 0:2 * P]).then_inc(vt_sb, 1)
                    ve.wait_ge(v_n, BASE + i + 1)
                    ve.wait_ge(tn_sb, BASE + i + 1)
                    ch.link(nc.vector.tensor_scalar(den[:, :], tn[:, :], vn[:, 0:1], EPS,
                                                    ALU.mult, ALU.max))
                    ch.link(nc.vector.reciprocal(rden[:, :], den[:, :]))
                    ve.wait_ge(d_mm, BASE + i + 1)
                    ch.link(nc.vector.tensor_tensor(cosv[:, :], psD[:, :], rden[:, :], ALU.mult))
                    ve.sem_inc(dots_read, 1)
                    ch.link(nc.vector.tensor_tensor(x[:, i, :], x[:, i, :], cosv[:, :], ALU.add))
                    assert ch.n == 6

            @block.tensor
            def _(pe):
                pe.wait_ge(s_cn, BASE + 16)
                ln.tensor(pe, 0)
                pe.wait_ge(s_w12, BASE + 32)
                pe.wait_ge(s_b, BASE + 32)

                def project(i, u):
                    pe.wait_ge(s_ct[u], BASE + 16 * i + 16)
                    for m in range(2):
                        if u:
                            pe.wait_ge(t_sb, BASE + 4 * i + 1 + m)
                            pe.wait_ge(t_sq, BASE + 4 * i + 1 + m)
                        else:
                            pe.wait_ge(t_sb, BASE + 4 * i)
                            pe.wait_ge(t_sq, BASE + 4 * i)
                        for k in range(CK):
                            mm = nc.tensor.matmul(psT[m][:, :], wt0[:, k, m * P:(m + 1) * P],
                                                  cT[:, u, k, :], start=(k == 0), stop=(k == CK - 1))
                        mm.then_inc(t_mm, 1)

                with pe.Fori(0, NT) as i:
                    pe.wait_ge(ln.xT_ready, BASE + i + 1)
                    pe.wait_ge(v_sb, BASE + i)
                    for k in range(DK):
                        nc.tensor.matmul(psV[:, 0:HX], xT[:, k, :], wv0[:, k, :],
                                         start=(k == 0), stop=False)
                    nc.tensor.matmul(psV[:, 0:HX], ones[0:1, :], bv[0:1, :],
                                     start=False, stop=True).then_inc(v_mm, 1)
                    project(i, 0)
                    pe.wait_ge(v_sb, BASE + i + 1)
                    pe.wait_ge(vt_sb, BASE + i)
                    for m in range(2):
                        tr = nc.tensor.transpose(psVT[:, m * P:(m + 1) * P],
                                                 v[:, m * P:(m + 1) * P], ident)
                    tr.then_inc(vt_mm, 1)
                    project(i, 1)
                    ln.tensor(pe, i + 1)
                    pe.wait_ge(vt_sb, BASE + i + 1)
                    pe.wait_ge(dots_read, BASE + i)
                    pe.wait_ge(tn_sb, BASE + i)
                    for u in range(2):
                        rows = slice(u * S, (u + 1) * S)
                        pe.wait_ge(t_sb, BASE + 4 * i + 2 * u + 2)
                        pe.wait_ge(t_sq, BASE + 4 * i + 2 * u + 2)
                        for m in range(2):
                            mn = nc.tensor.matmul(psN[rows, :], ones[:, 0:S], sq[:, u, m, :],
                                                  start=(m == 0), stop=(m == 1))
                        if u:
                            mn.then_inc(n_mm, 1)
                        for m in range(2):
                            mm = nc.tensor.matmul(psD[rows, :], vT[:, m, rows], tT[:, u, m, :],
                                                  start=(m == 0), stop=(m == 1))
                    mm.then_inc(d_mm, 1)

            @block.scalar
            def _(act):
                act.wait_ge(s_cn, BASE + 16)
                act.wait_ge(s_b, BASE + 32)
                ln.scalar(act, 0, v_mm)
                with act.Fori(0, NT) as i:
                    act.wait_ge(v_sb, BASE + i + 1)
                    act.wait_ge(v_n, BASE + i)
                    nc.scalar.activation(vsq[:, :], v[:, :], ACT.Square,
                                         accum_out=vn2[:, :]).then_inc(v_sq, 1)

                    def project_out(u):
                        for m in range(2):
                            act.wait_ge(t_mm, BASE + 4 * i + 2 * u + m + 1)
                            act.wait_ge(d_mm, BASE + i)
                            nc.scalar.activation(tT[:, u, m, :], psT[m][:, :], ACT.Identity,
                                                 bias=bt[:, m:m + 1]).then_inc(t_sb, 1)
                            nc.scalar.activation(sq[:, u, m, :], psT[m][:, :], ACT.Square,
                                                 bias=bt[:, m:m + 1]).then_inc(t_sq, 1)

                    project_out(0)
                    project_out(1)
                    ln.scalar(act, i + 1, v_mm)
                    act.wait_ge(n_mm, BASE + i + 1)
                    act.wait_ge(dots_read, BASE + i)
                    nc.scalar.activation(tn[:, :], psN[:, :], ACT.Sqrt).then_inc(tn_sb, 1)


def self_attention_layer(nc, a, e):
    x, cn, ps, PS, ident, sem, wqkv = e.x, e.cn, e.ps, e.PS, e.ident, e.sem, e.wqkv
    SCALE = float(np.float32(1.0) / np.sqrt(np.float32(DH0)))
    HH = P // DH0
    with ExitStack() as st:
        def sbuf(name, shape, dt=F32):
            return st.enter_context(nc.sbuf_tensor(name, shape, dt))

        xT = sbuf("xT2", [P, DK, P])
        q, k, v = sbuf("q2", [P, D]), sbuf("k2", [P, D]), sbuf("v2", [P, D])
        qT, kT = sbuf("qT2", [P, DK, P]), sbuf("kT2", [P, DK, P])
        mx = sbuf("mx2", [P, H0])
        sc = sbuf("sc2", [P, H0, S])
        pf = sbuf("pf2", [P, H0, P])
        pT = sbuf("pT2", [P, H0, P])
        sums, rs = sbuf("sums2", [P, H0]), sbuf("rsum2", [P, H0])
        o = sbuf("o2", [P, D])
        ln = Norm(nc, e, "2", sbuf, ps[7], xT)
        q_mm, k_mm, v_mm = sem("q_mm2"), sem("k_mm2"), sem("v_mm2")
        q_sb, k_sb, v_sb = sem("q_sb2"), sem("k_sb2"), sem("v_sb2")
        qT_mm, kT_mm, qT_sb, kT_sb = sem("qT_mm2"), sem("kT_mm2"), sem("qT_sb2"), sem("kT_sb2")
        s_mm, sub_done, e_sb, summed = sem("s_mm2"), sem("sub_done2"), sem("e_sb2"), sem("summed2")
        pt_mm, pt_act, pt_dve = sem("pt_mm2"), sem("pt_act2"), sem("pt_dve2")
        o_mm, o_read, zeroed, dve = sem("o_mm2"), sem("o_read2"), sem("zeroed2"), sem("dve2")
        S_BANKS = PS[:, 3:3 + HH, 0:DK * S]

        e.open_sems()
        with nc.Block() as block:
            @block.gpsimd
            def _(pool):
                nc.gpsimd.memset(pf[:, :, :], 0.0).then_inc(zeroed, 1)
                ln.pool(pool, 0)
                with pool.Fori(0, NT) as i:
                    ln.pool(pool, i + 1)

            @block.tensor
            def _(pe):
                def project(n):
                    pe.wait_ge(ln.xT_ready, BASE + n + 1)
                    for w, done, out_read in ((0, q_mm, qT_sb), (1, k_mm, kT_sb), (2, v_mm, v_sb)):
                        pe.wait_ge(out_read, BASE + n)
                        for kk in range(DK):
                            mm = nc.tensor.matmul(ps[w], xT[:, kk, :], wqkv[:, kk, w * D:(w + 1) * D],
                                                  start=(kk == 0), stop=(kk == DK - 1))
                        mm.then_inc(done, 1)

                pe.wait_ge(e.s_w12, BASE + 48)
                ln.tensor(pe, 0)
                project(0)
                with pe.Fori(0, NT) as i:
                    for src, bank, ready, done in ((q, 0, q_sb, qT_mm), (k, 1, k_sb, kT_mm)):
                        pe.wait_ge(ready, BASE + i + 1)
                        for m in range(DK):
                            tr = nc.tensor.transpose(ps[bank][:, m * P:(m + 1) * P],
                                                     src[:, m * P:(m + 1) * P], ident)
                        tr.then_inc(done, 1)
                    pe.wait_ge(qT_sb, BASE + i + 1)
                    pe.wait_ge(kT_sb, BASE + i + 1)
                    pe.wait_ge(pt_act, BASE + 2 * i)
                    pe.wait_ge(pt_dve, BASE + 2 * i)
                    for m in range(DK):
                        for hh in range(HH):
                            part = slice(hh * DH0, (hh + 1) * DH0)
                            for u in range(2):
                                tok = slice(u * S, (u + 1) * S)
                                mm = nc.tensor.matmul(PS[tok, 3 + hh, m * S:(m + 1) * S],
                                                      qT[part, m, tok], kT[part, m, tok],
                                                      start=True, stop=True)
                    mm.then_inc(s_mm, 1)
                    pe.wait_ge(o_read, BASE + i)
                    ln.tensor(pe, i + 1)
                    project(i + 1)
                    pe.wait_ge(e_sb, BASE + 2 * i + 2)
                    for g in range(HH):
                        for m in range(DK):
                            tr = nc.tensor.transpose(ps[3 + g][:, m * P:(m + 1) * P],
                                                     pf[:, g * DK + m, :], ident)
                        tr.then_inc(pt_mm, 1)
                    pe.wait_ge(pt_act, BASE + 2 * i + 2)
                    pe.wait_ge(pt_dve, BASE + 2 * i + 2)
                    pe.wait_ge(v_sb, BASE + i + 1)
                    for m in range(DK):
                        for hh in range(HH):
                            h = m * HH + hh
                            mm = nc.tensor.matmul(ps[7][:, h * DH0:(h + 1) * DH0], pT[:, hh * DK + m, :],
                                                  v[:, h * DH0:(h + 1) * DH0], start=True, stop=True)
                    mm.then_inc(o_mm, 1)

            @block.scalar
            def _(act):
                def take(n):
                    for dst, bank, done, turned, ready in ((q, 0, q_mm, qT_mm, q_sb),
                                                           (k, 1, k_mm, kT_mm, k_sb)):
                        act.wait_ge(done, BASE + n + 1)
                        act.wait_ge(turned, BASE + n)
                        nc.scalar.activation(dst[:, :], ps[bank], ACT.Copy).then_inc(ready, 1)

                ln.scalar(act, 0, v_mm)
                take(0)
                act.wait_ge(zeroed, BASE + 1)
                with act.Fori(0, NT) as i:
                    act.wait_ge(qT_mm, BASE + i + 1)
                    act.wait_ge(s_mm, BASE + i)
                    nc.scalar.activation(qT[:, :, :].rearrange("p m t -> p (m t)"), ps[0],
                                         ACT.Copy).then_inc(qT_sb, 1)
                    ln.scalar(act, i + 1, v_mm)
                    act.wait_ge(sub_done, BASE + i + 1)
                    act.wait_ge(pt_mm, BASE + 4 * i)
                    act.wait_ge(summed, BASE + i)
                    for u in range(2):
                        tok = slice(u * S, (u + 1) * S)
                        nc.scalar.activation(pf[tok, :, tok], sc[tok, :, :], ACT.Exp,
                                             scale=SCALE).then_inc(e_sb, 1)
                    take(i + 1)
                    for g in range(2):
                        act.wait_ge(pt_mm, BASE + 4 * i + g + 1)
                        act.wait_ge(o_mm, BASE + i)
                        nc.scalar.activation(pT[:, g * DK:(g + 1) * DK, :].rearrange("p m t -> p (m t)"),
                                             ps[3 + g], ACT.Copy).then_inc(pt_act, 1)

            @block.vector
            def _(ve):
                ch = Chain(ve, dve)
                ln.vector_stats(ch, 0)
                ln.vector_norm(ve, 0)

                def take_v(n):
                    ve.wait_ge(v_mm, BASE + n + 1)
                    ve.wait_ge(o_mm, BASE + n)
                    nc.vector.tensor_copy(v[:, :], ps[2]).then_inc(v_sb, 1)

                take_v(0)
                with ve.Fori(0, NT) as i:
                    ch.turn(i, 7)
                    ln.vector_stats(ch, i + 1)
                    ve.wait_ge(kT_mm, BASE + i + 1)
                    ve.wait_ge(s_mm, BASE + i)
                    nc.vector.tensor_copy(kT[:, :, :].rearrange("p m t -> p (m t)"),
                                          ps[1]).then_inc(kT_sb, 1)
                    ln.vector_norm(ve, i + 1)
                    ve.wait_ge(s_mm, BASE + i + 1)
                    s4 = S_BANKS.rearrange("p g (m s) -> p g m s", m=DK)
                    ch.link(nc.vector.tensor_reduce(mx[:, :].rearrange("p (g m) -> p g m", g=HH), s4,
                                                    AX.X, ALU.max))
                    ve.wait_ge(e_sb, BASE + 2 * i)
                    for g in range(HH):
                        part = sc[:, g * DK:(g + 1) * DK, :]
                        ins = nc.vector.tensor_tensor(part, s4[:, g],
                                                      mx[:, g * DK:(g + 1) * DK].unsqueeze(2).to_broadcast([P, DK, S]),
                                                      ALU.subtract)
                    ins.then_inc(sub_done, 1)
                    ve.wait_ge(e_sb, BASE + 2 * i + 2)
                    for u in range(2):
                        tok = slice(u * S, (u + 1) * S)
                        ins = nc.vector.tensor_reduce(sums[tok, :], pf[tok, :, tok], AX.X, ALU.add)
                        if u == 0:
                            ins.then_inc(dve, 1)
                            ch.n += 1
                    ch.link(ins)
                    ve.sem_inc(summed, 1)
                    ch.link(nc.vector.reciprocal(rs[:, :], sums[:, :]))
                    for g in range(2, HH):
                        ve.wait_ge(pt_mm, BASE + 4 * i + g + 1)
                        ve.wait_ge(o_mm, BASE + i)
                        nc.vector.tensor_copy(pT[:, g * DK:(g + 1) * DK, :].rearrange("p m t -> p (m t)"),
                                              ps[3 + g]).then_inc(pt_dve, 1)
                    ve.wait_ge(o_mm, BASE + i + 1)
                    r = rs[:, :].rearrange("p (hh m) -> p m hh", hh=HH).unsqueeze(3)
                    ch.link(nc.vector.tensor_tensor(
                        o[:, :].rearrange("p (m hh d) -> p m hh d", m=DK, hh=HH),
                        ps[7].rearrange("p (m hh d) -> p m hh d", m=DK, hh=HH),
                        r.to_broadcast([P, DK, HH, DH0]), ALU.mult))
                    ve.sem_inc(o_read, 1)
                    nc.vector.tensor_tensor(x[:, i, :], x[:, i, :], o[:, :], ALU.add)
                    take_v(i + 1)
                    assert ch.n == 7, ch.n


def expert_layer(nc, a, e):
    x, cn, ps, ones, ident, sem, W1 = e.x, e.cn, e.ps, e.ones, e.ident, e.sem, e.W1
    xg_d, yg_d = e.xg_d, e.yg_d
    tri = cn[:, CN_TRI:CN_TRI + P]
    iota = cn[:, CN_IOTA:CN_IOTA + NT * NE].rearrange("p (t e) -> p t e", t=NT)
    FK = FE // P
    HFE = FE // 2
    NFC = DK * 2 * FE
    with ExitStack() as st:
        def sbuf(name, shape, dt=F32):
            return st.enter_context(nc.sbuf_tensor(name, shape, dt))

        xn = sbuf("xnall3", [P, NT, D])
        slot = sbuf("slot3", [P, NT, 2], U32)
        top = sbuf("top3", [P, NT, 2])
        owner = sbuf("owner3", [1, ET], I32)
        s_slot, s_owner = sem("s_slot3"), sem("s_owner3")
        s_scat = sem("s_scat3", pool_dma=True)

        with ExitStack() as rt:
            def rbuf(name, shape, dt=F32):
                return rt.enter_context(nc.sbuf_tensor(name, shape, dt))

            xT = rbuf("xT3", [P, DK, P])
            gate = rbuf("gate3", [P, DK, NE])
            ln = Norm(nc, e, "3", rbuf, ps[7], xT)
            TE = [P, NT, NE]
            logit, prob, prob2 = rbuf("logit3", TE), rbuf("prob3", TE), rbuf("prob23", TE)
            eq, cand = rbuf("eq3", TE), rbuf("cand3", TE)
            oh = [rbuf("oh13", TE), rbuf("oh23", TE)]
            both, before, place, pick = rbuf("both3", TE), rbuf("before3", TE), rbuf("place3", TE), rbuf("pick3", TE)
            r8, first = rbuf("r83", [P, NT]), rbuf("first3", [P, NT])
            total, tiles, ends, starts = (rbuf(n, [P, NE]) for n in ("total3", "tiles3", "ends3", "starts3"))
            slotf = rbuf("slotf3", [P, NT])
            under = rbuf("under3", [1, ET, NE])
            ownf = rbuf("ownf3", [1, ET])
            s_gate, g_mm, kept = sem("s_gate3"), sem("g_mm3"), sem("kept3")
            s_max, s_exp, s_cnt, s_pos = sem("s_max3"), sem("s_exp3"), sem("s_cnt3"), sem("s_pos3")
            dve = sem("dve3")

            def wide(ap, shape=TE):
                return ap.unsqueeze(2).to_broadcast(shape)

            e.open_sems()
            with nc.Block() as block:
                @block.sync
                def _(sp):
                    sp.dma_start(gate[:, :, :], a["gate"]).then_inc(s_gate, 16)
                    for dst, name in ((e.wq4, "wq4"), (e.wk4, "wk4"), (e.wv4, "wv4"), (e.wo4, "wo4")):
                        sp.dma_start(dst, a[name]).then_inc(e.s_w4, 16)

                @block.gpsimd
                def _(pool):
                    ln.pool(pool, 0)
                    with pool.Fori(0, NT) as i:
                        pool.wait_ge(ln.norm, BASE + i + 1)
                        nc.gpsimd.tensor_copy(xn[:, i, :], ln.xn[:, :]).then_inc(kept, 1)
                        ln.pool(pool, i + 1)
                    pool.wait_ge(kept, BASE + NT)
                    pool.wait_ge(e.s_xg0, BASE + 16 * ET)
                    pool.wait_ge(s_slot, BASE + 2)
                    for t in range(NT):
                        for c in range(2):
                            nc.gpsimd.indirect_dma_start(
                                out=xg_d, out_offset=bass.IndirectOffsetOnAxis(slot[:, t, c:c + 1], axis=0),
                                in_=xn[:, t, :], in_offset=None).then_inc(s_scat, 16)
                    pool.wait_ge(s_scat, 16 * 2 * NT)

                @block.tensor
                def _(pe):
                    ln.tensor(pe, 0)
                    pe.wait_ge(s_gate, BASE + 16)
                    with pe.Fori(0, NT) as i:
                        pe.wait_ge(ln.xT_ready, BASE + i + 1)
                        for k in range(DK):
                            mm = nc.tensor.matmul(ps[0][:, bass.ds(i * NE, NE)], xT[:, k, :], gate[:, k, :],
                                                  start=(k == 0), stop=(k == DK - 1))
                        mm.then_inc(g_mm, 1)
                        ln.tensor(pe, i + 1)
                    pe.wait_ge(s_cnt, BASE + 1)
                    nc.tensor.matmul(ps[1][:, 0:NE], ones, total[:, :], start=True, stop=True)
                    nc.tensor.matmul(ps[2][:, 0:NT * NE], tri, both[:, :, :].rearrange("p t e -> p (t e)"),
                                     start=True, stop=False)
                    nc.tensor.matmul(ps[2][:, 0:NT * NE], ones, before[:, :, :].rearrange("p t e -> p (t e)"),
                                     start=False, stop=True).then_inc(s_pos, 1)

                @block.scalar
                def _(act):
                    ln.scalar(act, 0, g_mm)
                    with act.Fori(0, NT) as i:
                        ln.scalar(act, i + 1, g_mm)
                    act.wait_ge(s_max, BASE + 1)
                    nc.scalar.activation(prob[:, :, :], logit[:, :, :], ACT.Exp).then_inc(s_exp, 1)

                @block.vector
                def _(ve):
                    ch = Chain(ve, dve)
                    ln.vector_stats(ch, 0)
                    ln.vector_norm(ve, 0)
                    with ve.Fori(0, NT) as i:
                        ch.turn(i, 2)
                        ln.vector_stats(ch, i + 1)
                        ve.wait_ge(kept, BASE + i + 1)
                        ln.vector_norm(ve, i + 1)
                    ch.base, ch.n = 2 + 2 * NT, 0
                    ve.wait_ge(g_mm, BASE + NT)
                    lg = ps[0][:, 0:NT * NE].rearrange("p (t e) -> p t e", t=NT)
                    ch.link(nc.vector.tensor_reduce(r8[:, :], lg, AX.X, ALU.max))
                    nc.vector.tensor_tensor(logit[:, :, :], lg, wide(r8[:, :]), ALU.subtract).then_inc(s_max, 1)
                    ve.wait_ge(s_exp, BASE + 1)
                    ch.link(nc.vector.tensor_reduce(r8[:, :], prob[:, :, :], AX.X, ALU.add))
                    ch.link(nc.vector.reciprocal(first[:, :], r8[:, :]))
                    ch.link(nc.vector.tensor_tensor(prob[:, :, :], prob[:, :, :], wide(first[:, :]), ALU.mult))
                    for c, p in ((0, prob), (1, prob2)):
                        ch.link(nc.vector.tensor_reduce(top[:, :, c], p[:, :, :], AX.X, ALU.max))
                        ch.link(nc.vector.tensor_tensor(eq[:, :, :], p[:, :, :], wide(top[:, :, c]), ALU.is_equal))
                        ch.link(nc.vector.tensor_tensor(cand[:, :, :], eq[:, :, :], iota, ALU.mult))
                        ch.link(nc.vector.tensor_reduce(first[:, :], cand[:, :, :], AX.X, ALU.min))
                        ch.link(nc.vector.tensor_tensor(oh[c][:, :, :], iota, wide(first[:, :]), ALU.is_equal))
                        if c == 0:
                            ch.link(nc.vector.scalar_tensor_tensor(prob2[:, :, :], oh[0][:, :, :], -2.0,
                                                                   prob[:, :, :], ALU.mult, ALU.add))
                    ch.link(nc.vector.tensor_tensor(both[:, :, :], oh[0][:, :, :], oh[1][:, :, :], ALU.add))
                    ch.link(nc.vector.memset(before[:, 0, :], 0.0))
                    for t in range(1, NT):
                        ch.link(nc.vector.tensor_tensor(before[:, t, :], before[:, t - 1, :], both[:, t - 1, :],
                                                        ALU.add))
                    nc.vector.tensor_tensor(total[:, :], before[:, NT - 1, :], both[:, NT - 1, :],
                                            ALU.add).then_inc(s_cnt, 1)
                    ve.wait_ge(s_pos, BASE + 1)
                    ch.link(nc.vector.tensor_scalar(tiles[:, :], ps[1][:, 0:NE], (P - 1) / 2.0, 1.0 / P,
                                                    ALU.add, ALU.mult))
                    ch.link(nc.vector.tensor_scalar(tiles[:, :], tiles[:, :], ROUND, ROUND, ALU.add, ALU.subtract))
                    ch.link(nc.vector.tensor_tensor_scan(ends[:, :], ones[:, 0:NE], tiles[:, :], 0.0,
                                                         ALU.mult, ALU.add))
                    ch.link(nc.vector.tensor_tensor(starts[:, :], ends[:, :], tiles[:, :], ALU.subtract))
                    ch.link(nc.vector.tensor_scalar(starts[:, :], starts[:, :], float(P), None, ALU.mult))
                    ch.link(nc.vector.tensor_tensor(
                        under[:, :, :], ends[0:1, :].unsqueeze(1).to_broadcast([1, ET, NE]),
                        cn[0:1, CN_TILE:CN_TILE + ET * NE].rearrange("p (j e) -> p j e", j=ET), ALU.is_le))
                    ch.link(nc.vector.tensor_reduce(ownf[:, :], under[:, :, :], AX.X, ALU.add))
                    nc.vector.tensor_scalar(owner[:, :], ownf[:, :], float(NE - 1), None, ALU.min).then_inc(s_owner, 1)
                    ch.link(nc.vector.tensor_tensor(
                        place[:, :, :], ps[2][:, 0:NT * NE].rearrange("p (t e) -> p t e", t=NT),
                        starts[:, :].unsqueeze(1).to_broadcast(TE), ALU.add))
                    for c in range(2):
                        ch.link(nc.vector.tensor_tensor(pick[:, :, :], place[:, :, :], oh[c][:, :, :], ALU.mult))
                        ch.link(nc.vector.tensor_reduce(slotf[:, :], pick[:, :, :], AX.X, ALU.add))
                        nc.vector.tensor_copy(slot[:, :, c], slotf[:, :]).then_inc(s_slot, 1)

        xg = sbuf("xg3", [P, 2, D])
        xgT = sbuf("xgT3", [P, DK, P])
        gated, hid = sbuf("gated3", [P, FE]), sbuf("hid3", [P, FE])
        hT = sbuf("hT3", [P, FK, P])
        y = sbuf("y3", [P, 2, D])
        yb = sbuf("yb3", [P, 4, D])
        fc = [W1[:, u * 9216:u * 9216 + NFC].rearrange("p (k n) -> p k n", k=DK) for u in range(2)]
        pj = [W1[:, u * 9216 + NFC:(u + 1) * 9216].rearrange("p (k n) -> p k n", k=FK) for u in range(2)]
        s_fc, s_pj = [sem("s_fc3_0"), sem("s_fc3_1")], [sem("s_pj3_0"), sem("s_pj3_1")]
        xg_in, y_out = [sem("xg_in3_0"), sem("xg_in3_1")], [sem("y_out3_0"), sem("y_out3_1")]
        tr_mm, xgT_sb, a_mm, gl_mm = sem("tr_mm3"), sem("xgT_sb3"), sem("a_mm3"), sem("gl_mm3")
        silu_sb, hid_sb, hT_mm, hT_sb = sem("silu_sb3"), sem("hid_sb3"), sem("hT_mm3"), sem("hT_sb3")
        y_mm, y_sb = sem("y_mm3"), sem("y_sb3")
        s_yb = [sem(f"s_yb3_{n}", pool_dma=True) for n in range(2)]
        added, half = sem("added3"), sem("half3")
        TURNS = (ET - 3) // 2

        def steps(eng, step):
            step(0, 0, 0)
            step(1, 1, 0)
            with eng.Fori(0, TURNS) as i:
                step(2 * i + 2, 0, i + 1)
                step(2 * i + 3, 1, i + 1)
            step(ET - 1, 0, TURNS + 1)

        e.open_sems()
        with nc.Block() as block:
            @block.sync
            def _(sp):
                sp.wait_ge(s_owner, BASE + 1)

                def step(s, u, pair):
                    first = isinstance(s, int) and s < 2
                    own = sp.value_load(owner[0:1, bass.ds(s, 1)], min_val=0, max_val=NE - 1)
                    if not first:
                        sp.wait_ge(tr_mm, BASE + s - 1)
                    sp.dma_start(xg[:, u, :], xg_d[bass.ds(s * P, P), :]).then_inc(xg_in[u], 16)
                    if not first:
                        sp.wait_ge(gl_mm, BASE + s - 1)
                    sp.dma_start(fc[u], a["fc"][bass.ds(own, 1)].rearrange("o p k n -> (o p) k n")).then_inc(s_fc[u], 16)
                    if not first:
                        sp.wait_ge(y_mm, BASE + s - 1)
                    sp.dma_start(pj[u], a["proj"][bass.ds(own, 1)].rearrange("o p k n -> (o p) k n")).then_inc(s_pj[u], 16)
                    if not first:
                        store(s - 2, u)

                def store(s, u):
                    sp.wait_ge(y_sb, BASE + s + 1)
                    sp.dma_start(yg_d[bass.ds(s * P, P), :], y[:, u, :]).then_inc(y_out[u], 16)

                steps(sp, step)
                store(ET - 2, 1)
                store(ET - 1, 0)
                for u in range(2):
                    sp.wait_ge(y_out[u], BASE + 16 * ((ET + 1 - u) // 2))

            @block.tensor
            def _(pe):
                def out_proj(s, u, pair):
                    pe.wait_ge(hid_sb, BASE + s + 1)
                    pe.wait_ge(hT_sb, BASE + 2 * s)
                    for g in range(2):
                        for f in range(FK // 2):
                            tr = nc.tensor.transpose(ps[5 + g][:, f * P:(f + 1) * P],
                                                     hid[:, (g * FK // 2 + f) * P:(g * FK // 2 + f + 1) * P], ident)
                        tr.then_inc(hT_mm, 1)
                    pe.wait_ge(s_pj[u], BASE + 16 * pair + 16)
                    pe.wait_ge(y_sb, BASE + s)
                    for f in range(FK):
                        if f % (FK // 2) == 0:
                            pe.wait_ge(hT_sb, BASE + 2 * s + 1 + f // (FK // 2))
                        mm = nc.tensor.matmul(ps[7], hT[:, f, :], pj[u][:, f, :], start=(f == 0), stop=(f == FK - 1))
                    mm.then_inc(y_mm, 1)

                def step(s, u, pair):
                    pe.wait_ge(xg_in[u], BASE + 16 * pair + 16)
                    pe.wait_ge(xgT_sb, BASE + s)
                    for k in range(DK):
                        tr = nc.tensor.transpose(ps[4][:, k * P:(k + 1) * P], xg[:, u, k * P:(k + 1) * P], ident)
                    tr.then_inc(tr_mm, 1)
                    if not (isinstance(s, int) and s < 2):
                        out_proj(s - 2, u, pair - 1)
                    pe.wait_ge(xgT_sb, BASE + s + 1)
                    pe.wait_ge(s_fc[u], BASE + 16 * pair + 16)
                    for c in range(4):
                        pe.wait_ge(silu_sb if c < 2 else hid_sb, BASE + s)
                        for k in range(DK):
                            mm = nc.tensor.matmul(ps[c][:, 0:HFE], xgT[:, k, :], fc[u][:, k, c * HFE:(c + 1) * HFE],
                                                  start=(k == 0), stop=(k == DK - 1))
                        if c == 1:
                            mm.then_inc(a_mm, 1)
                    mm.then_inc(gl_mm, 1)

                steps(pe, step)
                out_proj(ET - 2, 1, (ET - 2) // 2)
                out_proj(ET - 1, 0, (ET - 1) // 2)

            @block.scalar
            def _(act):
                def hidden_out(s):
                    act.wait_ge(y_mm, BASE + s)
                    for g in range(2):
                        act.wait_ge(hT_mm, BASE + 2 * s + g + 1)
                        n = FK // 2
                        nc.scalar.activation(hT[:, g * n:(g + 1) * n, :].rearrange("p f t -> p (f t)"),
                                             ps[5 + g][:, 0:n * P], ACT.Copy).then_inc(hT_sb, 1)

                def step(s, u, pair):
                    act.wait_ge(tr_mm, BASE + s + 1)
                    act.wait_ge(gl_mm, BASE + s)
                    nc.scalar.activation(xgT[:, :, :].rearrange("p k t -> p (k t)"), ps[4],
                                         ACT.Copy).then_inc(xgT_sb, 1)
                    if not (isinstance(s, int) and s < 2):
                        hidden_out(s - 2)
                    act.wait_ge(a_mm, BASE + s + 1)
                    act.wait_ge(hid_sb, BASE + s)
                    for c in range(2):
                        ins = nc.scalar.activation(gated[:, c * HFE:(c + 1) * HFE], ps[c][:, 0:HFE], ACT.Silu)
                    ins.then_inc(silu_sb, 1)

                steps(act, step)
                hidden_out(ET - 2)
                hidden_out(ET - 1)

            @block.vector
            def _(ve):
                def y_take(s, u, pair):
                    ve.wait_ge(y_mm, BASE + s + 1)
                    ve.wait_ge(y_out[u], BASE + 16 * pair)
                    nc.vector.tensor_copy(y[:, u, :], ps[7]).then_inc(y_sb, 1)

                def step(s, u, pair):
                    if not (isinstance(s, int) and s < 2):
                        y_take(s - 2, u, pair - 1)
                    ve.wait_ge(silu_sb, BASE + s + 1)
                    ve.wait_ge(gl_mm, BASE + s + 1)
                    ve.wait_ge(hT_mm, BASE + 2 * s)
                    for c in range(2):
                        ins = nc.vector.tensor_tensor(hid[:, c * HFE:(c + 1) * HFE], gated[:, c * HFE:(c + 1) * HFE],
                                                      ps[2 + c][:, 0:HFE], ALU.mult)
                    ins.then_inc(hid_sb, 1)

                steps(ve, step)
                y_take(ET - 2, 1, (ET - 2) // 2)
                y_take(ET - 1, 0, (ET - 1) // 2)
                for t in range(NT):
                    ve.wait_ge(s_yb[t % 2], 32 * (t // 2 + 1))
                    for c in range(2):
                        ins = nc.vector.scalar_tensor_tensor(x[:, t, :], yb[:, t % 2 * 2 + c, :], top[:, t, c:c + 1],
                                                             x[:, t, :], ALU.mult, ALU.add)
                        if c == 0:
                            ins.then_inc(half, 1)
                            ve.wait_ge(half, BASE + t + 1)
                    ins.then_inc(added, 1)

            @block.gpsimd
            def _(pool):
                for u in range(2):
                    pool.wait_ge(y_out[u], BASE + 16 * ((ET + 1 - u) // 2))
                for t in range(NT):
                    if t >= 2:
                        pool.wait_ge(added, BASE + t - 1)
                    for c in range(2):
                        nc.gpsimd.indirect_dma_start(
                            out=yb[:, t % 2 * 2 + c, :], out_offset=None, in_=yg_d,
                            in_offset=bass.IndirectOffsetOnAxis(slot[:, t, c:c + 1], axis=0)).then_inc(s_yb[t % 2], 16)


def cross_attention_layer(nc, a, e):
    x, cn, ps, ones, ident, sem, W0 = e.x, e.cn, e.ps, e.ones, e.ident, e.sem, e.W0
    wq4, wk4, wv4, wo4 = e.wq4, e.wk4, e.wv4, e.wo4
    MK = HC // P
    PAIRS = 2 * MK
    JK = J // P
    SCALE = DH1 ** -0.5
    BANKS = 3
    U_U, U_Q, U_O, U_QP, USES = (0, 3, 6, 11), 9, 14, 16, 30
    PRE = 15
    SPLIT_N = (2, 11)
    QB = 3
    with ExitStack() as st:
        def sbuf(name, shape, dt=F32):
            return st.enter_context(nc.sbuf_tensor(name, shape, dt))

        ct_in, cn_in = sbuf("ct_in4", [P, CK, J]), sbuf("cn_in4", [P, JK, C])
        cT = [[sbuf(f"cT4{u}{part}", [P, CK, J], F32R) for part in range(2)] for u in range(2)]
        cN = [sbuf(f"cN4{part}", [P, JK, C], F32R) for part in range(2)]
        qp = sbuf("qp4", [P, 2, CK, H1, S])
        qs = [sbuf(f"qs4{part}", [P, QB, CK, P], F32R) for part in range(2)]
        pT = [sbuf(f"pT4{part}", [P, 2, JK, 512], F32R) for part in range(2)]
        pb = sbuf("pb4", [P, 2, J])
        qT = W0[:, 14336:15360].rearrange("p (m t) -> p m t", m=MK)
        oT = sbuf("oT4", [P, MK, P])
        xT = W0[:, 15360:15872].rearrange("p (k t) -> p k t", k=DK)
        bo = W0[0:1, 15872:16384]
        nmax, rsum, rinv = sbuf("nmax4", [P, 4]), sbuf("rsum4", [P, 4]), sbuf("rinv4", [P, 4])
        ln = Norm(nc, e, "4", sbuf, ps[6], xT)
        s_ct, s_cn, s_bo = sem("s_ct4"), sem("s_cn4"), sem("s_bo4")
        w_mm, w_sb, s_mm, m_dve = sem("w_mm4"), sem("w_sb4"), sem("s_mm4"), sem("m_dve4")
        e_sb, p_dve, pt_mm, pt_sb = sem("e_sb4"), sem("p_dve4"), sem("pt_mm4"), sem("pt_sb4")
        q_hi, q_lo, pt_hi, dve = sem("q_hi4"), sem("q_lo4"), sem("pt_hi4"), sem("dve4")
        ct_hi, ct_lo, cn_hi, cn_lo = sem("ct_hi4"), sem("ct_lo4"), sem("cn_hi4"), sem("cn_lo4")
        y_mm, added = sem("y_mm4"), sem("added4")
        work = [ps[4], ps[5], ps[7]]

        def pair_of(g):
            return qp[:, g // MK, :, 2 * (g % MK):2 * (g % MK) + 2, :].rearrange("p c h t -> p c (h t)")

        def turned(part, g):
            return part[:, g // 4 % 2, :, (g % 4) * P:(g % 4 + 1) * P]

        e.open_sems()
        with nc.Block() as block:
            @block.sync
            def _(sp):
                sp.dma_start(bo, a["bo4"]).then_inc(s_bo, 16)
                sp.dma_start(ct_in[:, :, :], a["ctxT"][0]).then_inc(s_ct, 16)
                sp.dma_start(cn_in[:, :, :], a["ctxN"][0]).then_inc(s_cn, 16)

                def next_T(n):
                    sp.wait_ge(ct_lo, BASE + n + 1)
                    sp.dma_start(ct_in[:, :, :], a["ctxT"][n + 1]).then_inc(s_ct, 16)

                def next_N(n):
                    sp.wait_ge(cn_lo, BASE + n + 1)
                    sp.dma_start(cn_in[:, :, :], a["ctxN"][n + 1]).then_inc(s_cn, 16)

                with sp.Fori(0, NT - 1) as i:
                    next_T(2 * i)
                    next_T(2 * i + 1)
                    next_N(2 * i)
                    next_N(2 * i + 1)
                next_T(B - 2)
                next_N(B - 2)

            @block.gpsimd
            def _(pool):
                ln.pool(pool, 0)
                with pool.Fori(0, NT - 1) as i:
                    ln.pool(pool, i + 1)

            @block.tensor
            def _(pe):
                def work_bank(use):
                    pe.wait_ge(w_sb, BASE + use + 1)

                def taken(use, count=1):
                    pe.wait_ge(w_sb, BASE + BANKS + use + count)

                def product(out, lhs, rhs, steps):
                    terms = [(s, m, n) for s in range(steps) for m, n in ((0, 0), (0, 1), (1, 0))]
                    for t in terms:
                        s, m, n = t
                        mm = nc.tensor.matmul(out, lhs(m, s), rhs(n, s), start=(t == terms[0]), stop=(t == terms[-1]))
                    return mm

                def scores(i, g):
                    b, m = g // MK, g % MK
                    if m == 0:
                        pe.wait_ge(ct_lo, BASE + 2 * i + b + 1)
                    pe.wait_ge(q_lo, BASE + PAIRS * i + g + 1)
                    pe.wait_ge(e_sb, BASE + PAIRS * i + g + 1)
                    product(ps[g % 2], lambda part, c: qs[part][:, g % QB, c, :],
                            lambda part, c: cT[b][part][:, c, :], CK).then_inc(s_mm, 1)

                def turn(i, g):
                    pe.wait_ge(p_dve, BASE + PAIRS * i + g + 1)
                    if g == 0:
                        pe.wait_ge(added, BASE + i)
                    pe.wait_ge(pt_sb, BASE + PAIRS * i + g + 1)
                    for j in range(JK):
                        tr = nc.tensor.transpose(ps[2 + g % 2][:, j * P:(j + 1) * P],
                                                 pb[:, g % 2, j * P:(j + 1) * P], ident)
                    tr.then_inc(pt_mm, 1)

                def weigh(i, h, final=1):
                    if h % 2 == 0:
                        pe.wait_ge(cn_lo, BASE + 2 * i + h // 2 + 1)
                    pe.wait_ge(pt_sb, BASE + PAIRS * i + 4 * h + 4 + 2)
                    for c in range(CK):
                        work_bank(PRE + USES * i + U_U[h] + c)
                        product(work[(U_U[h] + c) % BANKS], lambda part, j: cN[part][:, j, c * P:(c + 1) * P],
                                lambda part, j: pT[part][:, h % 2, j, :], JK).then_inc(w_mm, final if c == CK - 1 else 1)

                def queries(i, use, which):
                    pe.wait_ge(ln.xT_ready, BASE + i + 1)
                    for n in range(2):
                        work_bank(use + n)
                        for m in range(4):
                            col = (4 * n + m) * P
                            for k in range(DK):
                                mm = nc.tensor.matmul(work[(which + n) % BANKS][:, m * P:(m + 1) * P],
                                                      wq4[:, k, col:col + P], xT[:, k, :],
                                                      start=(k == 0), stop=(k == DK - 1))
                        mm.then_inc(w_mm, 1)

                def queries_through_Wk(i, use, which, final):
                    for n in range(2):
                        for c in range(CK):
                            for r in range(2):
                                part = slice(r * DH1, (r + 1) * DH1)
                                step = 2 * (3 * n + c) + r
                                work_bank(use + step)
                                for m in range(4):
                                    mm = nc.tensor.matmul(work[(which + step) % BANKS][:, m * P:(m + 1) * P],
                                                          wk4[part, 4 * n + m, c * P:(c + 1) * P],
                                                          qT[part, 4 * n + m, :], start=True, stop=True)
                                mm.then_inc(w_mm, final if step == 11 else 1)

                def tile(i, last):
                    use = PRE + USES * i
                    scores(i, 0)
                    scores(i, 1)
                    for g in range(PAIRS):
                        if g + 2 < PAIRS:
                            scores(i, g + 2)
                        turn(i, g)
                        if g == 3 and not last:
                            ln.tensor(pe, i + 1)
                        if g % 4 == 1 and g > 4:
                            weigh(i, g // 4 - 1, 3 if last and g == 13 else 1)
                    if not last:
                        queries(i + 1, use + U_Q, U_Q)
                    weigh(i, 3)
                    taken(use + U_U[2] + 2)
                    for n in range(2):
                        if n:
                            taken(use + U_U[3] + 2)
                        work_bank(use + U_O + n)
                        bank = work[(U_O + n) % BANKS]
                        for m in range(4):
                            for r in range(2):
                                h = 2 * (4 * n + m) + r
                                for c in range(CK):
                                    mm = nc.tensor.matmul(
                                        bank[r * DH1:(r + 1) * DH1, m * P:(m + 1) * P].rearrange("p (b t) -> p b t", b=2),
                                        wv4[:, c, h * DH1:(h + 1) * DH1], qp[:, :, c, h, :],
                                        start=(c == 0), stop=(c == CK - 1))
                        mm.then_inc(w_mm, 1)
                    if not last:
                        queries_through_Wk(i + 1, use + U_QP, U_QP, 3)
                    taken(use + U_O + 1)
                    pe.wait_ge(pt_sb, BASE + PAIRS * i + PAIRS + 1)
                    for m in range(MK):
                        nc.tensor.matmul(ps[2], oT[:, m, :], wo4[:, m, :], start=(m == 0), stop=False)
                    nc.tensor.matmul(ps[2], ones[0:1, :], bo, start=False, stop=True).then_inc(y_mm, 1)

                pe.sem_inc(pt_mm, 1)
                ln.tensor(pe, 0)
                pe.wait_ge(e.s_w4, BASE + 64)
                pe.wait_ge(s_bo, BASE + 16)
                queries(0, 0, 0)
                taken(1)
                queries_through_Wk(0, 2, 2, 2)
                with pe.Fori(0, NT - 1) as i:
                    tile(i, False)
                tile(NT - 1, True)

            @block.scalar
            def _(act):
                def take(use, which, out, scale=1.0, count=1):
                    act.wait_ge(w_mm, BASE + use + count)
                    src = work[which % BANKS]
                    if len(out.shape) == 4:
                        src = src.rearrange("p (m b t) -> p m b t", m=4, b=2)
                    nc.scalar.activation(out, src, ACT.Copy, scale=scale).then_inc(w_sb, count)

                def exponent(i, g):
                    act.wait_ge(m_dve, BASE + PAIRS * i + g + 1)
                    act.wait_ge(pt_mm, BASE + PAIRS * i + g)
                    nc.scalar.activation(pb[:, g % 2, :], ps[g % 2], ACT.Exp, bias=nmax[:, g % 4:g % 4 + 1],
                                         accum_out=rsum[:, g % 4:g % 4 + 1]).then_inc(e_sb, 1)

                def first_q(i, g):
                    nc.scalar.activation(qs[0][:, g % QB, :, :], pair_of(g), ACT.Copy).then_inc(q_hi, 1)

                def first_T(i, u):
                    act.wait_ge(s_ct, BASE + 16 * (2 * i + u) + 16)
                    nc.scalar.activation(cT[u][0][:, :, :], ct_in[:, :, :], ACT.Copy).then_inc(ct_hi, 1)

                def first_N(i, u):
                    act.wait_ge(s_cn, BASE + 16 * (2 * i + u) + 16)
                    nc.scalar.activation(cN[0][:, :, :], cn_in[:, :, :], ACT.Copy).then_inc(cn_hi, 1)

                def first_P(i, g):
                    act.wait_ge(pt_mm, BASE + PAIRS * i + g + 2)
                    nc.scalar.activation(turned(pT[0], g), ps[2 + g % 2].rearrange("p (j n) -> p j n", j=JK),
                                         ACT.Copy).then_inc(pt_hi, 1)

                def weighed(i, h, final=1):
                    for c in range(CK):
                        take(PRE + USES * i + U_U[h] + c, U_U[h] + c,
                             qp[:, h // 2, c, 8 * (h % 2):8 * (h % 2) + 8, :].rearrange("p h t -> p (h t)"),
                             count=final if c == CK - 1 else 1)

                def queries(use, which):
                    for n in range(2):
                        take(use + n, which + n, qT[:, 4 * n:4 * n + 4, :].rearrange("p m t -> p (m t)"), SCALE)

                def queries_through_Wk(i, use, which, final):
                    for n in range(2):
                        for c in range(CK):
                            for r in range(2):
                                heads = qp[:, :, c, 8 * n + r:8 * n + 8:2, :].rearrange("p b m t -> p m b t")
                                step = 2 * (3 * n + c) + r
                                take(use + step, which + step, heads, count=final if step == 11 else 1)
                        if n == 0:
                            act.wait_ge(w_sb, BASE + BANKS + use + 6)
                            for g in range(QB):
                                first_q(i, g)
                    act.wait_ge(w_sb, BASE + BANKS + use + 11 + final)

                def tile(i, last):
                    use = PRE + USES * i
                    for g in range(PAIRS):
                        if g < PAIRS - 1:
                            exponent(i, g)
                        if g == PAIRS - 2:
                            exponent(i, g + 1)
                        if g:
                            first_P(i, g - 1)
                        if g + QB < PAIRS:
                            first_q(i, g + QB)
                        if g % 4 == 2 and g > 4:
                            weighed(i, g // 4 - 1, 3 if last and g == 14 else 1)
                        if g == 0:
                            first_T(i, 1)
                        if g == 4 and not last:
                            ln.scalar(act, i + 1, w_mm, use - 13)
                        if g in SPLIT_N:
                            first_N(i, g // MK)
                    first_P(i, PAIRS - 1)
                    if not last:
                        queries(use + U_Q, U_Q)
                        first_T(i + 1, 0)
                    weighed(i, 3)
                    for n in range(2):
                        take(use + U_O + n, U_O + n, oT[:, 4 * n:4 * n + 4, :].rearrange("p m t -> p (m t)"))
                    if not last:
                        queries_through_Wk(i + 1, use + U_QP, U_QP, 3)

                act.sem_inc(w_sb, BANKS)
                act.sem_inc(e_sb, 2)
                ln.scalar(act, 0, w_mm, 0)
                queries(0, 0)
                first_T(0, 0)
                queries_through_Wk(0, 2, 2, 2)
                with act.Fori(0, NT - 1) as i:
                    tile(i, False)
                tile(NT - 1, True)

            @block.vector
            def _(ve):
                ch = Chain(ve, dve)

                def maximum(i, g):
                    ve.wait_ge(s_mm, BASE + PAIRS * i + g + 1)
                    nc.vector.tensor_reduce(nmax[:, g % 4:g % 4 + 1], ps[g % 2], AX.X, ALU.max,
                                            negate=True).then_inc(m_dve, 1)

                def rest(out, whole, first):
                    return nc.vector.tensor_tensor(out, whole, first.bitcast(F32), ALU.subtract)

                def rest_q(i, g):
                    ve.wait_ge(q_hi, BASE + PAIRS * i + g + 1)
                    rest(qs[1][:, g % QB, :, :], pair_of(g), qs[0][:, g % QB, :, :]).then_inc(q_lo, 1)

                def rest_T(i, u):
                    ve.wait_ge(ct_hi, BASE + 2 * i + u + 1)
                    rest(cT[u][1][:, :, :], ct_in[:, :, :], cT[u][0][:, :, :]).then_inc(ct_lo, 1)

                def rest_N(i, u):
                    ve.wait_ge(cn_hi, BASE + 2 * i + u + 1)
                    rest(cN[1][:, :, :], cn_in[:, :, :], cN[0][:, :, :]).then_inc(cn_lo, 1)

                def rest_P(i, g):
                    ve.wait_ge(pt_hi, BASE + PAIRS * i + g + 1)
                    rest(turned(pT[1], g), ps[2 + g % 2].rearrange("p (j n) -> p j n", j=JK),
                         turned(pT[0], g)).then_inc(pt_sb, 1)

                def tile(i, last):
                    if not last:
                        ln.vector_stats(ch, i + 1)
                        ln.vector_norm(ve, i + 1)
                    maximum(i, 0)
                    maximum(i, 1)
                    for g in range(PAIRS):
                        ve.wait_ge(e_sb, BASE + PAIRS * i + g + 1 + 2)
                        r = rinv[:, g % 4:g % 4 + 1]
                        ch.link(nc.vector.reciprocal(r, rsum[:, g % 4:g % 4 + 1]))
                        nc.vector.tensor_scalar(pb[:, g % 2, :], pb[:, g % 2, :], r, None, ALU.mult).then_inc(p_dve, 1)
                        if g:
                            rest_P(i, g - 1)
                        if g + QB < PAIRS:
                            rest_q(i, g + QB)
                        if g + 2 < PAIRS:
                            maximum(i, g + 2)
                        if g == 0:
                            rest_T(i, 1)
                        if g in SPLIT_N:
                            rest_N(i, g // MK)
                    rest_P(i, PAIRS - 1)
                    if not last:
                        rest_T(i + 1, 0)
                        for g in range(QB):
                            rest_q(i + 1, g)
                    ve.wait_ge(y_mm, BASE + i + 1)
                    nc.vector.tensor_tensor(x[:, i, :], x[:, i, :], ps[2], ALU.add).then_inc(added, 1)

                ve.sem_inc(pt_sb, 2)
                ln.vector_stats(ch, 0)
                ln.vector_norm(ve, 0)
                rest_T(0, 0)
                for g in range(QB):
                    rest_q(0, g)
                with ve.Fori(0, NT - 1) as i:
                    ch.turn(i, 2 + PAIRS)
                    tile(i, False)
                ch.again(NT - 1)
                tile(NT - 1, True)

def decayed_attention_layer(nc, a, e):
    x, cn, ps, ones, ident, sem, w5, W0 = e.x, e.cn, e.ps, e.ones, e.ident, e.sem, e.w5, e.W0
    v_d, ba_d = e.v_d, e.ba_d
    sel = cn[:, CN_SEL:CN_SEL + B]
    G = 8
    NG = S // G
    with ExitStack() as st:
        def sbuf(name, shape, dt=F32):
            return st.enter_context(nc.sbuf_tensor(name, shape, dt))

        ba = sbuf("ba5", [P, NT, 2 * HS])
        baT = sbuf("baT5", [2 * HS, B * S])
        s_w5 = [sem(f"s_w5_{w}") for w in range(5)]
        s_v, s_ba, baT_sb = sem("s_v5"), sem("s_ba5"), sem("baT_sb5")

        with ExitStack() as pt:
            def pbuf(name, shape, dt=F32):
                return pt.enter_context(nc.sbuf_tensor(name, shape, dt))

            xT = pbuf("xT5", [P, DK, P])
            ln = Norm(nc, e, "5", pbuf, ps[7], xT)
            q, qk, mag, ex, lg, soft = (pbuf(n, [P, D]) for n in ("q5", "qk5", "mag5", "ex5", "lg5", "soft5"))
            v0, ve_, vv = pbuf("v05", [P, D]), pbuf("veps5", [P, D]), pbuf("vv5", [P, 2, D])
            bal = pbuf("bal5", [1, D])
            s_bal, q_mm, k_mm, v_mm, a_mm = sem("s_bal5"), sem("q_mm5"), sem("k_mm5"), sem("v_mm5"), sem("a_mm5")
            q_sb, mag_sb, ex_sb, lg_sb = sem("q_sb5"), sem("mag_sb5"), sem("ex_sb5"), sem("lg_sb5")
            k_used, v_used, a_used, v_sb, vv_sb = sem("k_used5"), sem("v_used5"), sem("a_used5"), sem("v_sb5"), sem("vv_sb5")
            v_out = [sem("v_out5_0"), sem("v_out5_1")]
            ba_sb, t_mm, dve = sem("ba_sb5"), sem("t_mm5"), sem("dve5")

            e.open_sems()
            with nc.Block() as block:
                @block.sync
                def _(sp):
                    sp.dma_start(bal[:, :], a["ba5"]).then_inc(s_bal, 16)
                    for w in (0, 3, 1, 2, 4):
                        sp.dma_start(w5[:, w], a["w5"][:, w]).then_inc(s_w5[w], 16)
                    sp.dma_start(e.w16, a["w16"]).then_inc(e.s_w6, 16)
                    sp.dma_start(e.w26, a["w26"]).then_inc(e.s_w6, 16)
                    with sp.Fori(0, NT // 2) as i:
                        for u in range(2):
                            sp.wait_ge(vv_sb, BASE + 2 * i + u + 1)
                            sp.dma_start(v_d[bass.ds((2 * i + u) * P, P), :], vv[:, u, :]).then_inc(v_out[u], 16)
                    sp.wait_ge(baT_sb, BASE + 2)
                    for c in range(2):
                        sp.dma_start(ba_d[c].rearrange("(b h) t -> h b t", b=B),
                                     baT[c * HS:(c + 1) * HS, :].rearrange("h (b t) -> h b t", b=B)).then_inc(s_ba, 16)
                    for u in range(2):
                        sp.wait_ge(v_out[u], BASE + 16 * NT // 2)
                    sp.wait_ge(s_ba, BASE + 32)
                    sp.wait_ge(s_w5[4], BASE + 16)

                @block.gpsimd
                def _(pool):
                    ln.pool(pool, 0)
                    with pool.Fori(0, NT) as i:
                        ln.pool(pool, i + 1)

                @block.tensor
                def _(pe):
                    ln.tensor(pe, 0)
                    pe.wait_ge(s_bal, BASE + 16)
                    with pe.Fori(0, NT) as i:
                        pe.wait_ge(ln.xT_ready, BASE + i + 1)
                        for bank, w, done, used in ((0, 0, q_mm, q_sb), (1, 3, a_mm, a_used),
                                                    (2, 1, k_mm, k_used), (3, 2, v_mm, v_used)):
                            pe.wait_ge(s_w5[w], BASE + 16)
                            pe.wait_ge(used, BASE + i)
                            for k in range(DK):
                                mm = nc.tensor.matmul(ps[bank], xT[:, k, :], w5[:, w, k, :], start=(k == 0),
                                                      stop=(w != 3 and k == DK - 1))
                            if w == 3:
                                mm = nc.tensor.matmul(ps[bank], ones[0:1, :], bal[0:1, :], start=False, stop=True)
                            mm.then_inc(done, 1)
                        ln.tensor(pe, i + 1)
                    pe.wait_ge(ba_sb, BASE + 2 * NT)
                    for t in range(NT):
                        tr = nc.tensor.transpose(ps[4 + t // 4][0:2 * HS, t % 4 * P:(t % 4 + 1) * P], ba[:, t, :], ident)
                        if t % 4 == 3:
                            tr.then_inc(t_mm, 1)

                @block.scalar
                def _(act):
                    ln.scalar(act, 0, v_mm)
                    with act.Fori(0, NT) as i:
                        act.wait_ge(q_mm, BASE + i + 1)
                        act.wait_ge(k_used, BASE + i)
                        nc.scalar.activation(q[:, :], ps[0], ACT.Copy, scale=DHS ** -0.5).then_inc(q_sb, 1)
                        act.wait_ge(a_mm, BASE + i + 1)
                        nc.scalar.activation(mag[:, :], ps[1], ACT.Abs).then_inc(mag_sb, 1)
                        act.wait_ge(mag_sb, BASE + i + 1)
                        nc.scalar.activation(ex[:, :], mag[:, :], ACT.Exp, scale=-1.0).then_inc(ex_sb, 1)
                        act.wait_ge(ex_sb, BASE + i + 1)
                        act.wait_ge(a_used, BASE + i)
                        nc.scalar.activation(lg[:, :], ex[:, :], ACT.Ln, bias=cn[:, CN_ONE:CN_ONE + 1]).then_inc(lg_sb, 1)
                        ln.scalar(act, i + 1, v_mm)
                    for g in range(2):
                        act.wait_ge(t_mm, BASE + g + 1)
                        nc.scalar.activation(baT[:, g * 512:(g + 1) * 512], ps[4 + g][0:2 * HS, :],
                                             ACT.Copy).then_inc(baT_sb, 1)

                @block.vector
                def _(ve):
                    ch = Chain(ve, dve)
                    ln.vector_stats(ch, 0)
                    ln.vector_norm(ve, 0)
                    with ve.Fori(0, NT // 2) as i2:
                        ch.turn(i2, 4)
                        for u in range(2):
                            i = 2 * i2 + u
                            ln.vector_stats(ch, i + 1)
                            ve.wait_ge(lg_sb, BASE + i + 1)
                            nc.vector.scalar_tensor_tensor(soft[:, :], ps[1], 0.0, lg[:, :], ALU.max,
                                                           ALU.add).then_inc(a_used, 1)
                            ve.wait_ge(a_used, BASE + i + 1)
                            nc.vector.tensor_reduce(ba[:, i, HS:2 * HS], soft[:, :].rearrange("p (h d) -> p h d", h=HS),
                                                    AX.X, ALU.add, negate=True).then_inc(ba_sb, 1)
                            ve.wait_ge(q_sb, BASE + i + 1)
                            ve.wait_ge(k_mm, BASE + i + 1)
                            nc.vector.tensor_tensor(qk[:, :], q[:, :], ps[2], ALU.mult).then_inc(k_used, 1)
                            ln.vector_norm(ve, i + 1)
                            ve.wait_ge(k_used, BASE + i + 1)
                            nc.vector.tensor_reduce(ba[:, i, 0:HS], qk[:, :].rearrange("p (h d) -> p h d", h=HS),
                                                    AX.X, ALU.add).then_inc(ba_sb, 1)
                            ve.wait_ge(v_mm, BASE + i + 1)
                            nc.vector.tensor_scalar(v0[:, :], ps[3], 0.0, None, ALU.add).then_inc(v_used, 1)
                            ve.wait_ge(v_used, BASE + i + 1)
                            nc.vector.tensor_scalar(ve_[:, :].bitcast(U32), v0[:, :].bitcast(U32), SIGN_BIT, EPS_BITS,
                                                    ALU.bitwise_and, ALU.bitwise_or).then_inc(v_sb, 1)
                            ve.wait_ge(v_sb, BASE + i + 1)
                            ve.wait_ge(v_out[u], BASE + 16 * i2)
                            nc.vector.tensor_tensor(vv[:, u, :], v0[:, :], ve_[:, :], ALU.add).then_inc(vv_sb, 1)
                        assert ch.n == 4

        BS = [P, S]
        bS, aS, mx, t1, t2, eA, eB, dn, rd = (sbuf(n, BS) for n in
                                              ("bS5", "aS5", "mx5", "t15", "t25", "eA5", "eB5", "dn5", "rd5"))
        al, be, eal, ebe = (sbuf(n, BS) for n in ("al5", "be5", "eal5", "ebe5"))
        vb = sbuf("vb5", [P, 2, G, D])
        W1 = e.W1
        off = 10240
        rb = W1[:, off:off + 2048].rearrange("p (n d) -> p n d", n=4)
        bv = W1[:, off + 2048:off + 3072].rearrange("p (n d) -> p n d", n=2)
        ebv = W1[:, off + 3072:off + 4096].rearrange("p (n d) -> p n d", n=2)
        ear, s_, ep, sg = (W1[:, off + 4096 + n * D:off + 4096 + (n + 1) * D] for n in range(4))
        yT = W1[:, 0:DK * B * S].rearrange("p (k n) -> p k n", k=DK)
        s_in, s_vb = sem("s_in5"), [sem("s_vb5_0"), sem("s_vb5_1")]
        t_dve, t_exp, coef = sem("t_dve5"), sem("t_exp5"), sem("coef5")
        bv_sb, ebv_sb, ear_sb, r_sb = sem("bv_sb5"), sem("ebv_sb5"), sem("ear_sb5"), sem("r_sb5")
        s_sb, sg_sb = sem("s_sb5"), sem("sg_sb5")
        y_mm, yT_sb, z_mm, z_used, ch5 = sem("y_mm5"), sem("yT_sb5"), sem("z_mm5"), sem("z_used5"), sem("ch5")
        RB = 4

        e.open_sems()
        with nc.Block() as block:
            @block.sync
            def _(sp):
                sp.dma_start(bS[:, :], ba_d[0]).then_inc(s_in, 16)
                sp.dma_start(aS[:, :], ba_d[1]).then_inc(s_in, 16)

                def load(group, u):
                    for b in range(B):
                        rows = v_d[bass.ds(group * G + b * S, G), :].rearrange("t d -> (t d)")
                        sp.dma_start(vb[b * HS:(b + 1) * HS, u].rearrange("p t d -> p (t d)"),
                                     rows.partition_broadcast(HS)).then_inc(s_vb[u], 16)

                load(0, 0)
                load(1, 1)
                with sp.Fori(0, NG // 2 - 1) as i:
                    for u in range(2):
                        sp.wait_ge(ebv_sb, BASE + 2 * G * i + G * (u + 1))
                        load(2 * i + 2 + u, u)

            @block.vector
            def _(ve):
                ch = Chain(ve, ch5)
                ve.wait_ge(s_in, BASE + 32)
                ch.link(nc.vector.memset(eA[:, 0:1], 0.0))
                ch.link(nc.vector.memset(al[:, 0:1], 0.0))
                ch.link(nc.vector.memset(rb[:, RB - 1, :], 0.0))
                ch.link(nc.vector.tensor_tensor_scan(mx[:, :], aS[:, :], bS[:, :], -3.0e38, ALU.add, ALU.max))
                ch.link(nc.vector.tensor_tensor(t1[:, 1:S], aS[:, 1:S], mx[:, 0:S - 1], ALU.add))
                nc.vector.tensor_tensor(t1[:, 1:S], t1[:, 1:S], mx[:, 1:S], ALU.subtract).then_inc(t_dve, 1)
                nc.vector.tensor_tensor(t2[:, :], bS[:, :], mx[:, :], ALU.subtract).then_inc(t_dve, 1)
                ve.wait_ge(t_exp, BASE + 2)
                ch.link(nc.vector.tensor_tensor_scan(dn[:, :], eA[:, :], eB[:, :], 0.0, ALU.mult, ALU.add))
                ch.link(nc.vector.reciprocal(rd[:, :], dn[:, :]))
                ch.link(nc.vector.tensor_tensor(al[:, 1:S], eA[:, 1:S], dn[:, 0:S - 1], ALU.mult))
                ch.link(nc.vector.tensor_tensor(al[:, 1:S], al[:, 1:S], rd[:, 1:S], ALU.mult))
                ch.link(nc.vector.tensor_tensor(be[:, :], eB[:, :], rd[:, :], ALU.mult))
                ch.link(nc.vector.tensor_scalar(eal[:, :], al[:, :], EPS, None, ALU.mult))
                ch.link(nc.vector.tensor_scalar(ebe[:, :], be[:, :], EPS, None, ALU.mult))
                nc.vector.memset(ebe[:, 0:1], 0.0).then_inc(coef, 1)
                ve.wait_ge(coef, BASE + 1)
                with ve.Fori(0, S // (2 * G)) as i:
                    for j in range(2 * G):
                        t = 2 * G * i + j
                        old, new = rb[:, (j - 1) % RB, :], rb[:, j % RB, :]
                        ve.wait_ge(r_sb, BASE + t)
                        ve.wait_ge(bv_sb, BASE + t + 1)
                        nc.vector.scalar_tensor_tensor(s_, old, al[:, bass.ds(t, 1)], bv[:, j % 2, :],
                                                       ALU.mult, ALU.add).then_inc(s_sb, 1)
                        ve.wait_ge(ebv_sb, BASE + t + 1)
                        ve.wait_ge(ear_sb, BASE + t + 1)
                        nc.vector.tensor_tensor(ep, ear, ebv[:, j % 2, :], ALU.max).then_inc(sg_sb, 1)
                        ve.wait_ge(sg_sb, BASE + 2 * t + 1)
                        ve.wait_ge(s_sb, BASE + t + 1)
                        nc.vector.scalar_tensor_tensor(sg.bitcast(U32), s_.bitcast(U32), SIGN_BIT, ep.bitcast(U32),
                                                       ALU.bitwise_and, ALU.bitwise_or).then_inc(sg_sb, 1)
                        ve.wait_ge(sg_sb, BASE + 2 * t + 2)
                        ve.wait_ge(y_mm, BASE + t + 1)
                        nc.vector.tensor_tensor(new, s_, sg, ALU.add).then_inc(r_sb, 1)
                for t in range(NT):
                    ve.wait_ge(z_mm, BASE + t + 1)
                    nc.vector.tensor_tensor(x[:, t, :], x[:, t, :], ps[2 + t % 4], ALU.add).then_inc(z_used, 1)

            @block.scalar
            def _(act):
                act.wait_ge(t_dve, BASE + 2)
                nc.scalar.activation(eA[:, 1:S], t1[:, 1:S], ACT.Exp).then_inc(t_exp, 1)
                nc.scalar.activation(eB[:, :], t2[:, :], ACT.Exp).then_inc(t_exp, 1)
                act.wait_ge(coef, BASE + 1)
                with act.Fori(0, S // (2 * G)) as i:
                    for j in range(2 * G):
                        t = 2 * G * i + j
                        u = j // G
                        if j % G == 0:
                            act.wait_ge(s_vb[u], BASE + 16 * B * (i + 1))
                        act.wait_ge(s_sb, BASE + t)
                        nc.scalar.activation(bv[:, j % 2, :], vb[:, u, j % G, :], ACT.Copy,
                                             scale=be[:, bass.ds(t, 1)]).then_inc(bv_sb, 1)
                        nc.scalar.activation(ebv[:, j % 2, :], vb[:, u, j % G, :], ACT.Abs,
                                             scale=ebe[:, bass.ds(t, 1)]).then_inc(ebv_sb, 1)
                        act.wait_ge(r_sb, BASE + t)
                        nc.scalar.activation(ear, rb[:, (j - 1) % RB, :], ACT.Abs,
                                             scale=eal[:, bass.ds(t, 1)]).then_inc(ear_sb, 1)
                    for u in range(2):
                        act.wait_ge(y_mm, BASE + 2 * G * i + G * (u + 1) + RB)
                        out = yT[:, :, :].rearrange("p k (b t) -> p k t b", b=B)[:, :, bass.ds(2 * G * i + G * u, G), :]
                        nc.scalar.activation(out, ps[u].rearrange("p (k t b) -> p k t b", k=DK, t=G),
                                             ACT.Copy).then_inc(yT_sb, 1)

            @block.tensor
            def _(pe):
                pe.sem_inc(y_mm, RB)
                with pe.Fori(0, S // (2 * G)) as i:
                    for j in range(2 * G):
                        t = 2 * G * i + j
                        u = j // G
                        if j == 0:
                            pe.wait_ge(yT_sb, BASE + 2 * i)
                        pe.wait_ge(r_sb, BASE + t + 1)
                        for k in range(DK):
                            col = k * G * B + (j % G) * B
                            mm = nc.tensor.matmul(ps[u][:, col:col + B], rb[:, j % RB, k * P:(k + 1) * P], sel,
                                                  start=True, stop=True)
                        mm.then_inc(y_mm, 1)
                pe.wait_ge(yT_sb, BASE + NG)
                pe.wait_ge(s_w5[4], BASE + 16)
                for t in range(NT):
                    if t >= 4:
                        pe.wait_ge(z_used, BASE + t - 3)
                    for k in range(DK):
                        mm = nc.tensor.matmul(ps[2 + t % 4], yT[:, k, t * P:(t + 1) * P], w5[:, 4, k, :],
                                              start=(k == 0), stop=(k == DK - 1))
                    mm.then_inc(z_mm, 1)


def feed_forward_layer(nc, a, e):
    x, cn, ps, ident, sem, w16, w26, W1 = e.x, e.cn, e.ps, e.ident, e.sem, e.w16, e.w26, e.W1
    FT = FF // P
    TG = 4
    NGR = NT // TG
    TOP = 4.0 * QUANT
    STEP = QUANT / 4.0
    out = e.out
    with ExitStack() as st:
        def sbuf(name, shape, dt=F32):
            return st.enter_context(nc.sbuf_tensor(name, shape, dt))

        hs = W1[:, 0:NGR * FT * 512].rearrange("p (g f t) -> p g f t", g=NGR, f=FT)
        xT = [sbuf("xT6", [P, DK, TG * P]), W1[:, NGR * FT * 512:].rearrange("p (k t) -> p k t", k=DK)]
        b1, b1q = sbuf("b16", [P, FT]), sbuf("b1q6", [P, FT])
        b2 = sbuf("b26", [P, D])
        h, r, c, w, km, g0, g1, up = (sbuf(n, [P, 2, 512]) for n in
                                      ("h6", "r6", "c6", "w6", "km6", "g06", "g16", "up6"))
        dg = sbuf("dg6", [P, 2, 512])
        y = sbuf("y6", [P, 512])
        z = x[:, NT, :]
        ln = Norm(nc, e, "6", sbuf, ps[7], None)
        s_b, b_q, dve = sem("s_b6"), sem("b_q6"), sem("dve6")
        h_mm, h_sb, r_sb, c_sb, w_sb, km_sb, g_sb, up_sb, dg_sb, hs_sb = (
            sem(n) for n in ("h_mm6", "h_sb6", "r_sb6", "c_sb6", "w_sb6", "km_sb6", "g_sb6", "up_sb6", "dg_sb6", "hs_sb6"))
        z_mm, z_used, x_done, s_out = sem("z_mm6"), sem("z_used6"), sem("x_done6"), sem("s_out6")
        N = NGR * FT
        HB, ZB = 3, 3
        NORM_AT = [3 + 2 * t for t in range(TG)]

        e.open_sems()
        with nc.Block() as block:
            @block.sync
            def _(sp):
                sp.dma_start(b1[:, :], a["b16"]).then_inc(s_b, 16)
                sp.dma_start(b2[:, :], a["b26"]).then_inc(s_b, 16)
                for t in range(NT):
                    sp.wait_ge(x_done, BASE + t + 1)
                    sp.dma_start(out[:, t, :], x[:, t, :]).then_inc(s_out, 16)
                sp.wait_ge(s_out, BASE + 16 * NT)

            @block.gpsimd
            def _(pool):
                def slope(n):
                    pool.wait_ge(g_sb, BASE + 2 * n + 2)
                    if n >= 2:
                        pool.wait_ge(hs_sb, BASE + n - 1)
                    nc.gpsimd.tensor_tensor(dg[:, n % 2, :], g1[:, n % 2, :], g0[:, n % 2, :],
                                            ALU.subtract).then_inc(dg_sb, 1)

                for t in range(TG):
                    ln.pool(pool, t)
                for n in range(N):
                    slope(n)
                    if n in NORM_AT:
                        ln.pool(pool, TG + NORM_AT.index(n))

            @block.tensor
            def _(pe):
                def hidden(n):
                    g, f = divmod(n, FT)
                    if f == 0:
                        pe.wait_ge(ln.xT_ready, BASE + TG * (g + 1))
                    if n >= HB:
                        pe.wait_ge(h_sb, BASE + n - HB + 1)
                    for k in range(DK):
                        mm = nc.tensor.matmul(ps[n % HB], w16[:, k, f * P:(f + 1) * P], xT[g][:, k, :],
                                              start=(k == 0), stop=(k == DK - 1))
                    mm.then_inc(h_mm, 1)

                def output(t, f0, f1):
                    if f0 == 0 and t >= ZB:
                        pe.wait_ge(z_used, BASE + t - ZB + 1)
                    for f in range(f0, f1):
                        pe.wait_ge(hs_sb, BASE + FT * (t // TG) + f + 1)
                        mm = nc.tensor.matmul(ps[HB + t % ZB], hs[:, t // TG, f, (t % TG) * P:(t % TG + 1) * P],
                                              w26[:, f, :], start=(f == 0), stop=(f == FT - 1))
                    if f1 == FT:
                        mm.then_inc(z_mm, 1)

                for t in range(TG):
                    ln.tensor(pe, t)
                pe.wait_ge(e.s_w6, BASE + 32)
                for n in range(FT):
                    hidden(n)
                    if n - 2 in NORM_AT:
                        ln.tensor(pe, TG + NORM_AT.index(n - 2))
                per = FT // TG
                for f in range(FT):
                    hidden(FT + f)
                    output(f // per, f % per * per, (f % per + 1) * per)
                for t in range(TG, NT):
                    output(t, 0, FT)

            @block.scalar
            def _(act):
                def norm_out(t):
                    act.wait_ge(ln.turned, BASE + t + 1)
                    part = xT[t // TG][:, :, t % TG * P:(t % TG + 1) * P]
                    nc.scalar.activation(part, ps[7].rearrange("p (k t) -> p k t", k=DK),
                                         ACT.Copy).then_inc(ln.xT_ready, 1)

                def stage_a(n):
                    act.wait_ge(h_mm, BASE + n + 1)
                    if n >= 2:
                        act.wait_ge(r_sb, BASE + n - 1)
                    nc.scalar.activation(h[:, n % 2, :], ps[n % HB], ACT.Identity, scale=QUANT,
                                         bias=b1q[:, n % FT:n % FT + 1]).then_inc(h_sb, 1)

                def stage_b(n):
                    u = n % 2
                    act.wait_ge(w_sb, BASE + n + 1)
                    if n >= 2:
                        act.wait_ge(hs_sb, BASE + n - 1)
                        act.wait_ge(dg_sb, BASE + n - 1)
                    nc.scalar.activation(km[:, u, :], w[:, u, :], ACT.Identity,
                                         bias=cn[:, CN_ROUND:CN_ROUND + 1]).then_inc(km_sb, 1)
                    nc.scalar.activation(up[:, u, :], r[:, u, :], ACT.Relu,
                                         bias=cn[:, CN_TOP:CN_TOP + 1]).then_inc(up_sb, 1)
                    act.wait_ge(km_sb, BASE + n + 1)
                    nc.scalar.activation(g0[:, u, :], km[:, u, :], ACT.Gelu, scale=0.25,
                                         bias=cn[:, CN_K0:CN_K0 + 1]).then_inc(g_sb, 1)
                    nc.scalar.activation(g1[:, u, :], km[:, u, :], ACT.Gelu, scale=0.25,
                                         bias=cn[:, CN_K1:CN_K1 + 1]).then_inc(g_sb, 1)

                for t in range(TG):
                    norm_out(t)
                act.wait_ge(b_q, BASE + 2)
                stage_a(0)
                for n in range(N):
                    if n + 1 < N:
                        stage_a(n + 1)
                    stage_b(n)
                    if n - 2 in NORM_AT:
                        norm_out(TG + NORM_AT.index(n - 2))

            @block.vector
            def _(ve):
                ch = Chain(ve, dve)

                def round_(n):
                    u = n % 2
                    ve.wait_ge(h_sb, BASE + n + 1)
                    if n >= 2:
                        ve.wait_ge(up_sb, BASE + n - 1)
                    nc.vector.tensor_scalar(r[:, u, :], h[:, u, :], ROUND, ROUND, ALU.add,
                                            ALU.subtract).then_inc(r_sb, 1)
                    ve.wait_ge(r_sb, BASE + n + 1)
                    nc.vector.tensor_scalar(c[:, u, :], r[:, u, :], -TOP, TOP, ALU.max, ALU.min).then_inc(c_sb, 1)
                    ve.wait_ge(c_sb, BASE + n + 1)
                    if n >= 2:
                        ve.wait_ge(km_sb, BASE + n - 1)
                    nc.vector.tensor_scalar(w[:, u, :], c[:, u, :], -(STEP - 1) / 2, 1.0 / STEP, ALU.add,
                                            ALU.mult).then_inc(w_sb, 1)

                def interpolate(n):
                    g, f = divmod(n, FT)
                    u = n % 2
                    ve.wait_ge(km_sb, BASE + n + 1)
                    ch.link(nc.vector.scalar_tensor_tensor(c[:, u, :], km[:, u, :], ROUND, w[:, u, :],
                                                           ALU.subtract, ALU.subtract))
                    ve.wait_ge(dg_sb, BASE + n + 1)
                    ch.link(nc.vector.scalar_tensor_tensor(c[:, u, :], c[:, u, :], (STEP - 1) / 2 / STEP, dg[:, u, :],
                                                           ALU.subtract, ALU.mult))
                    ch.link(nc.vector.tensor_tensor(y[:, :], g0[:, u, :], c[:, u, :], ALU.subtract))
                    ch.link(nc.vector.tensor_scalar(y[:, :], y[:, :], QUANT, ROUND, ALU.mult, ALU.add))
                    ve.wait_ge(up_sb, BASE + n + 1)
                    nc.vector.scalar_tensor_tensor(hs[:, g, f, :], y[:, :], ROUND, up[:, u, :], ALU.subtract,
                                                   ALU.add).then_inc(hs_sb, 1)

                def finish(t):
                    if t:
                        ve.wait_ge(x_done, BASE + t)
                    ve.wait_ge(z_mm, BASE + t + 1)
                    nc.vector.tensor_tensor(z, ps[HB + t % ZB], b2[:, :], ALU.add).then_inc(z_used, 1)
                    ve.wait_ge(z_used, BASE + t + 1)
                    ch.link(nc.vector.tensor_scalar(z, z, ROUND, ROUND, ALU.add, ALU.subtract))
                    nc.vector.scalar_tensor_tensor(x[:, t, :], z, 1.0 / QUANT, x[:, t, :], ALU.mult,
                                                   ALU.add).then_inc(x_done, 1)

                ve.wait_ge(s_b, BASE + 32)
                nc.vector.tensor_scalar(b1q[:, :], b1[:, :], QUANT, None, ALU.mult).then_inc(b_q, 1)
                nc.vector.tensor_scalar(b2[:, :], b2[:, :], QUANT, None, ALU.mult).then_inc(b_q, 1)
                for t in range(TG):
                    ln.vector_stats(ch, t)
                    ln.vector_norm(ve, t)
                round_(0)
                for n in range(N):
                    if n + 1 < N:
                        round_(n + 1)
                    interpolate(n)
                    if n in NORM_AT:
                        ln.vector_stats(ch, TG + NORM_AT.index(n))
                        ln.vector_norm(ve, TG + NORM_AT.index(n))
                    per = FT // TG
                    if n >= FT + 1 and (n - FT) % per == 1 and (n - FT) // per >= 1:
                        finish((n - FT) // per - 1)
                for t in range(TG - 1, NT):
                    finish(t)


def perceiver_kernel(nc, a, out, stages=6):
    ctx = ExitStack()
    with ctx:
        def dram(name, shape, dt=F32):
            return nc.dram_tensor(name, shape, dt, kind="Internal").ap()

        xg_d = dram("routed_x", [ET * P, D])
        yg_d = dram("routed_y", [ET * P, D])
        v_d = dram("scan_v", [B * S, D])
        ba_d = dram("scan_ba", [2, B * HS, S])

        def sb(name, shape, dt=F32):
            return ctx.enter_context(nc.sbuf_tensor(name, shape, dt))

        x = sb("x", [P, NT + 1, D])
        cn = sb("cn", [P, CN_N])
        W0 = sb("W0", [P, 16384])
        PS = ctx.enter_context(nc.psum_tensor("PS", [P, 8, 512], F32))
        ps = [PS[:, i, :] for i in range(8)]
        ident = cn[:, CN_ID:CN_ID + P]
        ones = cn[:, CN_ONE:CN_ONE + P]

        wv0 = W0[:, 0:1024].rearrange("p (k n) -> p k n", k=DK)
        wt0 = W0[:, 1024:1792].rearrange("p (k n) -> p k n", k=CK)
        wqkv = W0[:, 1792:1792 + 6144].rearrange("p (k n) -> p k n", k=DK)
        wq4 = W0[:, 0:4096].rearrange("p (k n) -> p k n", k=DK)
        wk4 = W0[:, 4096:7168].rearrange("p (m n) -> p m n", m=H1 // 2)
        wv4 = W0[:, 7168:10240].rearrange("p (k n) -> p k n", k=CK)
        wo4 = W0[:, 10240:14336].rearrange("p (k n) -> p k n", k=HC // P)
        w16 = W0[:, 0:8192].rearrange("p (k n) -> p k n", k=DK)
        w26 = W0[:, 8192:16384].rearrange("p (k n) -> p k n", k=FF // P)

        fresh = []
        layer_sems = []

        def held(name):
            fresh.append(ctx.enter_context(nc.semaphore(name)))
            return fresh[-1]

        def sem(name, pool_dma=False):
            layer_sems.append(nc.alloc_semaphore(name=name))
            if not pool_dma:
                fresh.append(layer_sems[-1])
            return layer_sems[-1]

        def open_sems():
            with nc.Block() as block:
                for n, part in enumerate((block.gpsimd, block.vector, block.scalar, block.tensor, block.sync)):
                    @part
                    def _(eng, mine=fresh[n::5]):
                        for h in mine:
                            eng.sem_inc(h, BASE)
            fresh.clear()

        def reset_sems():
            with nc.Block() as block:
                @block.gpsimd
                def _(pool):
                    for h in layer_sems:
                        pool.sem_clear(h)
            for h in layer_sems:
                nc.release_semaphore(h)
            layer_sems.clear()

        s_cn, s_x = held("s_cn"), held("s_x")
        s_w12, s_w4, s_w6 = held("s_w12"), held("s_w4"), held("s_w6")

        env = Env()
        env.x, env.cn, env.W0, env.PS, env.ps, env.ident, env.ones = x, cn, W0, PS, ps, ident, ones
        env.out, env.xg_d, env.yg_d, env.v_d, env.ba_d = out, xg_d, yg_d, v_d, ba_d
        env.sem, env.open_sems = sem, open_sems
        env.s_cn, env.s_x, env.s_xg0 = s_cn, s_x, held("s_xg0")
        env.s_w12, env.s_w4, env.s_w6 = s_w12, s_w4, s_w6
        env.wv0, env.wt0, env.wqkv, env.wq4, env.wk4, env.wv4, env.wo4 = wv0, wt0, wqkv, wq4, wk4, wv4, wo4
        env.w16, env.w26 = w16, w26
        cosine_layer(nc, a, env)
        layers = [self_attention_layer, expert_layer, cross_attention_layer, decayed_attention_layer,
                  feed_forward_layer]
        for layer in layers[:stages - 1]:
            if layer is expert_layer:
                with nc.sbuf_tensor("W1", [P, 2 * (DK * 2 * FE + FE // P * D)], F32) as env.W1:
                    layer(nc, a, env)
                reset_sems()
            else:
                if layer is decayed_attention_layer:
                    env.W1 = sb("W1_last", [P, 2 * (DK * 2 * FE + FE // P * D)])
                    env.w5 = env.W1[:, 0:10240].rearrange("p (w k n) -> p w k n", w=5, k=DK)
                layer(nc, a, env)
        if stages < 6:
            s_o = sem("s_o")
            open_sems()
            with nc.Block() as block:
                @block.sync
                def _(sp):
                    sp.dma_start(out, x[:, 0:NT, :]).then_inc(s_o, 16)
                    sp.wait_ge(s_o, BASE + 16)


def arrays_of(i):
    def tiles(w):
        w = np.asarray(w)
        return np.ascontiguousarray(w.reshape(-1, P, w.shape[1]).transpose(1, 0, 2))

    g = {k: np.asarray(v) for k, v in i.items()}
    c = g["ctx_768"]
    w = g["L0_attn_W_qkv"].reshape(H0, 3, DH0, D).transpose(1, 0, 2, 3).reshape(3 * D, D)
    return {
        "consts": constant_table(),
        "x": tiles(g["x"].reshape(B * S, D)),
        "ctxT": np.ascontiguousarray(c.reshape(B, J, CK, P).transpose(0, 3, 2, 1)),
        "ctxN": np.ascontiguousarray(c.reshape(B, J // P, P, C).transpose(0, 2, 1, 3)),
        "wv0": tiles(g["L0_xattn_Wv"].T),
        "wt0": tiles(g["L0_xattn_Wt"].T),
        "bv0": g["L0_xattn_bv"].reshape(1, HX),
        "bt0": np.ascontiguousarray(g["L0_xattn_bt"].reshape(2, P).T),
        "wqkv": tiles(w.T),
        "gate": tiles(g["L0_ffn_w_gate"]),
        "fc": np.ascontiguousarray(g["L0_ffn_c_fc"].reshape(NE, DK, P, 2 * FE).transpose(0, 2, 1, 3)),
        "proj": np.ascontiguousarray(g["L0_ffn_c_proj"].reshape(NE, FE // P, P, D).transpose(0, 2, 1, 3)),
        "wq4": tiles(g["L1_xattn_Wq"]),
        "wk4": tiles(g["L1_xattn_Wk"].T),
        "wv4": tiles(g["L1_xattn_Wv"]),
        "wo4": tiles(g["L1_xattn_Wo"]),
        "bo4": g["L1_xattn_bo"].reshape(1, D),
        "w5": np.ascontiguousarray(np.stack([tiles(g["L1_attn_" + n].T) for n in
                                             ("W_q", "W_k", "W_v", "W_alpha_w", "W_o")], 1)),
        "ba5": g["L1_attn_W_alpha_b"].reshape(1, HS * DHS),
        "w16": tiles(g["L1_ffn_w1"]),
        "w26": tiles(g["L1_ffn_w2"]),
        "b16": np.ascontiguousarray(g["L1_ffn_b1"].reshape(FF // P, P).T),
        "b26": np.ascontiguousarray(np.broadcast_to(g["L1_ffn_b2"].reshape(1, D), (P, D))),
    }


def kernel(**inputs):
    import concourse.bacc as _bacc
    from concourse.bass_utils import run_bass_kernel_spmd as _run

    nc = _bacc.Bacc("TRN2", target_bir_lowering=False, num_devices=1)
    arrays, aps = {}, {}
    for name, w in arrays_of(inputs).items():
        arrays[f"in_{name}"] = np.ascontiguousarray(w)
        aps[name] = nc.dram_tensor(f"in_{name}", w.shape, mybir.dt.from_np(w.dtype), kind="ExternalInput").ap()
    out = nc.dram_tensor("out", (P, NT, D), F32, kind="ExternalOutput").ap()
    perceiver_kernel(nc, aps, out)
    r = _run(nc, [arrays], core_ids=[0])
    return r.results[0]["out"].transpose(1, 0, 2).reshape(B, S, D)
```

```python
from contextlib import ExitStack

import numpy as np

import concourse.bass as bass
from concourse import mybir

F32 = mybir.dt.float32
F32R = mybir.dt.float32r
U32 = mybir.dt.uint32
I32 = mybir.dt.int32
ALU = mybir.AluOpType
ACT = mybir.ActivationFunctionType
AX = mybir.AxisListType

P = 128
B, S, D = 16, 64, 512
J, C = 512, 384
NT = B * S // P
DK = D // P
CK = C // P
HX = 256
H0, DH0 = 16, 32
NE, FE = 8, 768
ET = 2 * B * S // P + NE - 1
H1, DH1 = 16, 64
HC = H1 * DH1
HS, DHS = 8, 64
FF = 2048
LN_EPS = 1e-5
EPS = 1e-8
EPS_BITS = int(np.float32(EPS).view(np.uint32))
SIGN_BIT = 0x80000000
ROUND = 12582912.0
QUANT = 256.0

CN_ID = 0
CN_TRI = CN_ID + P
CN_ONE = CN_TRI + P
CN_SEL = CN_ONE + P
CN_IOTA = CN_SEL + B
CN_TILE = CN_IOTA + NT * NE
CN_MISC = CN_TILE + ET * NE
CN_HALF, CN_MHALF, CN_ROUND, CN_TOP, CN_K0, CN_K1 = range(CN_MISC, CN_MISC + 6)
CN_N = CN_MISC + 6


def constant_table():
    t = np.zeros((P, CN_N), np.float32)
    p = np.arange(P)
    t[:, CN_ID:CN_ID + P] = np.eye(P)
    t[:, CN_TRI:CN_TRI + P] = p[:, None] < p[None, :]
    t[:, CN_ONE:CN_ONE + P] = 1.0
    t[:, CN_SEL:CN_SEL + B] = p[:, None] // HS == np.arange(B)[None, :]
    t[:, CN_IOTA:CN_IOTA + NT * NE] = np.tile(np.arange(NE) - NE, NT)
    t[:, CN_TILE:CN_TILE + ET * NE] = np.repeat(np.arange(ET), NE)
    t[:, CN_HALF] = 0.5
    t[:, CN_MHALF] = -0.5
    t[:, CN_ROUND] = ROUND
    t[:, CN_TOP] = -4.0 * QUANT
    t[:, CN_K0] = -0.25 * ROUND
    t[:, CN_K1] = 0.25 - 0.25 * ROUND
    return t


BASE = 1


class Env:
    pass


class Chain:

    def __init__(self, eng, sem):
        self.eng, self.sem, self.base, self.n = eng, sem, 0, 0

    def turn(self, i, per):
        self.start, self.per = self.n, per
        self.again(i)

    def again(self, i):
        self.base, self.n = i * self.per + self.start, 0

    def link(self, ins):
        ins.then_inc(self.sem, 1)
        self.n += 1
        self.eng.wait_ge(self.sem, BASE + self.base + self.n)


def split_product(nc, out, lhs, rhs, steps, opens=True):
    terms = [(s, m, n) for s in range(steps) for m, n in ((0, 0), (0, 1), (1, 0))]
    for s, m, n in terms:
        mm = nc.tensor.matmul(out, lhs(m, s), rhs(n, s), start=(opens and (s, m, n) == terms[0]), stop=((s, m, n) == terms[-1]))
    return mm


class Norm:

    def __init__(self, nc, e, tag, sbuf, bank, xT):
        self.nc, self.x, self.cn, self.ident = nc, e.x, e.cn, e.ident
        sem = e.sem
        self.st = sbuf(f"st{tag}", [P, 6])
        self.mv = sbuf(f"mv{tag}", [P, 2])
        self.ve = sbuf(f"ve{tag}", [P, 1])
        self.rs = sbuf(f"rs{tag}", [P, 1])
        self.xn = sbuf(f"xn{tag}", [P, D])
        self.bank, self.xT = bank, xT
        self.split = isinstance(xT, list)
        self.var, self.rstd = sem(f"var{tag}"), sem(f"rstd{tag}")
        self.norm, self.turned = sem(f"norm{tag}"), sem(f"turned{tag}")
        if self.split:
            self.xT_hi = sem(f"xT_hi{tag}")
        self.xT_ready, self.seen = sem(f"xT_ready{tag}"), sem(f"seen{tag}")

    def vector_stats(self, ch, n):
        ch.link(self.nc.vector.bn_stats(self.st[:, :], self.x[:, n, :]))
        self.nc.vector.sem_inc(self.seen)
        ch.link(self.nc.vector.bn_aggr(self.mv[:, :], self.st[:, :]))
        self.nc.vector.tensor_scalar(self.ve[:, :], self.mv[:, 1:2], LN_EPS, None,
                                ALU.add).then_inc(self.var, 1)

    def pool(self, eng, n):
        eng.wait_ge(self.var, BASE + n + 1)
        self.nc.gpsimd.tensor_tensor(self.rs[:, :], self.ve[:, :], self.cn[:, CN_MHALF:CN_MHALF + 1],
                                ALU.pow).then_inc(self.rstd, 1)

    def vector_norm(self, eng, n):
        eng.wait_ge(self.rstd, BASE + n + 1)
        eng.wait_ge(self.turned, BASE + n)
        self.nc.vector.tensor_scalar(self.xn[:, :], self.x[:, n, :], self.mv[:, 0:1], self.rs[:, 0:1],
                                ALU.subtract, ALU.mult).then_inc(self.norm, 1)

    def tensor(self, eng, n):
        eng.wait_ge(self.norm, BASE + n + 1)
        eng.wait_ge(self.xT_ready, BASE + n)
        for k in range(DK):
            last = self.nc.tensor.transpose(self.bank[:, k * P:(k + 1) * P],
                                       self.xn[:, k * P:(k + 1) * P], self.ident)
        last.then_inc(self.turned, 1)

    def scalar(self, eng, n, used, count=None):
        eng.wait_ge(self.turned, BASE + n + 1)
        eng.wait_ge(used, BASE + (n if count is None else count))
        whole = self.xT[0] if self.split else self.xT
        self.nc.scalar.activation(whole[:, :, :].rearrange("p k t -> p (k t)"), self.bank[:, :],
                             ACT.Copy).then_inc(self.xT_hi if self.split else self.xT_ready, 1)

    def vector_rest(self, eng, n):
        eng.wait_ge(self.xT_hi, BASE + n + 1)
        hi, lo = (part[:, :, :].rearrange("p k t -> p (k t)") for part in self.xT)
        self.nc.vector.tensor_tensor(lo, self.bank[:, :], hi.bitcast(F32), ALU.subtract).then_inc(self.xT_ready, 1)


def cosine_layer(nc, a, e):
    x, cn, ps, ones, ident, sem = e.x, e.cn, e.ps, e.ones, e.ident, e.sem
    s_cn, s_x, s_w12, s_xg0 = e.s_cn, e.s_x, e.s_w12, e.s_xg0
    wv0, wt0, wqkv, xg_d = e.wv0, e.wt0, e.wqkv, e.xg_d
    with ExitStack() as st:
        def sbuf(name, shape, dt=F32):
            return st.enter_context(nc.sbuf_tensor(name, shape, dt))

        cT = sbuf("cT1", [P, 2, CK, J])
        cs = [sbuf(f"cs1{part}", [P, 2, CK, J], F32R) for part in range(2)]
        ws = [sbuf(f"ws1{part}", [P, CK, HX], F32R) for part in range(2)]
        tT = sbuf("tT1", [P, 2, 2, J])
        sq = sbuf("sq1", [P, 2, 2, J])
        v = sbuf("v1", [P, HX])
        vsq = sbuf("vsq1", [P, HX])
        vT = sbuf("vT1", [P, 2, P])
        vn2 = sbuf("vn2_1", [P, 1])
        vn = sbuf("vn1", [P, 1])
        tn = sbuf("tn1", [P, J])
        den = sbuf("den1", [P, J])
        rden = sbuf("rden1", [P, J])
        cosv = sbuf("cos1", [P, J])
        bv = sbuf("bv1", [1, HX])
        bt = sbuf("bt1", [P, 2])
        xT = sbuf("xT1", [P, DK, P])
        zero = sbuf("zero1", [P, D])
        ln = Norm(nc, e, "1", sbuf, ps[7], xT)
        s_ct = [sem("s_ct1_0"), sem("s_ct1_1")]
        s_b = sem("s_b1")
        v_mm, v_sb, v_sq, v_n = sem("v_mm1"), sem("v_sb1"), sem("v_sq1"), sem("v_n1")
        vt_mm, vt_sb = sem("vt_mm1"), sem("vt_sb1")
        t_mm, t_sb, t_sq = sem("t_mm1"), sem("t_sb1"), sem("t_sq1")
        d_mm, n_mm, tn_sb = sem("d_mm1"), sem("n_mm1"), sem("tn_sb1")
        dots_read = sem("dots_read1")
        c_hi, c_lo, w_hi, w_lo = sem("c_hi1"), sem("c_lo1"), sem("w_hi1"), sem("w_lo1")
        s_w0, s_x2 = sem("s_w0_1"), sem("s_x2_1")
        s_zero = sem("s_zero1")
        dve = sem("dve1")
        psV, psVT, psT, psD, psN = ps[0], ps[1], (ps[2], ps[3]), ps[4], ps[5]

        e.open_sems()
        with nc.Block() as block:
            @block.sync
            def _(sp):
                sp.dma_start(cn[:, :], a["consts"]).then_inc(s_cn, 16)
                sp.dma_start(x[:, 0, :], a["x"][:, 0, :]).then_inc(s_x, 16)
                sp.dma_start(wt0, a["wt0"]).then_inc(s_w0, 16)
                sp.dma_start(wv0, a["wv0"]).then_inc(s_w12, 16)
                sp.dma_start(bv[:, :], a["bv0"]).then_inc(s_b, 16)
                sp.dma_start(bt[:, :], a["bt0"]).then_inc(s_b, 16)
                for u in range(2):
                    sp.dma_start(cT[:, u], a["ctxT"][u]).then_inc(s_ct[u], 16)
                sp.dma_start(x[:, 1:NT, :], a["x"][:, 1:NT, :]).then_inc(s_x2, 16)
                sp.dma_start(wqkv, a["wqkv"]).then_inc(s_w12, 16)
                sp.wait_ge(s_zero, BASE + 1)
                PER = ET // (NT - 1)
                with sp.Fori(0, NT - 1) as i:
                    for u in range(2):
                        sp.wait_ge(c_lo, BASE + 2 * i + u + 1)
                        sp.dma_start(cT[:, u], a["ctxT"][2 * i + 2 + u]).then_inc(s_ct[u], 16)
                    for n in range(PER):
                        sp.dma_start(xg_d[bass.ds((PER * i + n) * P, P), :], zero[:, :]).then_inc(s_xg0, 16)
                for n in range(PER * (NT - 1), ET):
                    sp.dma_start(xg_d[n * P:(n + 1) * P, :], zero[:, :]).then_inc(s_xg0, 16)
                sp.wait_ge(s_xg0, BASE + 16 * ET)

            @block.gpsimd
            def _(pool):
                nc.gpsimd.memset(zero[:, :], 0.0).then_inc(s_zero, 1)
                nc.gpsimd.memset(x[:, NT, :], 0.0)
                pool.wait_ge(s_cn, BASE + 16)
                ln.pool(pool, 0)
                def tile(i, last):
                    if not last:
                        ln.pool(pool, i + 1)
                    pool.wait_ge(v_sq, BASE + i + 1)
                    pool.wait_ge(dots_read, BASE + i)
                    nc.gpsimd.tensor_tensor(vn[:, :], vn2[:, :], cn[:, CN_HALF:CN_HALF + 1],
                                            ALU.pow).then_inc(v_n, 1)

                with pool.Fori(0, NT - 1) as i:
                    tile(i, False)
                tile(NT - 1, True)

            @block.vector
            def _(ve):
                ch = Chain(ve, dve)
                ve.wait_ge(s_x, BASE + 16)
                ln.vector_stats(ch, 0)
                ln.vector_norm(ve, 0)

                def rest(out, whole, first):
                    return nc.vector.tensor_tensor(out, whole, first.bitcast(F32), ALU.subtract)

                def rest_c(i, u):
                    ve.wait_ge(c_hi, BASE + 2 * i + u + 1)
                    rest(cs[1][:, u], cT[:, u], cs[0][:, u]).then_inc(c_lo, 1)

                def tile(i, last):
                    if not last:
                        ln.vector_stats(ch, i + 1)
                    ve.wait_ge(vt_mm, BASE + i + 1)
                    ve.wait_ge(d_mm, BASE + i)
                    nc.vector.tensor_copy(vT[:, :, :].rearrange("p m t -> p (m t)"),
                                          psVT[:, 0:2 * P]).then_inc(vt_sb, 1)
                    if not last:
                        ln.vector_norm(ve, i + 1)
                    if not last:
                        rest_c(i + 1, 0)
                        rest_c(i + 1, 1)
                    ve.wait_ge(v_n, BASE + i + 1)
                    ve.wait_ge(tn_sb, BASE + i + 1)
                    ch.link(nc.vector.tensor_scalar(den[:, :], tn[:, :], vn[:, 0:1], EPS,
                                                    ALU.mult, ALU.max))
                    ch.link(nc.vector.reciprocal(rden[:, :], den[:, :]))
                    ve.wait_ge(d_mm, BASE + i + 1)
                    ch.link(nc.vector.tensor_tensor(cosv[:, :], psD[:, :], rden[:, :], ALU.mult))
                    ve.sem_inc(dots_read, 1)
                    ch.link(nc.vector.tensor_tensor(x[:, i, :], x[:, i, :], cosv[:, :], ALU.add))

                ve.wait_ge(w_hi, BASE + 1)
                rest(ws[1][:, :, :], wt0, ws[0][:, :, :]).then_inc(w_lo, 1)
                rest_c(0, 0)
                rest_c(0, 1)
                ve.wait_ge(s_b, BASE + 32)
                ve.wait_ge(s_x2, BASE + 16)
                with ve.Fori(0, NT - 1) as i:
                    ch.turn(i, 6)
                    tile(i, False)
                    assert ch.n == 6
                ch.again(NT - 1)
                tile(NT - 1, True)

            @block.tensor
            def _(pe):
                pe.wait_ge(s_cn, BASE + 16)
                ln.tensor(pe, 0)
                pe.wait_ge(s_w12, BASE + 16)
                pe.wait_ge(w_lo, BASE + 1)
                pe.wait_ge(s_b, BASE + 32)

                def project(i, u):
                    pe.wait_ge(c_lo, BASE + 2 * i + u + 1)
                    for m in range(2):
                        pe.wait_ge(t_sb, BASE + 4 * i + (1 + m if u else 0))
                        split_product(nc, psT[m][:, :], lambda part, k: ws[part][:, k, m * P:(m + 1) * P],
                                      lambda part, k: cs[part][:, u, k, :], CK).then_inc(t_mm, 1)

                def tile(i, last):
                    pe.wait_ge(ln.xT_ready, BASE + i + 1)
                    pe.wait_ge(v_sb, BASE + i)
                    for k in range(DK):
                        nc.tensor.matmul(psV[:, 0:HX], xT[:, k, :], wv0[:, k, :],
                                         start=(k == 0), stop=False)
                    nc.tensor.matmul(psV[:, 0:HX], ones[0:1, :], bv[0:1, :],
                                     start=False, stop=True).then_inc(v_mm, 1)
                    project(i, 0)
                    pe.wait_ge(v_sb, BASE + i + 1)
                    pe.wait_ge(vt_sb, BASE + i)
                    for m in range(2):
                        tr = nc.tensor.transpose(psVT[:, m * P:(m + 1) * P],
                                                 v[:, m * P:(m + 1) * P], ident)
                    tr.then_inc(vt_mm, 1)
                    project(i, 1)
                    if not last:
                        ln.tensor(pe, i + 1)
                    pe.wait_ge(vt_sb, BASE + i + 1)
                    pe.wait_ge(dots_read, BASE + i)
                    pe.wait_ge(tn_sb, BASE + i)
                    for u in range(2):
                        rows = slice(u * S, (u + 1) * S)
                        pe.wait_ge(t_sb, BASE + 4 * i + 2 * u + 2)
                        pe.wait_ge(t_sq, BASE + 4 * i + 2 * u + 2)
                        for m in range(2):
                            mn = nc.tensor.matmul(psN[rows, :], ones[:, 0:S], sq[:, u, m, :],
                                                  start=(m == 0), stop=(m == 1))
                        if u:
                            mn.then_inc(n_mm, 1)
                        for m in range(2):
                            mm = nc.tensor.matmul(psD[rows, :], vT[:, m, rows], tT[:, u, m, :],
                                                  start=(m == 0), stop=(m == 1))
                    mm.then_inc(d_mm, 1)

                with pe.Fori(0, NT - 1) as i:
                    tile(i, False)
                tile(NT - 1, True)

            @block.scalar
            def _(act):
                act.wait_ge(s_cn, BASE + 16)
                act.wait_ge(s_b, BASE + 32)
                ln.scalar(act, 0, v_mm)

                def first_c(i, u):
                    act.wait_ge(s_ct[u], BASE + 16 * i + 16)
                    nc.scalar.activation(cs[0][:, u], cT[:, u], ACT.Copy).then_inc(c_hi, 1)

                def tile(i, last):
                    act.wait_ge(v_mm, BASE + i + 1)
                    act.wait_ge(vt_mm, BASE + i)
                    act.wait_ge(v_sq, BASE + i)
                    nc.scalar.activation(v[:, :], psV[:, 0:HX], ACT.Copy).then_inc(v_sb, 1)
                    act.wait_ge(v_sb, BASE + i + 1)
                    act.wait_ge(v_n, BASE + i)
                    nc.scalar.activation(vsq[:, :], v[:, :], ACT.Square,
                                         accum_out=vn2[:, :]).then_inc(v_sq, 1)

                    def project_out(u):
                        for m in range(2):
                            act.wait_ge(t_mm, BASE + 4 * i + 2 * u + m + 1)
                            act.wait_ge(d_mm, BASE + i)
                            nc.scalar.activation(tT[:, u, m, :], psT[m][:, :], ACT.Identity,
                                                 bias=bt[:, m:m + 1]).then_inc(t_sb, 1)
                        for m in range(2):
                            act.wait_ge(t_sb, BASE + 4 * i + 2 * u + m + 1)
                            act.wait_ge(n_mm, BASE + i)
                            nc.scalar.activation(sq[:, u, m, :], tT[:, u, m, :], ACT.Square).then_inc(t_sq, 1)
                        if not last:
                            first_c(i + 1, u)

                    project_out(0)
                    project_out(1)
                    if not last:
                        ln.scalar(act, i + 1, v_mm)
                    act.wait_ge(n_mm, BASE + i + 1)
                    act.wait_ge(dots_read, BASE + i)
                    nc.scalar.activation(tn[:, :], psN[:, :], ACT.Sqrt).then_inc(tn_sb, 1)

                act.wait_ge(s_w0, BASE + 16)
                nc.scalar.activation(ws[0][:, :, :], wt0, ACT.Copy).then_inc(w_hi, 1)
                first_c(0, 0)
                first_c(0, 1)
                with act.Fori(0, NT - 1) as i:
                    tile(i, False)
                tile(NT - 1, True)


def self_attention_layer(nc, a, e):
    x, cn, ps, PS, ident, sem, wqkv = e.x, e.cn, e.ps, e.PS, e.ident, e.sem, e.wqkv
    SCALE = float(np.float32(1.0) / np.sqrt(np.float32(DH0)))
    HH = P // DH0
    with ExitStack() as st:
        def sbuf(name, shape, dt=F32):
            return st.enter_context(nc.sbuf_tensor(name, shape, dt))

        xT = [sbuf(f"xT2{part}", [P, DK, P], F32R) for part in range(2)]
        ws = [[sbuf(f"ws2{w}{part}", [P, DK, D], F32R) for part in range(2)] for w in range(3)]
        q, k, v = sbuf("q2", [P, D]), sbuf("k2", [P, D]), sbuf("v2", [P, D])
        qT, kT = sbuf("qT2", [P, DK, P]), sbuf("kT2", [P, DK, P])
        mx = sbuf("mx2", [P, H0])
        sc = sbuf("sc2", [P, H0, S])
        pf = sbuf("pf2", [P, H0, P])
        pT = sbuf("pT2", [P, H0, P])
        sums, rs = sbuf("sums2", [P, H0]), sbuf("rsum2", [P, H0])
        o = sbuf("o2", [P, D])
        ln = Norm(nc, e, "2", sbuf, ps[7], xT)
        q_mm, k_mm, v_mm = sem("q_mm2"), sem("k_mm2"), sem("v_mm2")
        q_sb, k_sb, v_sb = sem("q_sb2"), sem("k_sb2"), sem("v_sb2")
        qT_mm, kT_mm, qT_sb, kT_sb = sem("qT_mm2"), sem("kT_mm2"), sem("qT_sb2"), sem("kT_sb2")
        s_mm, sub_done, e_sb, summed = sem("s_mm2"), sem("sub_done2"), sem("e_sb2"), sem("summed2")
        pt_mm, pt_act, pt_dve = sem("pt_mm2"), sem("pt_act2"), sem("pt_dve2")
        w_hi, w_lo = sem("w_hi2"), sem("w_lo2")
        o_mm, o_read, zeroed, dve = sem("o_mm2"), sem("o_read2"), sem("zeroed2"), sem("dve2")
        TURN = (0, 2, 1, 3)
        S_BANKS = PS[:, 3:3 + HH, 0:DK * S]

        e.open_sems()
        with nc.Block() as block:
            @block.gpsimd
            def _(pool):
                nc.gpsimd.memset(pf[:, :, :], 0.0).then_inc(zeroed, 1)
                ln.pool(pool, 0)
                ln.pool(pool, 1)
                with pool.Fori(0, NT - 1) as i:
                    ln.pool(pool, i + 2)

            @block.tensor
            def _(pe):
                def project(n):
                    pe.wait_ge(ln.xT_ready, BASE + n + 1)
                    for w, done, out_read in ((0, q_mm, qT_sb), (1, k_mm, kT_sb), (2, v_mm, v_sb)):
                        pe.wait_ge(out_read, BASE + n)
                        if isinstance(n, int):
                            pe.wait_ge(w_lo, BASE + w + 1)
                        split_product(nc, ps[w], lambda part, kk: xT[part][:, kk, :],
                                      lambda part, kk: ws[w][part][:, kk, :], DK).then_inc(done, 1)

                ln.tensor(pe, 0)
                project(0)

                def tile(i, last):
                    for src, bank, ready, done in ((q, 0, q_sb, qT_mm), (k, 1, k_sb, kT_mm)):
                        pe.wait_ge(ready, BASE + i + 1)
                        for m in range(DK):
                            tr = nc.tensor.transpose(ps[bank][:, m * P:(m + 1) * P],
                                                     src[:, m * P:(m + 1) * P], ident)
                        tr.then_inc(done, 1)
                    pe.wait_ge(o_read, BASE + i)
                    if not last:
                        ln.tensor(pe, i + 1)
                    pe.wait_ge(qT_sb, BASE + i + 1)
                    pe.wait_ge(kT_sb, BASE + i + 1)
                    pe.wait_ge(pt_act, BASE + 2 * i)
                    pe.wait_ge(pt_dve, BASE + 2 * i)
                    for m in range(DK):
                        for hh in range(HH):
                            part = slice(hh * DH0, (hh + 1) * DH0)
                            for u in range(2):
                                tok = slice(u * S, (u + 1) * S)
                                mm = nc.tensor.matmul(PS[tok, 3 + hh, m * S:(m + 1) * S],
                                                      qT[part, m, tok], kT[part, m, tok],
                                                      start=True, stop=True)
                    mm.then_inc(s_mm, 1)
                    if not last:
                        project(i + 1)
                    pe.wait_ge(e_sb, BASE + 2 * i + 2)
                    for g in TURN:
                        for m in range(DK):
                            tr = nc.tensor.transpose(ps[3 + g][:, m * P:(m + 1) * P],
                                                     pf[:, g * DK + m, :], ident)
                        tr.then_inc(pt_mm, 1)
                    pe.wait_ge(v_sb, BASE + i + 1)
                    for hh in TURN:
                        pe.wait_ge(pt_act if hh < 2 else pt_dve, BASE + 2 * i + hh % 2 + 1)
                        for m in range(DK):
                            h = m * HH + hh
                            mm = nc.tensor.matmul(ps[7][:, h * DH0:(h + 1) * DH0], pT[:, hh * DK + m, :],
                                                  v[:, h * DH0:(h + 1) * DH0], start=True, stop=True)
                    mm.then_inc(o_mm, 1)

                with pe.Fori(0, NT - 1) as i:
                    tile(i, False)
                tile(NT - 1, True)

            @block.scalar
            def _(act):
                def take(n):
                    for dst, bank, done, turned, ready in ((q, 0, q_mm, qT_mm, q_sb),
                                                           (k, 1, k_mm, kT_mm, k_sb)):
                        act.wait_ge(done, BASE + n + 1)
                        act.wait_ge(turned, BASE + n)
                        nc.scalar.activation(dst[:, :], ps[bank], ACT.Copy).then_inc(ready, 1)

                ln.scalar(act, 0, v_mm)
                act.wait_ge(e.s_w12, BASE + 32)
                for w in range(3):
                    nc.scalar.activation(ws[w][0][:, :, :], wqkv[:, :, w * D:(w + 1) * D], ACT.Copy).then_inc(w_hi, 1)
                take(0)
                act.wait_ge(zeroed, BASE + 1)

                def tile(i, last):
                    act.wait_ge(qT_mm, BASE + i + 1)
                    act.wait_ge(s_mm, BASE + i)
                    nc.scalar.activation(qT[:, :, :].rearrange("p m t -> p (m t)"), ps[0],
                                         ACT.Copy).then_inc(qT_sb, 1)
                    if not last:
                        ln.scalar(act, i + 1, v_mm)
                    act.wait_ge(sub_done, BASE + i + 1)
                    act.wait_ge(pt_mm, BASE + 4 * i)
                    act.wait_ge(summed, BASE + i)
                    for u in range(2):
                        tok = slice(u * S, (u + 1) * S)
                        nc.scalar.activation(pf[tok, :, tok], sc[tok, :, :], ACT.Exp,
                                             scale=SCALE).then_inc(e_sb, 1)
                    if not last:
                        take(i + 1)
                    for g in range(2):
                        act.wait_ge(pt_mm, BASE + 4 * i + TURN.index(g) + 1)
                        act.wait_ge(o_mm, BASE + i)
                        nc.scalar.activation(pT[:, g * DK:(g + 1) * DK, :].rearrange("p m t -> p (m t)"),
                                             ps[3 + g], ACT.Copy).then_inc(pt_act, 1)

                with act.Fori(0, NT - 1) as i:
                    tile(i, False)
                tile(NT - 1, True)

            @block.vector
            def _(ve):
                ch = Chain(ve, dve)
                ln.vector_stats(ch, 0)
                ln.vector_norm(ve, 0)
                ln.vector_rest(ve, 0)
                for w in range(3):
                    ve.wait_ge(w_hi, BASE + w + 1)
                    nc.vector.tensor_tensor(ws[w][1][:, :, :], wqkv[:, :, w * D:(w + 1) * D],
                                            ws[w][0][:, :, :].bitcast(F32), ALU.subtract).then_inc(w_lo, 1)

                def take_v(n):
                    ve.wait_ge(v_mm, BASE + n + 1)
                    ve.wait_ge(o_mm, BASE + n)
                    nc.vector.tensor_copy(v[:, :], ps[2]).then_inc(v_sb, 1)

                take_v(0)
                ln.vector_stats(ch, 1)
                ln.vector_norm(ve, 1)

                def tile(i, last):
                    ve.wait_ge(kT_mm, BASE + i + 1)
                    ve.wait_ge(s_mm, BASE + i)
                    nc.vector.tensor_copy(kT[:, :, :].rearrange("p m t -> p (m t)"),
                                          ps[1]).then_inc(kT_sb, 1)
                    if not last:
                        ln.vector_rest(ve, i + 1)
                    ve.wait_ge(s_mm, BASE + i + 1)
                    s4 = S_BANKS.rearrange("p g (m s) -> p g m s", m=DK)
                    ch.link(nc.vector.tensor_reduce(mx[:, :].rearrange("p (g m) -> p g m", g=HH), s4,
                                                    AX.X, ALU.max))
                    ve.wait_ge(e_sb, BASE + 2 * i)
                    for g in range(HH):
                        part = sc[:, g * DK:(g + 1) * DK, :]
                        ins = nc.vector.tensor_tensor(part, s4[:, g],
                                                      mx[:, g * DK:(g + 1) * DK].unsqueeze(2).to_broadcast([P, DK, S]),
                                                      ALU.subtract)
                    ins.then_inc(sub_done, 1)
                    ve.wait_ge(e_sb, BASE + 2 * i + 2)
                    for u in range(2):
                        tok = slice(u * S, (u + 1) * S)
                        ins = nc.vector.tensor_reduce(sums[tok, :], pf[tok, :, tok], AX.X, ALU.add)
                        if u == 0:
                            ins.then_inc(dve, 1)
                            ch.n += 1
                    ch.link(ins)
                    ve.sem_inc(summed, 1)
                    ch.link(nc.vector.reciprocal(rs[:, :], sums[:, :]))
                    if not last:
                        ln.vector_stats(ch, i + 2)
                        ln.vector_norm(ve, i + 2)
                    for g in range(2, HH):
                        ve.wait_ge(pt_mm, BASE + 4 * i + TURN.index(g) + 1)
                        ve.wait_ge(o_mm, BASE + i)
                        nc.vector.tensor_copy(pT[:, g * DK:(g + 1) * DK, :].rearrange("p m t -> p (m t)"),
                                              ps[3 + g]).then_inc(pt_dve, 1)
                    ve.wait_ge(o_mm, BASE + i + 1)
                    r = rs[:, :].rearrange("p (hh m) -> p m hh", hh=HH).unsqueeze(3)
                    ch.link(nc.vector.tensor_tensor(
                        o[:, :].rearrange("p (m hh d) -> p m hh d", m=DK, hh=HH),
                        ps[7].rearrange("p (m hh d) -> p m hh d", m=DK, hh=HH),
                        r.to_broadcast([P, DK, HH, DH0]), ALU.mult))
                    ve.sem_inc(o_read, 1)
                    nc.vector.tensor_tensor(x[:, i, :], x[:, i, :], o[:, :], ALU.add)
                    if not last:
                        take_v(i + 1)

                with ve.Fori(0, NT - 1) as i:
                    ch.turn(i, 7)
                    tile(i, False)
                    assert ch.n == 7, ch.n
                ch.again(NT - 1)
                tile(NT - 1, True)


def expert_layer(nc, a, e):
    x, cn, ps, ones, ident, sem, W1 = e.x, e.cn, e.ps, e.ones, e.ident, e.sem, e.W1
    xg_d, yg_d = e.xg_d, e.yg_d
    tri = cn[:, CN_TRI:CN_TRI + P]
    iota = cn[:, CN_IOTA:CN_IOTA + NT * NE].rearrange("p (t e) -> p t e", t=NT)
    FK = FE // P
    HFE = FE // 2
    NFC = DK * 2 * FE
    with ExitStack() as st:
        def sbuf(name, shape, dt=F32):
            return st.enter_context(nc.sbuf_tensor(name, shape, dt))

        xn = sbuf("xnall3", [P, NT, D])
        slot = sbuf("slot3", [P, NT, 2], U32)
        top = sbuf("top3", [P, NT, 2])
        owner = sbuf("owner3", [1, ET], I32)
        s_slot, s_owner = sem("s_slot3"), sem("s_owner3")
        s_scat = sem("s_scat3", pool_dma=True)

        fc = [W1[:, u * 9216:u * 9216 + NFC].rearrange("p (k n) -> p k n", k=DK) for u in range(2)]
        pj = [W1[:, u * 9216 + NFC:(u + 1) * 9216].rearrange("p (k n) -> p k n", k=FK) for u in range(2)]
        s_fc, s_pj = [sem("s_fc3_0"), sem("s_fc3_1")], [sem("s_pj3_0"), sem("s_pj3_1")]
        xg_in, y_out = [sem("xg_in3_0"), sem("xg_in3_1")], [sem("y_out3_0"), sem("y_out3_1")]
        tr_mm, xgT_sb, a_mm, gl_mm = sem("tr_mm3"), sem("xgT_sb3"), sem("a_mm3"), sem("gl_mm3")
        silu_sb, hid_sb, hT_mm, hT_sb = sem("silu_sb3"), sem("hid_sb3"), sem("hT_mm3"), sem("hT_sb3")
        y_mm, y_sb = sem("y_mm3"), sem("y_sb3")
        s_yb = [sem(f"s_yb3_{n}", pool_dma=True) for n in range(NT // 2)]
        added, half = sem("added3"), sem("half3")

        def load_fc(sp, u, own):
            sp.dma_start(fc[u], a["fc"][bass.ds(own, 1)].rearrange("o p k n -> (o p) k n")).then_inc(s_fc[u], 16)

        def load_pj(sp, u, own):
            sp.dma_start(pj[u], a["proj"][bass.ds(own, 1)].rearrange("o p k n -> (o p) k n")).then_inc(s_pj[u], 16)

        with ExitStack() as rt:
            def rbuf(name, shape, dt=F32):
                return rt.enter_context(nc.sbuf_tensor(name, shape, dt))

            xT = rbuf("xT3", [P, DK, P])
            gate = rbuf("gate3", [P, DK, NE])
            ln = Norm(nc, e, "3", rbuf, ps[7], xT)
            TE = [P, NT, NE]
            logit, prob, prob2 = rbuf("logit3", TE), rbuf("prob3", TE), rbuf("prob23", TE)
            eq, cand = rbuf("eq3", TE), rbuf("cand3", TE)
            oh = [rbuf("oh13", TE), rbuf("oh23", TE)]
            both, before, place, pick = rbuf("both3", TE), rbuf("before3", TE), rbuf("place3", TE), rbuf("pick3", TE)
            r8, first = rbuf("r83", [P, NT]), rbuf("first3", [P, NT])
            total, tiles, ends, starts = (rbuf(n, [P, NE]) for n in ("total3", "tiles3", "ends3", "starts3"))
            slotf = rbuf("slotf3", [P, NT])
            under = rbuf("under3", [1, ET, NE])
            ownf = rbuf("ownf3", [1, ET])
            s_gate, g_mm, kept = sem("s_gate3"), sem("g_mm3"), sem("kept3")
            s_max, s_exp, s_cnt, s_pos = sem("s_max3"), sem("s_exp3"), sem("s_cnt3"), sem("s_pos3")
            dve = sem("dve3")

            def wide(ap, shape=TE):
                return ap.unsqueeze(2).to_broadcast(shape)

            e.open_sems()
            with nc.Block() as block:
                @block.sync
                def _(sp):
                    sp.dma_start(gate[:, :, :], a["gate"]).then_inc(s_gate, 16)
                    for dst, name in ((e.wq4, "wq4"), (e.wk4, "wk4"), (e.wv4, "wv4"), (e.wo4, "wo4")):
                        sp.dma_start(dst, a[name]).then_inc(e.s_w4, 16)
                    sp.wait_ge(s_owner, BASE + 1)
                    load_fc(sp, 0, sp.value_load(owner[0:1, 0:1], min_val=0, max_val=NE - 1))

                @block.gpsimd
                def _(pool):
                    ln.pool(pool, 0)
                    with pool.Fori(0, NT) as i:
                        pool.wait_ge(ln.norm, BASE + i + 1)
                        nc.gpsimd.tensor_copy(xn[:, i, :], ln.xn[:, :]).then_inc(kept, 1)
                        ln.pool(pool, i + 1)
                    pool.wait_ge(kept, BASE + NT)
                    pool.wait_ge(e.s_xg0, BASE + 16 * ET)
                    pool.wait_ge(s_slot, BASE + 2)
                    for t in range(NT):
                        for c in range(2):
                            nc.gpsimd.indirect_dma_start(
                                out=xg_d, out_offset=bass.IndirectOffsetOnAxis(slot[:, t, c:c + 1], axis=0),
                                in_=xn[:, t, :], in_offset=None).then_inc(s_scat, 16)
                    pool.wait_ge(s_scat, 16 * 2 * NT)

                @block.tensor
                def _(pe):
                    ln.tensor(pe, 0)
                    pe.wait_ge(s_gate, BASE + 16)
                    with pe.Fori(0, NT) as i:
                        pe.wait_ge(ln.xT_ready, BASE + i + 1)
                        for k in range(DK):
                            mm = nc.tensor.matmul(ps[0][:, bass.ds(i * NE, NE)], xT[:, k, :], gate[:, k, :],
                                                  start=(k == 0), stop=(k == DK - 1))
                        mm.then_inc(g_mm, 1)
                        ln.tensor(pe, i + 1)
                    pe.wait_ge(s_cnt, BASE + 1)
                    nc.tensor.matmul(ps[1][:, 0:NE], ones, total[:, :], start=True, stop=True)
                    nc.tensor.matmul(ps[2][:, 0:NT * NE], tri, both[:, :, :].rearrange("p t e -> p (t e)"),
                                     start=True, stop=False)
                    nc.tensor.matmul(ps[2][:, 0:NT * NE], ones, before[:, :, :].rearrange("p t e -> p (t e)"),
                                     start=False, stop=True).then_inc(s_pos, 1)

                @block.scalar
                def _(act):
                    ln.scalar(act, 0, g_mm)
                    with act.Fori(0, NT) as i:
                        ln.scalar(act, i + 1, g_mm)
                    act.wait_ge(s_max, BASE + 1)
                    nc.scalar.activation(prob[:, :, :], logit[:, :, :], ACT.Exp).then_inc(s_exp, 1)

                @block.vector
                def _(ve):
                    ch = Chain(ve, dve)
                    ln.vector_stats(ch, 0)
                    ln.vector_norm(ve, 0)
                    with ve.Fori(0, NT) as i:
                        ch.turn(i, 2)
                        ln.vector_stats(ch, i + 1)
                        ve.wait_ge(kept, BASE + i + 1)
                        ln.vector_norm(ve, i + 1)
                    ch.base, ch.n = 2 + 2 * NT, 0
                    ve.wait_ge(g_mm, BASE + NT)
                    lg = ps[0][:, 0:NT * NE].rearrange("p (t e) -> p t e", t=NT)
                    ch.link(nc.vector.tensor_reduce(r8[:, :], lg, AX.X, ALU.max))
                    nc.vector.tensor_tensor(logit[:, :, :], lg, wide(r8[:, :]), ALU.subtract).then_inc(s_max, 1)
                    ve.wait_ge(s_exp, BASE + 1)
                    ch.link(nc.vector.tensor_reduce(r8[:, :], prob[:, :, :], AX.X, ALU.add))
                    ch.link(nc.vector.reciprocal(first[:, :], r8[:, :]))
                    ch.link(nc.vector.tensor_tensor(prob[:, :, :], prob[:, :, :], wide(first[:, :]), ALU.mult))
                    for c, p in ((0, prob), (1, prob2)):
                        ch.link(nc.vector.tensor_reduce(top[:, :, c], p[:, :, :], AX.X, ALU.max))
                        ch.link(nc.vector.tensor_tensor(eq[:, :, :], p[:, :, :], wide(top[:, :, c]), ALU.is_equal))
                        ch.link(nc.vector.tensor_tensor(cand[:, :, :], eq[:, :, :], iota, ALU.mult))
                        ch.link(nc.vector.tensor_reduce(first[:, :], cand[:, :, :], AX.X, ALU.min))
                        ch.link(nc.vector.tensor_tensor(oh[c][:, :, :], iota, wide(first[:, :]), ALU.is_equal))
                        if c == 0:
                            ch.link(nc.vector.scalar_tensor_tensor(prob2[:, :, :], oh[0][:, :, :], -2.0,
                                                                   prob[:, :, :], ALU.mult, ALU.add))
                    ch.link(nc.vector.tensor_tensor(both[:, :, :], oh[0][:, :, :], oh[1][:, :, :], ALU.add))
                    ch.link(nc.vector.memset(before[:, 0, :], 0.0))
                    for t in range(1, NT):
                        ch.link(nc.vector.tensor_tensor(before[:, t, :], before[:, t - 1, :], both[:, t - 1, :],
                                                        ALU.add))
                    nc.vector.tensor_tensor(total[:, :], before[:, NT - 1, :], both[:, NT - 1, :],
                                            ALU.add).then_inc(s_cnt, 1)
                    ve.wait_ge(s_pos, BASE + 1)
                    ch.link(nc.vector.tensor_scalar(tiles[:, :], ps[1][:, 0:NE], (P - 1) / 2.0, 1.0 / P,
                                                    ALU.add, ALU.mult))
                    ch.link(nc.vector.tensor_scalar(tiles[:, :], tiles[:, :], ROUND, ROUND, ALU.add, ALU.subtract))
                    ch.link(nc.vector.tensor_tensor_scan(ends[:, :], ones[:, 0:NE], tiles[:, :], 0.0,
                                                         ALU.mult, ALU.add))
                    ch.link(nc.vector.tensor_tensor(starts[:, :], ends[:, :], tiles[:, :], ALU.subtract))
                    ch.link(nc.vector.tensor_scalar(starts[:, :], starts[:, :], float(P), None, ALU.mult))
                    ch.link(nc.vector.tensor_tensor(
                        under[:, :, :], ends[0:1, :].unsqueeze(1).to_broadcast([1, ET, NE]),
                        cn[0:1, CN_TILE:CN_TILE + ET * NE].rearrange("p (j e) -> p j e", j=ET), ALU.is_le))
                    ch.link(nc.vector.tensor_reduce(ownf[:, :], under[:, :, :], AX.X, ALU.add))
                    nc.vector.tensor_scalar(owner[:, :], ownf[:, :], float(NE - 1), None, ALU.min).then_inc(s_owner, 1)
                    ch.link(nc.vector.tensor_tensor(
                        place[:, :, :], ps[2][:, 0:NT * NE].rearrange("p (t e) -> p t e", t=NT),
                        starts[:, :].unsqueeze(1).to_broadcast(TE), ALU.add))
                    for c in range(2):
                        ch.link(nc.vector.tensor_tensor(pick[:, :, :], place[:, :, :], oh[c][:, :, :], ALU.mult))
                        ch.link(nc.vector.tensor_reduce(slotf[:, :], pick[:, :, :], AX.X, ALU.add))
                        nc.vector.tensor_copy(slot[:, :, c], slotf[:, :]).then_inc(s_slot, 1)

        xg = sbuf("xg3", [P, 2, D])
        xgT = sbuf("xgT3", [P, DK, P])
        gated, hid = sbuf("gated3", [P, FE]), sbuf("hid3", [P, FE])
        hT = sbuf("hT3", [P, FK, P])
        y = sbuf("y3", [P, 2, D])
        YB = NT // 2
        yb = xn
        TURNS = (ET - 3) // 2

        def steps(eng, step):
            step(0, 0, 0)
            step(1, 1, 0)
            with eng.Fori(0, TURNS) as i:
                step(2 * i + 2, 0, i + 1)
                step(2 * i + 3, 1, i + 1)
            step(ET - 1, 0, TURNS + 1)

        with nc.Block() as block:
            @block.sync
            def _(sp):
                def step(s, u, pair):
                    first = isinstance(s, int) and s < 2
                    own = sp.value_load(owner[0:1, bass.ds(s, 1)], min_val=0, max_val=NE - 1)
                    if not first:
                        sp.wait_ge(tr_mm, BASE + s - 1)
                    sp.dma_start(xg[:, u, :], xg_d[bass.ds(s * P, P), :]).then_inc(xg_in[u], 16)
                    if not first:
                        sp.wait_ge(gl_mm, BASE + s - 1)
                    if not (isinstance(s, int) and s == 0):
                        load_fc(sp, u, own)
                    if not first:
                        sp.wait_ge(y_mm, BASE + s - 1)
                    load_pj(sp, u, own)
                    if not first:
                        store(s - 2, u)

                def store(s, u):
                    sp.wait_ge(y_sb, BASE + s + 1)
                    sp.dma_start(yg_d[bass.ds(s * P, P), :], y[:, u, :]).then_inc(y_out[u], 16)

                steps(sp, step)
                store(ET - 2, 1)
                store(ET - 1, 0)
                for u in range(2):
                    sp.wait_ge(y_out[u], BASE + 16 * ((ET + 1 - u) // 2))

            @block.tensor
            def _(pe):
                def out_proj(s, u, pair):
                    pe.wait_ge(hid_sb, BASE + s + 1)
                    pe.wait_ge(hT_sb, BASE + 2 * s)
                    for g in range(2):
                        for f in range(FK // 2):
                            tr = nc.tensor.transpose(ps[5 + g][:, f * P:(f + 1) * P],
                                                     hid[:, (g * FK // 2 + f) * P:(g * FK // 2 + f + 1) * P], ident)
                        tr.then_inc(hT_mm, 1)
                    pe.wait_ge(s_pj[u], BASE + 16 * pair + 16)
                    pe.wait_ge(y_sb, BASE + s)
                    for f in range(FK):
                        if f % (FK // 2) == 0:
                            pe.wait_ge(hT_sb, BASE + 2 * s + 1 + f // (FK // 2))
                        mm = nc.tensor.matmul(ps[7], hT[:, f, :], pj[u][:, f, :], start=(f == 0), stop=(f == FK - 1))
                    mm.then_inc(y_mm, 1)

                def step(s, u, pair):
                    pe.wait_ge(xg_in[u], BASE + 16 * pair + 16)
                    pe.wait_ge(xgT_sb, BASE + s)
                    for k in range(DK):
                        tr = nc.tensor.transpose(ps[4][:, k * P:(k + 1) * P], xg[:, u, k * P:(k + 1) * P], ident)
                    tr.then_inc(tr_mm, 1)
                    if not (isinstance(s, int) and s < 2):
                        out_proj(s - 2, u, pair - 1)
                    pe.wait_ge(xgT_sb, BASE + s + 1)
                    pe.wait_ge(s_fc[u], BASE + 16 * pair + 16)
                    for c in range(4):
                        pe.wait_ge(silu_sb if c < 2 else hid_sb, BASE + s)
                        for k in range(DK):
                            mm = nc.tensor.matmul(ps[c][:, 0:HFE], xgT[:, k, :], fc[u][:, k, c * HFE:(c + 1) * HFE],
                                                  start=(k == 0), stop=(k == DK - 1))
                        if c == 1:
                            mm.then_inc(a_mm, 1)
                    mm.then_inc(gl_mm, 1)

                steps(pe, step)
                out_proj(ET - 2, 1, (ET - 2) // 2)
                out_proj(ET - 1, 0, (ET - 1) // 2)

            @block.scalar
            def _(act):
                def hidden_out(s):
                    act.wait_ge(y_mm, BASE + s)
                    for g in range(2):
                        act.wait_ge(hT_mm, BASE + 2 * s + g + 1)
                        n = FK // 2
                        nc.scalar.activation(hT[:, g * n:(g + 1) * n, :].rearrange("p f t -> p (f t)"),
                                             ps[5 + g][:, 0:n * P], ACT.Copy).then_inc(hT_sb, 1)

                def step(s, u, pair):
                    act.wait_ge(tr_mm, BASE + s + 1)
                    act.wait_ge(gl_mm, BASE + s)
                    nc.scalar.activation(xgT[:, :, :].rearrange("p k t -> p (k t)"), ps[4],
                                         ACT.Copy).then_inc(xgT_sb, 1)
                    if not (isinstance(s, int) and s < 2):
                        hidden_out(s - 2)
                    act.wait_ge(a_mm, BASE + s + 1)
                    act.wait_ge(hid_sb, BASE + s)
                    for c in range(2):
                        ins = nc.scalar.activation(gated[:, c * HFE:(c + 1) * HFE], ps[c][:, 0:HFE], ACT.Silu)
                    ins.then_inc(silu_sb, 1)

                steps(act, step)
                hidden_out(ET - 2)
                hidden_out(ET - 1)

            @block.vector
            def _(ve):
                def y_take(s, u, pair):
                    ve.wait_ge(y_mm, BASE + s + 1)
                    ve.wait_ge(y_out[u], BASE + 16 * pair)
                    nc.vector.tensor_copy(y[:, u, :], ps[7]).then_inc(y_sb, 1)

                def step(s, u, pair):
                    if not (isinstance(s, int) and s < 2):
                        y_take(s - 2, u, pair - 1)
                    ve.wait_ge(silu_sb, BASE + s + 1)
                    ve.wait_ge(gl_mm, BASE + s + 1)
                    ve.wait_ge(hT_mm, BASE + 2 * s)
                    for c in range(2):
                        ins = nc.vector.tensor_tensor(hid[:, c * HFE:(c + 1) * HFE], gated[:, c * HFE:(c + 1) * HFE],
                                                      ps[2 + c][:, 0:HFE], ALU.mult)
                    ins.then_inc(hid_sb, 1)

                steps(ve, step)
                y_take(ET - 2, 1, (ET - 2) // 2)
                y_take(ET - 1, 0, (ET - 1) // 2)
                for t in range(NT):
                    ve.wait_ge(s_yb[t % YB], 32 * (t // YB + 1))
                    for c in range(2):
                        ins = nc.vector.scalar_tensor_tensor(x[:, t, :], yb[:, t % YB * 2 + c, :], top[:, t, c:c + 1],
                                                             x[:, t, :], ALU.mult, ALU.add)
                        if c == 0:
                            ins.then_inc(half, 1)
                            ve.wait_ge(half, BASE + t + 1)
                    ins.then_inc(added, 1)

            @block.gpsimd
            def _(pool):
                for u in range(2):
                    pool.wait_ge(y_out[u], BASE + 16 * ((ET + 1 - u) // 2))
                for t in range(NT):
                    if t >= YB:
                        pool.wait_ge(added, BASE + t - YB + 1)
                    for c in range(2):
                        nc.gpsimd.indirect_dma_start(
                            out=yb[:, t % YB * 2 + c, :], out_offset=None, in_=yg_d,
                            in_offset=bass.IndirectOffsetOnAxis(slot[:, t, c:c + 1], axis=0)).then_inc(s_yb[t % YB], 16)


def cross_attention_layer(nc, a, e):
    x, cn, ps, ones, ident, sem, W0 = e.x, e.cn, e.ps, e.ones, e.ident, e.sem, e.W0
    wq4, wk4, wv4, wo4 = e.wq4, e.wk4, e.wv4, e.wo4
    MK = HC // P
    PAIRS = 2 * MK
    JK = J // P
    SCALE = DH1 ** -0.5
    BANKS = 3
    U_U, U_Q, U_O, U_QP, USES = (0, 3, 6, 11), 9, 14, 16, 30
    PRE = 15
    SPLIT_T = {3: [(1, 0)], 4: [(1, 1)], 5: [(1, 2)]}
    SPLIT_N = {0: [(0, 0)], 1: [(0, 1)], 2: [(0, 2)], 3: [(0, 3)], 11: [(1, 0), (1, 1)], 12: [(1, 2), (1, 3)]}
    QB = 3
    with ExitStack() as st:
        def sbuf(name, shape, dt=F32):
            return st.enter_context(nc.sbuf_tensor(name, shape, dt))

        ct_in, cn_in = sbuf("ct_in4", [P, CK, J]), sbuf("cn_in4", [P, JK, C])
        cT = [[sbuf(f"cT4{u}{part}", [P, CK, J], F32R) for part in range(2)] for u in range(2)]
        cN = [sbuf(f"cN4{part}", [P, JK, C], F32R) for part in range(2)]
        qp = sbuf("qp4", [P, 2, CK, H1, S])
        qs = [sbuf(f"qs4{part}", [P, QB, CK, P], F32R) for part in range(2)]
        pT = [sbuf(f"pT4{part}", [P, 2, JK, 512], F32R) for part in range(2)]
        pb = sbuf("pb4", [P, 2, J])
        qT = W0[:, 14336:15360].rearrange("p (m t) -> p m t", m=MK)
        oT = sbuf("oT4", [P, MK, P])
        xT = W0[:, 15360:15872].rearrange("p (k t) -> p k t", k=DK)
        bo = W0[0:1, 15872:16384]
        nmax, rsum, rinv = sbuf("nmax4", [P, 4]), sbuf("rsum4", [P, 4]), sbuf("rinv4", [P, 4])
        ln = Norm(nc, e, "4", sbuf, ps[6], xT)
        s_ct, s_cn, s_bo = sem("s_ct4"), sem("s_cn4"), sem("s_bo4")
        w_mm, w_sb, s_mm, m_dve = sem("w_mm4"), sem("w_sb4"), sem("s_mm4"), sem("m_dve4")
        e_sb, p_dve, pt_mm, pt_sb = sem("e_sb4"), sem("p_dve4"), sem("pt_mm4"), sem("pt_sb4")
        q_hi, q_lo, pt_hi, dve = sem("q_hi4"), sem("q_lo4"), sem("pt_hi4"), sem("dve4")
        ct_hi, ct_lo, cn_hi, cn_lo = sem("ct_hi4"), sem("ct_lo4"), sem("cn_hi4"), sem("cn_lo4")
        y_mm, added = sem("y_mm4"), sem("added4")
        work = [ps[4], ps[5], ps[7]]

        def pair_of(g):
            return qp[:, g // MK, :, 2 * (g % MK):2 * (g % MK) + 2, :].rearrange("p c h t -> p c (h t)")

        def turned(part, g):
            return part[:, g // 4 % 2, :, (g % 4) * P:(g % 4 + 1) * P]

        e.open_sems()
        with nc.Block() as block:
            @block.sync
            def _(sp):
                sp.dma_start(bo, a["bo4"]).then_inc(s_bo, 16)
                sp.dma_start(ct_in[:, :, :], a["ctxT"][0]).then_inc(s_ct, 16)
                sp.dma_start(cn_in[:, :, :], a["ctxN"][0]).then_inc(s_cn, 16)

                def next_T(n):
                    sp.wait_ge(ct_lo, BASE + CK * (n + 1))
                    sp.dma_start(ct_in[:, :, :], a["ctxT"][n + 1]).then_inc(s_ct, 16)

                def next_N(n):
                    sp.wait_ge(cn_lo, BASE + JK * (n + 1))
                    sp.dma_start(cn_in[:, :, :], a["ctxN"][n + 1]).then_inc(s_cn, 16)

                with sp.Fori(0, NT - 1) as i:
                    next_T(2 * i)
                    next_T(2 * i + 1)
                    next_N(2 * i)
                    next_N(2 * i + 1)
                next_T(B - 2)
                next_N(B - 2)

            @block.gpsimd
            def _(pool):
                ln.pool(pool, 0)
                with pool.Fori(0, NT - 1) as i:
                    ln.pool(pool, i + 1)

            @block.tensor
            def _(pe):
                def work_bank(use):
                    pe.wait_ge(w_sb, BASE + use + 1)

                def taken(use, count=1):
                    pe.wait_ge(w_sb, BASE + BANKS + use + count)

                def scores(i, g):
                    b, m = g // MK, g % MK
                    if m == 0:
                        pe.wait_ge(ct_lo, BASE + CK * (2 * i + b + 1))
                    pe.wait_ge(q_lo, BASE + PAIRS * i + g + 1)
                    pe.wait_ge(e_sb, BASE + PAIRS * i + g + 1)
                    split_product(nc, ps[g % 2], lambda part, c: qs[part][:, g % QB, c, :],
                            lambda part, c: cT[b][part][:, c, :], CK).then_inc(s_mm, 1)

                def turn(i, g):
                    pe.wait_ge(p_dve, BASE + PAIRS * i + g + 1)
                    if g == 0:
                        pe.wait_ge(added, BASE + i)
                    pe.wait_ge(pt_sb, BASE + PAIRS * i + g + 1)
                    for j in range(JK):
                        tr = nc.tensor.transpose(ps[2 + g % 2][:, j * P:(j + 1) * P],
                                                 pb[:, g % 2, j * P:(j + 1) * P], ident)
                    tr.then_inc(pt_mm, 1)

                def weigh(i, h, final=1):
                    if h % 2 == 0:
                        pe.wait_ge(cn_lo, BASE + JK * (2 * i + h // 2 + 1))
                    pe.wait_ge(pt_sb, BASE + PAIRS * i + 4 * h + 4 + 2)
                    for c in range(CK):
                        work_bank(PRE + USES * i + U_U[h] + c)
                        split_product(nc, work[(U_U[h] + c) % BANKS], lambda part, j: cN[part][:, j, c * P:(c + 1) * P],
                                lambda part, j: pT[part][:, h % 2, j, :], JK).then_inc(w_mm, final if c == CK - 1 else 1)

                def queries(i, use, which):
                    pe.wait_ge(ln.xT_ready, BASE + i + 1)
                    for n in range(2):
                        work_bank(use + n)
                        for m in range(4):
                            col = (4 * n + m) * P
                            for k in range(DK):
                                mm = nc.tensor.matmul(work[(which + n) % BANKS][:, m * P:(m + 1) * P],
                                                      wq4[:, k, col:col + P], xT[:, k, :],
                                                      start=(k == 0), stop=(k == DK - 1))
                        mm.then_inc(w_mm, 1)

                def queries_through_Wk(i, use, which, final):
                    for n in range(2):
                        for c in range(CK):
                            for r in range(2):
                                part = slice(r * DH1, (r + 1) * DH1)
                                step = 2 * (3 * n + c) + r
                                work_bank(use + step)
                                for m in range(4):
                                    mm = nc.tensor.matmul(work[(which + step) % BANKS][:, m * P:(m + 1) * P],
                                                          wk4[part, 4 * n + m, c * P:(c + 1) * P],
                                                          qT[part, 4 * n + m, :], start=True, stop=True)
                                mm.then_inc(w_mm, final if step == 11 else 1)

                def tile(i, last):
                    use = PRE + USES * i
                    scores(i, 0)
                    scores(i, 1)
                    for g in range(PAIRS):
                        if g + 2 < PAIRS:
                            scores(i, g + 2)
                        turn(i, g)
                        if g == 9 and not last:
                            ln.tensor(pe, i + 1)
                        if g % 4 == 1 and g > 4:
                            weigh(i, g // 4 - 1, 3 if last and g == 13 else 1)
                    if not last:
                        queries(i + 1, use + U_Q, U_Q)
                    weigh(i, 3)
                    taken(use + U_U[2] + 2)
                    for n in range(2):
                        if n:
                            taken(use + U_U[3] + 2)
                        work_bank(use + U_O + n)
                        bank = work[(U_O + n) % BANKS]
                        for m in range(4):
                            for r in range(2):
                                h = 2 * (4 * n + m) + r
                                for c in range(CK):
                                    mm = nc.tensor.matmul(
                                        bank[r * DH1:(r + 1) * DH1, m * P:(m + 1) * P].rearrange("p (b t) -> p b t", b=2),
                                        wv4[:, c, h * DH1:(h + 1) * DH1], qp[:, :, c, h, :],
                                        start=(c == 0), stop=(c == CK - 1))
                        mm.then_inc(w_mm, 1)
                    if not last:
                        queries_through_Wk(i + 1, use + U_QP, U_QP, 3)
                    taken(use + U_O + 1)
                    pe.wait_ge(pt_sb, BASE + PAIRS * i + PAIRS + 1)
                    for m in range(MK):
                        nc.tensor.matmul(ps[2], oT[:, m, :], wo4[:, m, :], start=(m == 0), stop=False)
                    nc.tensor.matmul(ps[2], ones[0:1, :], bo, start=False, stop=True).then_inc(y_mm, 1)

                pe.sem_inc(pt_mm, 1)
                ln.tensor(pe, 0)
                pe.wait_ge(e.s_w4, BASE + 64)
                pe.wait_ge(s_bo, BASE + 16)
                queries(0, 0, 0)
                taken(1)
                queries_through_Wk(0, 2, 2, 2)
                with pe.Fori(0, NT - 1) as i:
                    tile(i, False)
                tile(NT - 1, True)

            @block.scalar
            def _(act):
                def take(use, which, out, scale=1.0, count=1):
                    act.wait_ge(w_mm, BASE + use + count)
                    src = work[which % BANKS]
                    if len(out.shape) == 4:
                        src = src.rearrange("p (m b t) -> p m b t", m=4, b=2)
                    nc.scalar.activation(out, src, ACT.Copy, scale=scale).then_inc(w_sb, count)

                def exponent(i, g):
                    act.wait_ge(m_dve, BASE + PAIRS * i + g + 1)
                    act.wait_ge(pt_mm, BASE + PAIRS * i + g)
                    nc.scalar.activation(pb[:, g % 2, :], ps[g % 2], ACT.Exp, bias=nmax[:, g % 4:g % 4 + 1],
                                         accum_out=rsum[:, g % 4:g % 4 + 1]).then_inc(e_sb, 1)

                def first_q(i, g):
                    nc.scalar.activation(qs[0][:, g % QB, :, :], pair_of(g), ACT.Copy).then_inc(q_hi, 1)

                def first_T(i, u, c):
                    act.wait_ge(s_ct, BASE + 16 * (2 * i + u) + 16)
                    nc.scalar.activation(cT[u][0][:, c, :], ct_in[:, c, :], ACT.Copy).then_inc(ct_hi, 1)

                def first_N(i, u, j):
                    act.wait_ge(s_cn, BASE + 16 * (2 * i + u) + 16)
                    nc.scalar.activation(cN[0][:, j, :], cn_in[:, j, :], ACT.Copy).then_inc(cn_hi, 1)

                def first_P(i, g):
                    act.wait_ge(pt_mm, BASE + PAIRS * i + g + 2)
                    nc.scalar.activation(turned(pT[0], g), ps[2 + g % 2].rearrange("p (j n) -> p j n", j=JK),
                                         ACT.Copy).then_inc(pt_hi, 1)

                def weighed(i, h, final=1):
                    for c in range(CK):
                        take(PRE + USES * i + U_U[h] + c, U_U[h] + c,
                             qp[:, h // 2, c, 8 * (h % 2):8 * (h % 2) + 8, :].rearrange("p h t -> p (h t)"),
                             count=final if c == CK - 1 else 1)

                def queries(use, which):
                    for n in range(2):
                        take(use + n, which + n, qT[:, 4 * n:4 * n + 4, :].rearrange("p m t -> p (m t)"), SCALE)

                def queries_through_Wk(i, use, which, final):
                    for n in range(2):
                        for c in range(CK):
                            for r in range(2):
                                heads = qp[:, :, c, 8 * n + r:8 * n + 8:2, :].rearrange("p b m t -> p m b t")
                                step = 2 * (3 * n + c) + r
                                take(use + step, which + step, heads, count=final if step == 11 else 1)
                        if n == 0:
                            act.wait_ge(w_sb, BASE + BANKS + use + 6)
                            for g in range(QB):
                                first_q(i, g)
                    act.wait_ge(w_sb, BASE + BANKS + use + 11 + final)

                def tile(i, last):
                    use = PRE + USES * i
                    for g in range(PAIRS):
                        if g < PAIRS - 1:
                            exponent(i, g)
                        if g == PAIRS - 2:
                            exponent(i, g + 1)
                        if g + QB < PAIRS:
                            first_q(i, g + QB)
                        if g:
                            first_P(i, g - 1)
                        if g % 4 == 2 and g > 4:
                            weighed(i, g // 4 - 1, 3 if last and g == 14 else 1)
                        for u, c in SPLIT_T.get(g, []):
                            first_T(i, u, c)
                        if g == 10 and not last:
                            ln.scalar(act, i + 1, w_mm, use - 13)
                        for u, j in SPLIT_N.get(g, []):
                            first_N(i, u, j)
                    first_P(i, PAIRS - 1)
                    if not last:
                        queries(use + U_Q, U_Q)
                        for c in range(CK):
                            first_T(i + 1, 0, c)
                    weighed(i, 3)
                    for n in range(2):
                        take(use + U_O + n, U_O + n, oT[:, 4 * n:4 * n + 4, :].rearrange("p m t -> p (m t)"))
                    if not last:
                        queries_through_Wk(i + 1, use + U_QP, U_QP, 3)

                act.sem_inc(w_sb, BANKS)
                act.sem_inc(e_sb, 2)
                ln.scalar(act, 0, w_mm, 0)
                queries(0, 0)
                for c in range(CK):
                    first_T(0, 0, c)
                queries_through_Wk(0, 2, 2, 2)
                with act.Fori(0, NT - 1) as i:
                    tile(i, False)
                tile(NT - 1, True)

            @block.vector
            def _(ve):
                ch = Chain(ve, dve)

                def maximum(i, g):
                    ve.wait_ge(s_mm, BASE + PAIRS * i + g + 1)
                    nc.vector.tensor_reduce(nmax[:, g % 4:g % 4 + 1], ps[g % 2], AX.X, ALU.max,
                                            negate=True).then_inc(m_dve, 1)

                def rest(out, whole, first):
                    return nc.vector.tensor_tensor(out, whole, first.bitcast(F32), ALU.subtract)

                def rest_q(i, g):
                    ve.wait_ge(q_hi, BASE + PAIRS * i + g + 1)
                    rest(qs[1][:, g % QB, :, :], pair_of(g), qs[0][:, g % QB, :, :]).then_inc(q_lo, 1)

                def rest_T(i, u, c):
                    ve.wait_ge(ct_hi, BASE + CK * (2 * i + u) + c + 1)
                    rest(cT[u][1][:, c, :], ct_in[:, c, :], cT[u][0][:, c, :]).then_inc(ct_lo, 1)

                def rest_N(i, u, j):
                    ve.wait_ge(cn_hi, BASE + JK * (2 * i + u) + j + 1)
                    rest(cN[1][:, j, :], cn_in[:, j, :], cN[0][:, j, :]).then_inc(cn_lo, 1)

                def rest_P(i, g):
                    ve.wait_ge(pt_hi, BASE + PAIRS * i + g + 1)
                    rest(turned(pT[1], g), ps[2 + g % 2].rearrange("p (j n) -> p j n", j=JK),
                         turned(pT[0], g)).then_inc(pt_sb, 1)

                def tile(i, last):
                    maximum(i, 0)
                    maximum(i, 1)
                    for g in range(PAIRS):
                        ve.wait_ge(e_sb, BASE + PAIRS * i + g + 1 + 2)
                        r = rinv[:, g % 4:g % 4 + 1]
                        ch.link(nc.vector.reciprocal(r, rsum[:, g % 4:g % 4 + 1]))
                        nc.vector.tensor_scalar(pb[:, g % 2, :], pb[:, g % 2, :], r, None, ALU.mult).then_inc(p_dve, 1)
                        if g + QB < PAIRS:
                            rest_q(i, g + QB)
                        if g:
                            rest_P(i, g - 1)
                        if g + 2 < PAIRS:
                            maximum(i, g + 2)
                        for u, c in SPLIT_T.get(g, []):
                            rest_T(i, u, c)
                        for u, j in SPLIT_N.get(g, []):
                            rest_N(i, u, j)
                        if g == 6 and not last:
                            ln.vector_stats(ch, i + 1)
                        if g == 7 and not last:
                            ln.vector_norm(ve, i + 1)
                    rest_P(i, PAIRS - 1)
                    if not last:
                        for c in range(CK):
                            rest_T(i + 1, 0, c)
                        for g in range(QB):
                            rest_q(i + 1, g)
                    ve.wait_ge(y_mm, BASE + i + 1)
                    nc.vector.tensor_tensor(x[:, i, :], x[:, i, :], ps[2], ALU.add).then_inc(added, 1)

                ve.sem_inc(pt_sb, 2)
                ln.vector_stats(ch, 0)
                ln.vector_norm(ve, 0)
                for c in range(CK):
                    rest_T(0, 0, c)
                for g in range(QB):
                    rest_q(0, g)
                with ve.Fori(0, NT - 1) as i:
                    ch.turn(i, 2 + PAIRS)
                    tile(i, False)
                ch.again(NT - 1)
                tile(NT - 1, True)

def decayed_attention_layer(nc, a, e):
    x, cn, ps, ones, ident, sem, W0 = e.x, e.cn, e.ps, e.ones, e.ident, e.sem, e.W0
    W5_Q, W5_K, W5_V, W5_A, W5_O = range(5)
    v_d, ba_d = e.v_d, e.ba_d
    sel = cn[:, CN_SEL:CN_SEL + B]
    G = 8
    NG = S // G
    with ExitStack() as st:
        def sbuf(name, shape, dt=F32):
            return st.enter_context(nc.sbuf_tensor(name, shape, dt))

        ba = sbuf("ba5", [P, NT, 2 * HS])
        baT = sbuf("baT5", [2 * HS, B * S])
        s_w5 = [sem(f"s_w5_{w}") for w in range(5)]
        s_v, s_ba, baT_sb = sem("s_v5"), sem("s_ba5"), sem("baT_sb5")

        s_in, s_vb = sem("s_in5"), [sem("s_vb5_0"), sem("s_vb5_1")]
        t_dve, t_exp, coef = sem("t_dve5"), sem("t_exp5"), sem("coef5")
        bv_sb, ebv_sb, ear_sb, r_sb = sem("bv_sb5"), sem("ebv_sb5"), sem("ear_sb5"), sem("r_sb5")
        s_sb, ep_sb, sg_sb, seen = sem("s_sb5"), sem("ep_sb5"), sem("sg_sb5"), sem("seen5s")
        y_mm, yT_sb, z_mm, z_used, ch5 = sem("y_mm5"), sem("yT_sb5"), sem("z_mm5"), sem("z_used5"), sem("ch5")

        with ExitStack() as pt:
            def pbuf(name, shape, dt=F32):
                return pt.enter_context(nc.sbuf_tensor(name, shape, dt))

            xT = [[pbuf(f"xT5{u}{part}", [P, DK, P], F32R) for part in range(2)] for u in range(2)]
            ws = [[pbuf(f"ws5{w}{part}", [P, DK, D], F32R) for part in range(2)] for w in range(4)]
            w_in = W0[:, 0:4 * DK * D].rearrange("p (w k n) -> p w k n", w=4, k=DK)
            ORDER = (W5_Q, W5_A, W5_K, W5_V)
            w_hi, w_lo = sem("w_hi5"), sem("w_lo5")
            ln = Norm(nc, e, "5", pbuf, ps[7], xT[0])
            q, qk, mag, ex, lg, soft = (pbuf(n, [P, D]) for n in ("q5", "qk5", "mag5", "ex5", "lg5", "soft5"))
            v0, ve_, vv = pbuf("v05", [P, D]), pbuf("veps5", [P, D]), pbuf("vv5", [P, 2, D])
            bal = pbuf("bal5", [1, D])
            s_bal, q_mm, k_mm, v_mm, a_mm = sem("s_bal5"), sem("q_mm5"), sem("k_mm5"), sem("v_mm5"), sem("a_mm5")
            q_sb, mag_sb, ex_sb, lg_sb = sem("q_sb5"), sem("mag_sb5"), sem("ex_sb5"), sem("lg_sb5")
            k_used, v_used, a_used, v_sb, vv_sb = sem("k_used5"), sem("v_used5"), sem("a_used5"), sem("v_sb5"), sem("vv_sb5")
            v_out = [sem("v_out5_0"), sem("v_out5_1")]
            ba_sb, t_mm, dve = sem("ba_sb5"), sem("t_mm5"), sem("dve5")

            e.open_sems()
            with nc.Block() as block:
                @block.sync
                def _(sp):
                    sp.dma_start(bal[:, :], a["ba5"]).then_inc(s_bal, 16)
                    for w in ORDER:
                        sp.dma_start(w_in[:, w], a["w5"][:, w]).then_inc(s_w5[w], 16)
                    with sp.Fori(0, NT // 2) as i:
                        for u in range(2):
                            sp.wait_ge(vv_sb, BASE + 2 * i + u + 1)
                            sp.dma_start(v_d[bass.ds((2 * i + u) * P, P), :], vv[:, u, :]).then_inc(v_out[u], 16)
                    sp.wait_ge(baT_sb, BASE + 2)
                    for c in range(2):
                        sp.dma_start(ba_d[c].rearrange("(b h) t -> h b t", b=B),
                                     baT[c * HS:(c + 1) * HS, :].rearrange("h (b t) -> h b t", b=B)).then_inc(s_ba, 16)
                    for u in range(2):
                        sp.wait_ge(v_out[u], BASE + 16 * NT // 2)
                    sp.wait_ge(s_ba, BASE + 32)

                @block.gpsimd
                def _(pool):
                    ln.pool(pool, 0)
                    with pool.Fori(0, NT) as i:
                        ln.pool(pool, i + 1)

                @block.tensor
                def _(pe):
                    ln.tensor(pe, 0)
                    pe.wait_ge(s_bal, BASE + 16)

                    def tile(i, u):
                        pe.wait_ge(ln.xT_ready, BASE + i + 1)
                        for bank, w, done, used in ((0, 0, q_mm, q_sb), (1, W5_A, a_mm, a_used),
                                                    (2, 1, k_mm, k_used), (3, 2, v_mm, v_used)):
                            pe.wait_ge(w_lo, BASE + ORDER.index(w) + 1)
                            pe.wait_ge(used, BASE + i)
                            if w == W5_A:
                                nc.tensor.matmul(ps[bank], ones[0:1, :], bal[0:1, :], start=True, stop=False)
                            split_product(nc, ps[bank], lambda part, k: xT[u][part][:, k, :],
                                          lambda part, k: ws[w][part][:, k, :], DK, w != W5_A).then_inc(done, 1)
                            if w == W5_A:
                                ln.tensor(pe, i + 1)

                    with pe.Fori(0, NT // 2) as i2:
                        tile(2 * i2, 0)
                        tile(2 * i2 + 1, 1)
                    pe.wait_ge(ba_sb, BASE + 2 * NT)
                    for t in range(NT):
                        tr = nc.tensor.transpose(ps[4 + t // 4][0:2 * HS, t % 4 * P:(t % 4 + 1) * P], ba[:, t, :], ident)
                        if t % 4 == 3:
                            tr.then_inc(t_mm, 1)

                @block.scalar
                def _(act):
                    ln.xT = xT[0]
                    ln.scalar(act, 0, v_mm)
                    for w in ORDER:
                        act.wait_ge(s_w5[w], BASE + 16)
                        nc.scalar.activation(ws[w][0][:, :, :], w_in[:, w], ACT.Copy).then_inc(w_hi, 1)

                    def tile(i, u):
                        act.wait_ge(q_mm, BASE + i + 1)
                        act.wait_ge(k_used, BASE + i)
                        nc.scalar.activation(q[:, :], ps[0], ACT.Copy, scale=DHS ** -0.5).then_inc(q_sb, 1)
                        act.wait_ge(a_mm, BASE + i + 1)
                        nc.scalar.activation(mag[:, :], ps[1], ACT.Abs).then_inc(mag_sb, 1)
                        ln.xT = xT[1 - u]
                        ln.scalar(act, i + 1, v_mm, i)
                        act.wait_ge(mag_sb, BASE + i + 1)
                        nc.scalar.activation(ex[:, :], mag[:, :], ACT.Exp, scale=-1.0).then_inc(ex_sb, 1)
                        act.wait_ge(ex_sb, BASE + i + 1)
                        act.wait_ge(a_used, BASE + i)
                        nc.scalar.activation(lg[:, :], ex[:, :], ACT.Ln, bias=cn[:, CN_ONE:CN_ONE + 1]).then_inc(lg_sb, 1)

                    with act.Fori(0, NT // 2) as i2:
                        tile(2 * i2, 0)
                        tile(2 * i2 + 1, 1)
                    for g in range(2):
                        act.wait_ge(t_mm, BASE + g + 1)
                        nc.scalar.activation(baT[:, g * 512:(g + 1) * 512], ps[4 + g][0:2 * HS, :],
                                             ACT.Copy).then_inc(baT_sb, 1)

                @block.vector
                def _(ve):
                    ch = Chain(ve, dve)
                    ln.vector_stats(ch, 0)
                    ln.vector_norm(ve, 0)
                    ln.xT = xT[0]
                    ln.vector_rest(ve, 0)
                    for n, w in enumerate(ORDER):
                        ve.wait_ge(w_hi, BASE + n + 1)
                        nc.vector.tensor_tensor(ws[w][1][:, :, :], w_in[:, w], ws[w][0][:, :, :].bitcast(F32),
                                                ALU.subtract).then_inc(w_lo, 1)
                    with ve.Fori(0, NT // 2) as i2:
                        ch.turn(i2, 4)
                        for u in range(2):
                            i = 2 * i2 + u
                            ln.vector_stats(ch, i + 1)
                            ln.vector_norm(ve, i + 1)
                            ln.xT = xT[1 - u]
                            ln.vector_rest(ve, i + 1)
                            ve.wait_ge(lg_sb, BASE + i + 1)
                            nc.vector.scalar_tensor_tensor(soft[:, :], ps[1], 0.0, lg[:, :], ALU.max,
                                                           ALU.add).then_inc(a_used, 1)
                            ve.wait_ge(a_used, BASE + i + 1)
                            nc.vector.tensor_reduce(ba[:, i, HS:2 * HS], soft[:, :].rearrange("p (h d) -> p h d", h=HS),
                                                    AX.X, ALU.add, negate=True).then_inc(ba_sb, 1)
                            ve.wait_ge(q_sb, BASE + i + 1)
                            ve.wait_ge(k_mm, BASE + i + 1)
                            nc.vector.tensor_tensor(qk[:, :], q[:, :], ps[2], ALU.mult).then_inc(k_used, 1)
                            ve.wait_ge(k_used, BASE + i + 1)
                            nc.vector.tensor_reduce(ba[:, i, 0:HS], qk[:, :].rearrange("p (h d) -> p h d", h=HS),
                                                    AX.X, ALU.add).then_inc(ba_sb, 1)
                            ve.wait_ge(v_mm, BASE + i + 1)
                            nc.vector.tensor_scalar(v0[:, :], ps[3], 0.0, None, ALU.add).then_inc(v_used, 1)
                            ve.wait_ge(v_used, BASE + i + 1)
                            nc.vector.tensor_scalar(ve_[:, :].bitcast(U32), v0[:, :].bitcast(U32), SIGN_BIT, EPS_BITS,
                                                    ALU.bitwise_and, ALU.bitwise_or).then_inc(v_sb, 1)
                            ve.wait_ge(v_sb, BASE + i + 1)
                            ve.wait_ge(v_out[u], BASE + 16 * i2)
                            nc.vector.tensor_tensor(vv[:, u, :], v0[:, :], ve_[:, :], ALU.add).then_inc(vv_sb, 1)
                        assert ch.n == 4

        BS = [P, S]
        bS, aS, mx, t1, t2, eA, eB, dn, rd = (sbuf(n, BS) for n in
                                              ("bS5", "aS5", "mx5", "t15", "t25", "eA5", "eB5", "dn5", "rd5"))
        al, be, eal, ebe = (sbuf(n, BS) for n in ("al5", "be5", "eal5", "ebe5"))
        vb = sbuf("vb5", [P, 2, G, D])
        W1 = sbuf("W1s", [P, 16384])
        wo = W1[:, 8192:8192 + DK * D].rearrange("p (k n) -> p k n", k=DK)
        off = 10240
        rb = W1[:, off:off + 2048].rearrange("p (n d) -> p n d", n=4)
        bv = W1[:, off + 2048:off + 3072].rearrange("p (n d) -> p n d", n=2)
        ebv = W1[:, off + 3072:off + 4096].rearrange("p (n d) -> p n d", n=2)
        ear, s_, ep, sg = (W1[:, off + 4096 + n * D:off + 4096 + (n + 1) * D] for n in range(4))
        yT = W1[:, 0:DK * B * S].rearrange("p (k n) -> p k n", k=DK)
        RB = 4
        HALVES = slice(0, D // 2), slice(D // 2, D)

        with nc.Block() as block:
            @block.sync
            def _(sp):
                sp.dma_start(bS[:, :], ba_d[0]).then_inc(s_in, 16)
                sp.dma_start(aS[:, :], ba_d[1]).then_inc(s_in, 16)

                def load(group, u):
                    for b in range(B):
                        rows = v_d[bass.ds(group * G + b * S, G), :].rearrange("t d -> (t d)")
                        sp.dma_start(vb[b * HS:(b + 1) * HS, u].rearrange("p t d -> p (t d)"),
                                     rows.partition_broadcast(HS)).then_inc(s_vb[u], 16)

                load(0, 0)
                load(1, 1)
                sp.dma_start(wo, a["w5"][:, W5_O]).then_inc(s_w5[W5_O], 16)
                sp.dma_start(e.w16, a["w16"]).then_inc(e.s_w6, 16)
                sp.dma_start(e.w26, a["w26"]).then_inc(e.s_w6, 16)
                with sp.Fori(0, NG // 2 - 1) as i:
                    for u in range(2):
                        sp.wait_ge(ebv_sb, BASE + 2 * G * i + G * (u + 1))
                        load(2 * i + 2 + u, u)

            @block.vector
            def _(ve):
                ch = Chain(ve, ch5)
                ve.wait_ge(s_in, BASE + 32)
                ch.link(nc.vector.memset(eA[:, 0:1], 0.0))
                ch.link(nc.vector.memset(al[:, 0:1], 0.0))
                ch.link(nc.vector.memset(rb[:, RB - 1, :], 0.0))
                ch.link(nc.vector.tensor_tensor_scan(mx[:, :], aS[:, :], bS[:, :], -3.0e38, ALU.add, ALU.max))
                ch.link(nc.vector.tensor_tensor(t1[:, 1:S], aS[:, 1:S], mx[:, 0:S - 1], ALU.add))
                nc.vector.tensor_tensor(t1[:, 1:S], t1[:, 1:S], mx[:, 1:S], ALU.subtract).then_inc(t_dve, 1)
                nc.vector.tensor_tensor(t2[:, :], bS[:, :], mx[:, :], ALU.subtract).then_inc(t_dve, 1)
                ve.wait_ge(t_exp, BASE + 2)
                ch.link(nc.vector.tensor_tensor_scan(dn[:, :], eA[:, :], eB[:, :], 0.0, ALU.mult, ALU.add))
                ch.link(nc.vector.reciprocal(rd[:, :], dn[:, :]))
                ch.link(nc.vector.tensor_tensor(al[:, 1:S], eA[:, 1:S], dn[:, 0:S - 1], ALU.mult))
                ch.link(nc.vector.tensor_tensor(al[:, 1:S], al[:, 1:S], rd[:, 1:S], ALU.mult))
                ch.link(nc.vector.tensor_tensor(be[:, :], eB[:, :], rd[:, :], ALU.mult))
                ch.link(nc.vector.tensor_scalar(eal[:, :], al[:, :], EPS, None, ALU.mult))
                ch.link(nc.vector.tensor_scalar(ebe[:, :], be[:, :], EPS, None, ALU.mult))
                nc.vector.memset(ebe[:, 0:1], 0.0).then_inc(coef, 1)
                ve.wait_ge(coef, BASE + 1)
                ve.sem_inc(r_sb, 1)
                with ve.Fori(0, S // (2 * G)) as i:
                    for j in range(2 * G):
                        t = 2 * G * i + j
                        old, new = rb[:, (j - 1) % RB, :], rb[:, j % RB, :]
                        for h, cols in enumerate(HALVES):
                            ve.wait_ge(r_sb, BASE + 2 * t + h)
                            ve.wait_ge(bv_sb, BASE + t + 1)
                            nc.vector.scalar_tensor_tensor(s_[:, cols], old[:, cols], al[:, bass.ds(t, 1)],
                                                           bv[:, j % 2, cols], ALU.mult, ALU.add).then_inc(s_sb, 1)
                        for h, cols in enumerate(HALVES):
                            ve.wait_ge(ebv_sb, BASE + t + 1)
                            ve.wait_ge(ear_sb, BASE + 2 * t + h + 1)
                            nc.vector.tensor_tensor(ep[:, cols], ear[:, cols], ebv[:, j % 2, cols],
                                                    ALU.max).then_inc(ep_sb, 1)
                        for h, cols in enumerate(HALVES):
                            ve.wait_ge(ep_sb, BASE + 2 * t + h + 1)
                            ve.wait_ge(s_sb, BASE + 2 * t + h + 1)
                            nc.vector.scalar_tensor_tensor(sg[:, cols].bitcast(U32), s_[:, cols].bitcast(U32), SIGN_BIT,
                                                           ep[:, cols].bitcast(U32), ALU.bitwise_and,
                                                           ALU.bitwise_or).then_inc(sg_sb, 1)
                        for h, cols in enumerate(HALVES):
                            ve.wait_ge(sg_sb, BASE + 2 * t + h + 1)
                            ve.wait_ge(y_mm, BASE + t + 1)
                            nc.vector.tensor_tensor(new[:, cols], s_[:, cols], sg[:, cols], ALU.add).then_inc(r_sb, 1)
                for t in range(NT):
                    ve.wait_ge(z_mm, BASE + t + 1)
                    nc.vector.tensor_tensor(x[:, t, :], x[:, t, :], ps[2 + t % 4], ALU.add).then_inc(z_used, 1)

            @block.scalar
            def _(act):
                act.wait_ge(t_dve, BASE + 2)
                nc.scalar.activation(eA[:, 1:S], t1[:, 1:S], ACT.Exp).then_inc(t_exp, 1)
                nc.scalar.activation(eB[:, :], t2[:, :], ACT.Exp).then_inc(t_exp, 1)
                act.wait_ge(coef, BASE + 1)
                def outputs(i, u):
                    act.wait_ge(y_mm, BASE + 2 * G * i + G * (u + 1) + RB)
                    out = yT[:, :, :].rearrange("p k (b t) -> p k t b", b=B)[:, :, bass.ds(2 * G * i + G * u, G), :]
                    nc.scalar.activation(out, ps[u].rearrange("p (k t b) -> p k t b", k=DK, t=G),
                                         ACT.Copy).then_inc(yT_sb, 1)

                def turn(i, first):
                    for j in range(2 * G):
                        t = 2 * G * i + j
                        u = j // G
                        if j % G == 0:
                            act.wait_ge(s_vb[u], BASE + 16 * B * (i + 1))
                        act.wait_ge(s_sb, BASE + 2 * t)
                        nc.scalar.activation(bv[:, j % 2, :], vb[:, u, j % G, :], ACT.Copy,
                                             scale=be[:, bass.ds(t, 1)]).then_inc(bv_sb, 1)
                        nc.scalar.activation(ebv[:, j % 2, :], vb[:, u, j % G, :], ACT.Abs,
                                             scale=ebe[:, bass.ds(t, 1)]).then_inc(ebv_sb, 1)
                        for h, cols in enumerate(HALVES):
                            act.wait_ge(r_sb, BASE + 2 * t + h)
                            act.sem_inc(seen)
                            nc.scalar.activation(ear[:, cols], rb[:, (j - 1) % RB, cols], ACT.Abs,
                                                 scale=eal[:, bass.ds(t, 1)]).then_inc(ear_sb, 1)
                        if j == G + 1:
                            outputs(i, 0)
                        if j == 1 and not first:
                            outputs(i - 1, 1)

                act.sem_inc(yT_sb, 1)
                turn(0, True)
                with act.Fori(0, S // (2 * G) - 1) as i:
                    turn(i + 1, False)
                outputs(S // (2 * G) - 1, 1)

            @block.tensor
            def _(pe):
                pe.sem_inc(y_mm, RB)
                with pe.Fori(0, S // (2 * G)) as i:
                    for j in range(2 * G):
                        t = 2 * G * i + j
                        u = j // G
                        if j % G == 0:
                            pe.wait_ge(yT_sb, BASE + 2 * i + u)
                        for k in range(DK):
                            pe.wait_ge(r_sb, BASE + 2 * t + 2 + 2 * k // DK)
                            col = k * G * B + (j % G) * B
                            mm = nc.tensor.matmul(ps[u][:, col:col + B], rb[:, j % RB, k * P:(k + 1) * P], sel,
                                                  start=True, stop=True)
                        mm.then_inc(y_mm, 1)
                pe.wait_ge(yT_sb, BASE + NG + 1)
                pe.wait_ge(s_w5[W5_O], BASE + 16)
                for t in range(NT):
                    if t >= 4:
                        pe.wait_ge(z_used, BASE + t - 3)
                    for k in range(DK):
                        mm = nc.tensor.matmul(ps[2 + t % 4], yT[:, k, t * P:(t + 1) * P], wo[:, k, :],
                                              start=(k == 0), stop=(k == DK - 1))
                    mm.then_inc(z_mm, 1)


def feed_forward_layer(nc, a, e):
    x, cn, ps, ident, sem, w16, w26 = e.x, e.cn, e.ps, e.ident, e.sem, e.w16, e.w26
    FT = FF // P
    TG = 4
    NGR = NT // TG
    TOP = 4.0 * QUANT
    STEP = QUANT / 4.0
    out = e.out
    with ExitStack() as st:
        def sbuf(name, shape, dt=F32):
            return st.enter_context(nc.sbuf_tensor(name, shape, dt))

        hs = sbuf("hs6", [P, NGR, FT, 512])
        xT = [sbuf(f"xT6{g}", [P, DK, TG * P]) for g in range(NGR)]
        b1, b1q = sbuf("b16", [P, FT]), sbuf("b1q6", [P, FT])
        b2 = sbuf("b26", [P, D])
        h, r, c, w, km, g0, g1, up = (sbuf(n, [P, 2, 512]) for n in
                                      ("h6", "r6", "c6", "w6", "km6", "g06", "g16", "up6"))
        dg = sbuf("dg6", [P, 2, 512])
        y = sbuf("y6", [P, 512])
        z = x[:, NT, :]
        ln = Norm(nc, e, "6", sbuf, ps[7], None)
        s_b, b_q, dve = sem("s_b6"), sem("b_q6"), sem("dve6")
        h_mm, h_sb, r_sb, c_sb, w_sb, km_sb, g_sb, up_sb, dg_sb, hs_sb = (
            sem(n) for n in ("h_mm6", "h_sb6", "r_sb6", "c_sb6", "w_sb6", "km_sb6", "g_sb6", "up_sb6", "dg_sb6", "hs_sb6"))
        z_mm, z_used, x_done, s_out = sem("z_mm6"), sem("z_used6"), sem("x_done6"), sem("s_out6")
        N = NGR * FT
        HB, ZB = 3, 3
        NORM_AT = [1 + 2 * t for t in range(TG)]
        TURN_LAG, OUT_LAG = 6, 4

        e.open_sems()
        with nc.Block() as block:
            @block.sync
            def _(sp):
                sp.dma_start(b1[:, :], a["b16"]).then_inc(s_b, 16)
                sp.dma_start(b2[:, :], a["b26"]).then_inc(s_b, 16)
                for t in range(NT):
                    sp.wait_ge(x_done, BASE + t + 1)
                    sp.dma_start(out[:, t, :], x[:, t, :]).then_inc(s_out, 16)
                sp.wait_ge(s_out, BASE + 16 * NT)

            @block.gpsimd
            def _(pool):
                def slope(n):
                    pool.wait_ge(g_sb, BASE + 2 * n + 2)
                    if n >= 2:
                        pool.wait_ge(hs_sb, BASE + n - 1)
                    nc.gpsimd.tensor_tensor(dg[:, n % 2, :], g1[:, n % 2, :], g0[:, n % 2, :],
                                            ALU.subtract).then_inc(dg_sb, 1)

                for t in range(TG):
                    ln.pool(pool, t)
                for n in range(N):
                    slope(n)
                    if n in NORM_AT:
                        ln.pool(pool, TG + NORM_AT.index(n))

            @block.tensor
            def _(pe):
                def hidden(n):
                    g, f = divmod(n, FT)
                    if f == 0:
                        pe.wait_ge(ln.xT_ready, BASE + TG * (g + 1))
                    if n >= HB:
                        pe.wait_ge(h_sb, BASE + n - HB + 1)
                    for k in range(DK):
                        mm = nc.tensor.matmul(ps[n % HB], w16[:, k, f * P:(f + 1) * P], xT[g][:, k, :],
                                              start=(k == 0), stop=(k == DK - 1))
                    mm.then_inc(h_mm, 1)

                def output(t, f0, f1):
                    if f0 == 0 and t >= ZB:
                        pe.wait_ge(z_used, BASE + t - ZB + 1)
                    for f in range(f0, f1):
                        pe.wait_ge(hs_sb, BASE + FT * (t // TG) + f + 1)
                        mm = nc.tensor.matmul(ps[HB + t % ZB], hs[:, t // TG, f, (t % TG) * P:(t % TG + 1) * P],
                                              w26[:, f, :], start=(f == 0), stop=(f == FT - 1))
                    if f1 == FT:
                        mm.then_inc(z_mm, 1)

                for t in range(TG):
                    ln.tensor(pe, t)
                pe.wait_ge(e.s_w6, BASE + 32)
                for n in range(FT):
                    hidden(n)
                    if n - TURN_LAG in NORM_AT:
                        ln.tensor(pe, TG + NORM_AT.index(n - TURN_LAG))
                per = FT // TG
                for f in range(FT):
                    hidden(FT + f)
                    output(f // per, f % per * per, (f % per + 1) * per)
                for t in range(TG, NT):
                    output(t, 0, FT)

            @block.scalar
            def _(act):
                def norm_out(t):
                    act.wait_ge(ln.turned, BASE + t + 1)
                    part = xT[t // TG][:, :, t % TG * P:(t % TG + 1) * P]
                    nc.scalar.activation(part, ps[7].rearrange("p (k t) -> p k t", k=DK),
                                         ACT.Copy).then_inc(ln.xT_ready, 1)

                def stage_a(n):
                    act.wait_ge(h_mm, BASE + n + 1)
                    if n >= 2:
                        act.wait_ge(r_sb, BASE + n - 1)
                    nc.scalar.activation(h[:, n % 2, :], ps[n % HB], ACT.Identity, scale=QUANT,
                                         bias=b1q[:, n % FT:n % FT + 1]).then_inc(h_sb, 1)

                def stage_b(n):
                    u = n % 2
                    act.wait_ge(w_sb, BASE + n + 1)
                    if n >= 2:
                        act.wait_ge(hs_sb, BASE + n - 1)
                        act.wait_ge(dg_sb, BASE + n - 1)
                    nc.scalar.activation(km[:, u, :], w[:, u, :], ACT.Identity,
                                         bias=cn[:, CN_ROUND:CN_ROUND + 1]).then_inc(km_sb, 1)
                    nc.scalar.activation(up[:, u, :], r[:, u, :], ACT.Relu,
                                         bias=cn[:, CN_TOP:CN_TOP + 1]).then_inc(up_sb, 1)
                    act.wait_ge(km_sb, BASE + n + 1)
                    nc.scalar.activation(g0[:, u, :], km[:, u, :], ACT.Gelu, scale=0.25,
                                         bias=cn[:, CN_K0:CN_K0 + 1]).then_inc(g_sb, 1)
                    nc.scalar.activation(g1[:, u, :], km[:, u, :], ACT.Gelu, scale=0.25,
                                         bias=cn[:, CN_K1:CN_K1 + 1]).then_inc(g_sb, 1)

                for t in range(TG):
                    norm_out(t)
                act.wait_ge(b_q, BASE + 2)
                stage_a(0)
                for n in range(N):
                    if n + 1 < N:
                        stage_a(n + 1)
                    stage_b(n)
                    if n - OUT_LAG in NORM_AT:
                        norm_out(TG + NORM_AT.index(n - OUT_LAG))

            @block.vector
            def _(ve):
                ch = Chain(ve, dve)

                def round_(n):
                    u = n % 2
                    ve.wait_ge(h_sb, BASE + n + 1)
                    if n >= 2:
                        ve.wait_ge(up_sb, BASE + n - 1)
                    nc.vector.tensor_scalar(r[:, u, :], h[:, u, :], ROUND, ROUND, ALU.add,
                                            ALU.subtract).then_inc(r_sb, 1)
                    ve.wait_ge(r_sb, BASE + n + 1)
                    nc.vector.tensor_scalar(c[:, u, :], r[:, u, :], -TOP, TOP, ALU.max, ALU.min).then_inc(c_sb, 1)
                    ve.wait_ge(c_sb, BASE + n + 1)
                    if n >= 2:
                        ve.wait_ge(km_sb, BASE + n - 1)
                    nc.vector.tensor_scalar(w[:, u, :], c[:, u, :], -(STEP - 1) / 2, 1.0 / STEP, ALU.add,
                                            ALU.mult).then_inc(w_sb, 1)

                def interpolate(n):
                    g, f = divmod(n, FT)
                    u = n % 2
                    ve.wait_ge(km_sb, BASE + n + 1)
                    ch.link(nc.vector.scalar_tensor_tensor(c[:, u, :], km[:, u, :], ROUND, w[:, u, :],
                                                           ALU.subtract, ALU.subtract))
                    ve.wait_ge(dg_sb, BASE + n + 1)
                    ch.link(nc.vector.scalar_tensor_tensor(c[:, u, :], c[:, u, :], (STEP - 1) / 2 / STEP, dg[:, u, :],
                                                           ALU.subtract, ALU.mult))
                    ch.link(nc.vector.tensor_tensor(y[:, :], g0[:, u, :], c[:, u, :], ALU.subtract))
                    ch.link(nc.vector.tensor_scalar(y[:, :], y[:, :], QUANT, ROUND, ALU.mult, ALU.add))
                    ve.wait_ge(up_sb, BASE + n + 1)
                    nc.vector.scalar_tensor_tensor(hs[:, g, f, :], y[:, :], ROUND, up[:, u, :], ALU.subtract,
                                                   ALU.add).then_inc(hs_sb, 1)

                def finish(t):
                    if t:
                        ve.wait_ge(x_done, BASE + t)
                    ve.wait_ge(z_mm, BASE + t + 1)
                    nc.vector.tensor_tensor(z, ps[HB + t % ZB], b2[:, :], ALU.add).then_inc(z_used, 1)
                    ve.wait_ge(z_used, BASE + t + 1)
                    ch.link(nc.vector.tensor_scalar(z, z, ROUND, ROUND, ALU.add, ALU.subtract))
                    nc.vector.scalar_tensor_tensor(x[:, t, :], z, 1.0 / QUANT, x[:, t, :], ALU.mult,
                                                   ALU.add).then_inc(x_done, 1)

                ve.wait_ge(s_b, BASE + 32)
                nc.vector.tensor_scalar(b1q[:, :], b1[:, :], QUANT, None, ALU.mult).then_inc(b_q, 1)
                nc.vector.tensor_scalar(b2[:, :], b2[:, :], QUANT, None, ALU.mult).then_inc(b_q, 1)
                for t in range(TG):
                    ln.vector_stats(ch, t)
                    ln.vector_norm(ve, t)
                round_(0)
                for n in range(N):
                    if n + 1 < N:
                        round_(n + 1)
                    interpolate(n)
                    if n in NORM_AT:
                        ln.vector_stats(ch, TG + NORM_AT.index(n))
                        ln.vector_norm(ve, TG + NORM_AT.index(n))
                    per = FT // TG
                    if n >= FT + 1 and (n - FT) % per == 1 and (n - FT) // per >= 1:
                        finish((n - FT) // per - 1)
                for t in range(TG - 1, NT):
                    finish(t)


def perceiver_kernel(nc, a, out):
    ctx = ExitStack()
    with ctx:
        def dram(name, shape, dt=F32):
            return nc.dram_tensor(name, shape, dt, kind="Internal").ap()

        xg_d = dram("routed_x", [ET * P, D])
        yg_d = dram("routed_y", [ET * P, D])
        v_d = dram("scan_v", [B * S, D])
        ba_d = dram("scan_ba", [2, B * HS, S])

        def sb(name, shape, dt=F32):
            return ctx.enter_context(nc.sbuf_tensor(name, shape, dt))

        x = sb("x", [P, NT + 1, D])
        cn = sb("cn", [P, CN_N])
        W0 = sb("W0", [P, 16384])
        PS = ctx.enter_context(nc.psum_tensor("PS", [P, 8, 512], F32))
        ps = [PS[:, i, :] for i in range(8)]
        ident = cn[:, CN_ID:CN_ID + P]
        ones = cn[:, CN_ONE:CN_ONE + P]

        wv0 = W0[:, 0:1024].rearrange("p (k n) -> p k n", k=DK)
        wt0 = W0[:, 1024:1792].rearrange("p (k n) -> p k n", k=CK)
        wqkv = W0[:, 1792:1792 + 6144].rearrange("p (k n) -> p k n", k=DK)
        wq4 = W0[:, 0:4096].rearrange("p (k n) -> p k n", k=DK)
        wk4 = W0[:, 4096:7168].rearrange("p (m n) -> p m n", m=H1 // 2)
        wv4 = W0[:, 7168:10240].rearrange("p (k n) -> p k n", k=CK)
        wo4 = W0[:, 10240:14336].rearrange("p (k n) -> p k n", k=HC // P)
        w16 = W0[:, 0:8192].rearrange("p (k n) -> p k n", k=DK)
        w26 = W0[:, 8192:16384].rearrange("p (k n) -> p k n", k=FF // P)

        fresh = []
        layer_sems = []

        def held(name):
            fresh.append(ctx.enter_context(nc.semaphore(name)))
            return fresh[-1]

        def sem(name, pool_dma=False):
            layer_sems.append(nc.alloc_semaphore(name=name))
            if not pool_dma:
                fresh.append(layer_sems[-1])
            return layer_sems[-1]

        def open_sems():
            with nc.Block() as block:
                for n, part in enumerate((block.gpsimd, block.vector, block.scalar, block.tensor, block.sync)):
                    @part
                    def _(eng, mine=fresh[n::5]):
                        for h in mine:
                            eng.sem_inc(h, BASE)
            fresh.clear()

        def reset_sems():
            with nc.Block() as block:
                for n, part in enumerate((block.gpsimd, block.vector, block.scalar, block.tensor, block.sync)):
                    @part
                    def _(eng, mine=layer_sems[n::5]):
                        for h in mine:
                            eng.sem_clear(h)
            for h in layer_sems:
                nc.release_semaphore(h)
            layer_sems.clear()

        s_cn, s_x = held("s_cn"), held("s_x")
        s_w12, s_w4, s_w6 = held("s_w12"), held("s_w4"), held("s_w6")

        env = Env()
        env.x, env.cn, env.W0, env.PS, env.ps, env.ident, env.ones = x, cn, W0, PS, ps, ident, ones
        env.out, env.xg_d, env.yg_d, env.v_d, env.ba_d = out, xg_d, yg_d, v_d, ba_d
        env.sem, env.open_sems = sem, open_sems
        env.s_cn, env.s_x, env.s_xg0 = s_cn, s_x, held("s_xg0")
        env.s_w12, env.s_w4, env.s_w6 = s_w12, s_w4, s_w6
        env.wv0, env.wt0, env.wqkv, env.wq4, env.wk4, env.wv4, env.wo4 = wv0, wt0, wqkv, wq4, wk4, wv4, wo4
        env.w16, env.w26 = w16, w26
        cosine_layer(nc, a, env)
        layers = [self_attention_layer, expert_layer, cross_attention_layer, decayed_attention_layer,
                  feed_forward_layer]
        for layer in layers:
            if layer is expert_layer:
                with nc.sbuf_tensor("W1", [P, 2 * (DK * 2 * FE + FE // P * D)], F32) as env.W1:
                    layer(nc, a, env)
                reset_sems()
            else:
                layer(nc, a, env)


def arrays_of(i):
    def tiles(w):
        w = np.asarray(w)
        return np.ascontiguousarray(w.reshape(-1, P, w.shape[1]).transpose(1, 0, 2))

    g = {k: np.asarray(v) for k, v in i.items()}
    c = g["ctx_768"]
    w = g["L0_attn_W_qkv"].reshape(H0, 3, DH0, D).transpose(1, 0, 2, 3).reshape(3 * D, D)
    return {
        "consts": constant_table(),
        "x": tiles(g["x"].reshape(B * S, D)),
        "ctxT": np.ascontiguousarray(c.reshape(B, J, CK, P).transpose(0, 3, 2, 1)),
        "ctxN": np.ascontiguousarray(c.reshape(B, J // P, P, C).transpose(0, 2, 1, 3)),
        "wv0": tiles(g["L0_xattn_Wv"].T),
        "wt0": tiles(g["L0_xattn_Wt"].T),
        "bv0": g["L0_xattn_bv"].reshape(1, HX),
        "bt0": np.ascontiguousarray(g["L0_xattn_bt"].reshape(2, P).T),
        "wqkv": tiles(w.T),
        "gate": tiles(g["L0_ffn_w_gate"]),
        "fc": np.ascontiguousarray(g["L0_ffn_c_fc"].reshape(NE, DK, P, 2 * FE).transpose(0, 2, 1, 3)),
        "proj": np.ascontiguousarray(g["L0_ffn_c_proj"].reshape(NE, FE // P, P, D).transpose(0, 2, 1, 3)),
        "wq4": tiles(g["L1_xattn_Wq"]),
        "wk4": tiles(g["L1_xattn_Wk"].T),
        "wv4": tiles(g["L1_xattn_Wv"]),
        "wo4": tiles(g["L1_xattn_Wo"]),
        "bo4": g["L1_xattn_bo"].reshape(1, D),
        "w5": np.ascontiguousarray(np.stack([tiles(g["L1_attn_" + n].T) for n in
                                             ("W_q", "W_k", "W_v", "W_alpha_w", "W_o")], 1)),
        "ba5": g["L1_attn_W_alpha_b"].reshape(1, HS * DHS),
        "w16": tiles(g["L1_ffn_w1"]),
        "w26": tiles(g["L1_ffn_w2"]),
        "b16": np.ascontiguousarray(g["L1_ffn_b1"].reshape(FF // P, P).T),
        "b26": np.ascontiguousarray(np.broadcast_to(g["L1_ffn_b2"].reshape(1, D), (P, D))),
    }


def kernel(**inputs):
    import concourse.bacc as _bacc
    from concourse.bass_utils import run_bass_kernel_spmd as _run

    nc = _bacc.Bacc("TRN2", target_bir_lowering=False, num_devices=1)
    arrays, aps = {}, {}
    for name, w in arrays_of(inputs).items():
        arrays[f"in_{name}"] = np.ascontiguousarray(w)
        aps[name] = nc.dram_tensor(f"in_{name}", w.shape, mybir.dt.from_np(w.dtype), kind="ExternalInput").ap()
    out = nc.dram_tensor("out", (P, NT, D), F32, kind="ExternalOutput").ap()
    perceiver_kernel(nc, aps, out)
    r = _run(nc, [arrays], core_ids=[0])
    return r.results[0]["out"].transpose(1, 0, 2).reshape(B, S, D)
```
